# Optimizing a Trainium2 kernel written in Bass

```python
import numpy as np
import jax
import jax.numpy as jnp

def _softmax(x, axis=-1):
    return jax.nn.softmax(x, axis=axis)

def _gelu(x):
    return jax.nn.gelu(x, approximate=True)

def _silu(x):
    return jax.nn.silu(x)

def _sigmoid(x):
    return jax.nn.sigmoid(x)

def _layernorm(x, axis=-1, eps=1e-05):
    m = jnp.mean(x, axis=axis, keepdims=True)
    v = jnp.var(x, axis=axis, keepdims=True)
    return (x - m) / jnp.sqrt(v + eps)

def _scatter_add(tgt, idx, src, axis=0):
    return tgt.at[idx].add(src)

def _segment_sum(src, seg, n):
    return jax.ops.segment_sum(src, seg, n)
kernel_name = 'mk_lm_tower_d2_tok_ids1024_r4_09b19f'

def setup_inputs(seed: int=0):
    np.random.seed(seed)
    _w = jnp.asarray

    def _rec_inputs():
        import jax
        import jax.numpy as jnp
        _rk = jax.random.key(seed)
        x = jax.random.randint(jax.random.fold_in(_rk, 1), (2, 1024), 0, 31999, jnp.int32)
        return x
    x = _rec_inputs()

    def _L0_tok_setup():
        import jax, jax.numpy as jnp
        import numpy as np
        VOCAB = 8000
        HIDDEN = 256
        key = jax.random.key(seed)
        k1, k2, k3 = jax.random.split(key, 3)
        inputs = jax.random.randint(k1, (4, 1024), 0, VOCAB, dtype=jnp.int64 if jax.config.jax_enable_x64 else jnp.int32)
        W0 = jax.random.normal(k2, (VOCAB, 2 * HIDDEN), dtype=jnp.float32)
        W1 = jax.random.normal(k3, (2 * HIDDEN, HIDDEN), dtype=jnp.float32)
        return {'inputs': inputs, 'W0': W0, 'W1': W1}
    _L0_tok_all = _L0_tok_setup()
    _L0_tok_in = {k: v for k, v in _L0_tok_all.items() if k in ('W0', 'W1')}
    del _L0_tok_all

    def _L0_attn_setup():
        import jax, jax.numpy as jnp
        import numpy as np
        B, T, C = (2, 512, 256)
        H = 16
        HS = C // H
        key = jax.random.key(seed)
        k1, k2, k3 = jax.random.split(key, 3)
        x = jax.random.normal(k1, (B, T, C), dtype=jnp.float32)
        w_qkv = jax.random.normal(k2, (3 * C, C), dtype=jnp.float32) * C ** (-0.5)
        w_proj = jax.random.normal(k3, (C, C), dtype=jnp.float32) * C ** (-0.5)
        b_proj = jnp.zeros((C,), dtype=jnp.float32)
        return {'x': x, 'w_qkv': w_qkv, 'w_proj': w_proj, 'b_proj': b_proj}
    _L0_attn_all = _L0_attn_setup()
    _L0_attn_in = {k: v for k, v in _L0_attn_all.items() if k in ('w_qkv', 'w_proj', 'b_proj')}
    del _L0_attn_all

    def _L0_ffn_setup():
        import jax, jax.numpy as jnp
        import numpy as np
        EMB_DIM = 256
        N_EXPERTS = 8
        TOP_K = 2
        MOE_HIDDEN = 256
        NORM_TOPK = True

        def _swiglu(h):
            gate = h[:, ::2]
            up = h[:, 1::2]
            return jnp.clip(gate, -7.0, 7.0) * jax.nn.sigmoid(1.702 * gate) * (jnp.clip(up, -7.0, 7.0) + 1.0)
        key = jax.random.key(seed)
        ks = jax.random.split(key, 7)
        s = 0.02
        return {'x': jax.random.normal(ks[0], (2, 512, EMB_DIM), dtype=jnp.float32), 'router_w': jax.random.normal(ks[1], (N_EXPERTS, EMB_DIM), dtype=jnp.float32) * s, 'router_b': jnp.zeros((N_EXPERTS,), dtype=jnp.float32), 'gate_up_w': jax.random.normal(ks[2], (N_EXPERTS, 2 * MOE_HIDDEN, EMB_DIM), dtype=jnp.float32) * s, 'gate_up_b': jnp.zeros((N_EXPERTS, 2 * MOE_HIDDEN), dtype=jnp.float32), 'down_w': jax.random.normal(ks[3], (N_EXPERTS, EMB_DIM, MOE_HIDDEN), dtype=jnp.float32) * s, 'down_b': jnp.zeros((N_EXPERTS, EMB_DIM), dtype=jnp.float32)}
    _L0_ffn_all = _L0_ffn_setup()
    _L0_ffn_in = {k: v for k, v in _L0_ffn_all.items() if k in ('router_w', 'router_b', 'gate_up_w', 'gate_up_b', 'down_w', 'down_b')}
    del _L0_ffn_all

    def _L1_attn_setup():
        import jax, jax.numpy as jnp
        import numpy as np
        D_MODEL = 256
        NUM_HEADS = 16
        D_H = D_MODEL // NUM_HEADS
        BATCH, SEQ = (4, 512)
        key = jax.random.key(seed)
        kx, kq, kk, kv, ko = jax.random.split(key, 5)
        sigma = (2.0 / (D_MODEL + D_MODEL)) ** 0.5

        def trunc(k):
            return jax.random.truncated_normal(k, -3.0, 3.0, (D_MODEL, D_MODEL), dtype=jnp.float32) * sigma
        return {'x': jax.random.normal(kx, (BATCH, SEQ, D_MODEL), dtype=jnp.float32), 'Wq': trunc(kq), 'Wk': trunc(kk), 'Wv': trunc(kv), 'Wo': trunc(ko)}
    _L1_attn_all = _L1_attn_setup()
    _L1_attn_in = {k: v for k, v in _L1_attn_all.items() if k in ('Wq', 'Wk', 'Wv', 'Wo')}
    del _L1_attn_all

    def _L1_ffn_setup():
        import jax, jax.numpy as jnp
        import numpy as np

        def _binarize(w):
            alpha = jax.lax.stop_gradient(jnp.mean(jnp.abs(w), axis=1, keepdims=True))
            bw = alpha * jnp.sign(w)
            return w + jax.lax.stop_gradient(bw - w)
        key = jax.random.key(seed)
        k1, k2, k3, k4, k5 = jax.random.split(key, 5)
        D, H = (256, 1024)
        x = jax.random.normal(k1, (64, 196, D), dtype=jnp.float32)
        w1 = jax.random.normal(k2, (H, D), dtype=jnp.float32) * 0.02
        b1 = jax.random.normal(k3, (H,), dtype=jnp.float32) * 0.02
        w2 = jax.random.normal(k4, (D, H), dtype=jnp.float32) * 0.02
        b2 = jax.random.normal(k5, (D,), dtype=jnp.float32) * 0.02
        return {'x': x, 'w1': w1, 'b1': b1, 'w2': w2, 'b2': b2}
    _L1_ffn_all = _L1_ffn_setup()
    _L1_ffn_in = {k: v for k, v in _L1_ffn_all.items() if k in ('w1', 'b1', 'w2', 'b2')}
    del _L1_ffn_all
    return {'x': x, 'L0_tok_W0': _L0_tok_in['W0'], 'L0_tok_W1': _L0_tok_in['W1'], 'L0_attn_w_qkv': _L0_attn_in['w_qkv'], 'L0_attn_w_proj': _L0_attn_in['w_proj'], 'L0_attn_b_proj': _L0_attn_in['b_proj'], 'L0_ffn_router_w': _L0_ffn_in['router_w'], 'L0_ffn_router_b': _L0_ffn_in['router_b'], 'L0_ffn_gate_up_w': _L0_ffn_in['gate_up_w'], 'L0_ffn_gate_up_b': _L0_ffn_in['gate_up_b'], 'L0_ffn_down_w': _L0_ffn_in['down_w'], 'L0_ffn_down_b': _L0_ffn_in['down_b'], 'L1_attn_Wq': _L1_attn_in['Wq'], 'L1_attn_Wk': _L1_attn_in['Wk'], 'L1_attn_Wv': _L1_attn_in['Wv'], 'L1_attn_Wo': _L1_attn_in['Wo'], 'L1_ffn_w1': _L1_ffn_in['w1'], 'L1_ffn_b1': _L1_ffn_in['b1'], 'L1_ffn_w2': _L1_ffn_in['w2'], 'L1_ffn_b2': _L1_ffn_in['b2']}

def reference(x, L0_tok_W0, L0_tok_W1, L0_attn_w_qkv, L0_attn_w_proj, L0_attn_b_proj, L0_ffn_router_w, L0_ffn_router_b, L0_ffn_gate_up_w, L0_ffn_gate_up_b, L0_ffn_down_w, L0_ffn_down_b, L1_attn_Wq, L1_attn_Wk, L1_attn_Wv, L1_attn_Wo, L1_ffn_w1, L1_ffn_b1, L1_ffn_w2, L1_ffn_b2):
    import jax
    import jax.numpy as jnp

    def _L0_tok_ref(inputs, W0, W1):
        import jax, jax.numpy as jnp
        import numpy as np
        VOCAB = 8000
        HIDDEN = 256
        x = W0[inputs]
        emb = jnp.einsum('blk,kh->blh', x, W1)
        mask = (inputs != 0).astype(emb.dtype)
        emb = emb * mask[..., None]
        emb = emb * jnp.asarray(HIDDEN ** 0.5, emb.dtype)
        return emb

    def _L0_attn_ref(x, w_qkv, w_proj, b_proj):
        import jax, jax.numpy as jnp
        import numpy as np
        B, T, C = (2, 512, 256)
        H = 16
        HS = C // H
        b, t, c = x.shape
        hs = c // H
        qkv = jnp.einsum('btc,fc->btf', x, w_qkv)
        qkv = qkv.reshape(b, t, 3, H, hs)
        q = jnp.transpose(qkv[:, :, 0], (0, 2, 1, 3))
        k = jnp.transpose(qkv[:, :, 1], (0, 2, 1, 3))
        v = jnp.transpose(qkv[:, :, 2], (0, 2, 1, 3))
        scores = jnp.einsum('bhqd,bhkd->bhqk', q, k) * hs ** (-0.5)
        p = jax.nn.softplus(scores)
        p = p * p
        causal = jnp.tril(jnp.ones((t, t), dtype=p.dtype))
        p = p * causal
        attn = p / (jnp.sum(p, axis=-1, keepdims=True) + 1e-09)
        out = jnp.einsum('bhqk,bhkd->bhqd', attn, v)
        out = jnp.transpose(out, (0, 2, 1, 3)).reshape(b, t, c)
        return jnp.einsum('btc,oc->bto', out, w_proj) + b_proj

    def _L0_ffn_ref(x, router_w, router_b, gate_up_w, gate_up_b, down_w, down_b):
        import jax, jax.numpy as jnp
        import numpy as np
        EMB_DIM = 256
        N_EXPERTS = 8
        TOP_K = 2
        MOE_HIDDEN = 256
        NORM_TOPK = True

        def _swiglu(h):
            gate = h[:, ::2]
            up = h[:, 1::2]
            return jnp.clip(gate, -7.0, 7.0) * jax.nn.sigmoid(1.702 * gate) * (jnp.clip(up, -7.0, 7.0) + 1.0)
        B, S, D = x.shape
        h = x.reshape(B * S, D)
        scores = h @ router_w.T + router_b
        vals, idx = jax.lax.top_k(scores, TOP_K)
        if NORM_TOPK:
            vals = jax.nn.softmax(vals, axis=-1)
        cw = jnp.sum(jax.nn.one_hot(idx, N_EXPERTS, dtype=vals.dtype) * vals[..., None], axis=1)
        out = jnp.zeros_like(h)
        for e in range(N_EXPERTS):
            g = h @ gate_up_w[e].T + gate_up_b[e]
            a = _swiglu(g)
            oe = a @ down_w[e].T + down_b[e]
            out = out + oe * cw[:, e:e + 1]
        return out.reshape(B, S, D)

    def _L1_attn_ref(x, Wq, Wk, Wv, Wo):
        import jax, jax.numpy as jnp
        import numpy as np
        D_MODEL = 256
        NUM_HEADS = 16
        D_H = D_MODEL // NUM_HEADS
        BATCH, SEQ = (4, 512)
        B, S, D = x.shape
        H, Dh = (NUM_HEADS, D_H)
        q = jnp.einsum('oi,bsi->bso', Wq, x)
        k = jnp.einsum('oi,bsi->bso', Wk, x)
        v = jnp.einsum('oi,bsi->bso', Wv, x)
        q = q.reshape(B, S, H, Dh).transpose(0, 2, 1, 3)
        k = k.reshape(B, S, H, Dh).transpose(0, 2, 1, 3)
        v = v.reshape(B, S, H, Dh).transpose(0, 2, 1, 3)
        scale = 1.0 / jnp.sqrt(jnp.asarray(Dh, dtype=x.dtype))
        score = jnp.einsum('bhnd,bhmd->bhnm', q, k) * scale
        causal = jnp.tril(jnp.ones((S, S), dtype=bool))
        score = jnp.where(causal, score, -jnp.inf)
        attn = jax.nn.softmax(score, axis=-1)
        out = jnp.einsum('bhnm,bhmd->bhnd', attn, v)
        out = out.transpose(0, 2, 1, 3).reshape(B, S, D)
        return jnp.einsum('oi,bsi->bso', Wo, out)

    def _L1_ffn_ref(x, w1, b1, w2, b2):
        import jax, jax.numpy as jnp
        import numpy as np

        def _binarize(w):
            alpha = jax.lax.stop_gradient(jnp.mean(jnp.abs(w), axis=1, keepdims=True))
            bw = alpha * jnp.sign(w)
            return w + jax.lax.stop_gradient(bw - w)
        bw1 = _binarize(w1)
        h = jnp.einsum('bsd,hd->bsh', x, bw1) + b1
        h = jax.nn.gelu(h, approximate=False)
        bw2 = _binarize(w2)
        out = jnp.einsum('bsh,dh->bsd', h, bw2) + b2
        return out
    h = _L0_tok_ref(x, L0_tok_W0, L0_tok_W1)
    h = h + _L0_attn_ref(_layernorm(h, axis=-1), L0_attn_w_qkv, L0_attn_w_proj, L0_attn_b_proj)
    h = h + _L0_ffn_ref(_layernorm(h, axis=-1), L0_ffn_router_w, L0_ffn_router_b, L0_ffn_gate_up_w, L0_ffn_gate_up_b, L0_ffn_down_w, L0_ffn_down_b)
    h = h + _L1_attn_ref(_layernorm(h, axis=-1), L1_attn_Wq, L1_attn_Wk, L1_attn_Wv, L1_attn_Wo)
    h = h + _L1_ffn_ref(_layernorm(h, axis=-1), L1_ffn_w1, L1_ffn_b1, L1_ffn_w2, L1_ffn_b2)
    return h

_drawn_inputs = setup_inputs


def setup_inputs(seed=0):
    import zlib

    import numpy as np

    out = dict(_drawn_inputs(seed))
    spreads = {'L0_attn_b_proj': (0.0, 2.0),
     'L0_ffn_router_b': (0.0, 2.0),
     'L0_ffn_gate_up_b': (0.0, 2.0),
     'L0_ffn_down_b': (0.0, 2.0)}
    factors = {'L0_attn_w_qkv': 8.0,
     'L0_attn_w_proj': 8.0,
     'L0_ffn_router_w': 8.0,
     'L0_ffn_gate_up_w': 8.0,
     'L0_ffn_down_w': 8.0,
     'L1_attn_Wq': 8.0,
     'L1_attn_Wk': 8.0,
     'L1_attn_Wv': 8.0,
     'L1_attn_Wo': 8.0,
     'L1_ffn_w1': 31.94,
     'L1_ffn_b1': 64.0,
     'L1_ffn_w2': 26.514,
     'L1_ffn_b2': 64.0}
    for name, (base, spread) in spreads.items():
        noise = np.random.default_rng([zlib.crc32(name.encode()), seed]).standard_normal(out[name].shape)
        drawn = base * np.exp(spread * noise) if base else spread * noise
        out[name] = jnp.asarray(drawn.astype(out[name].dtype))
    for name, factor in factors.items():
        out[name] = (out[name] * factor).astype(out[name].dtype)
    return out
```

```python
from contextlib import ExitStack

import concourse.bass as bass
from concourse import mybir

F32 = mybir.dt.float32
BF16 = mybir.dt.bfloat16
I32 = mybir.dt.int32
U32 = mybir.dt.uint32
ALU = mybir.AluOpType
ACT = mybir.ActivationFunctionType
AX = mybir.AxisListType

P = 128
EPS = 1e-5
NEG = -1e30
CAP = 40.0


def lm_tower(nc, ids, W0, w1_tok, wqkv0, wproj0, bproj0, router_w, router_b, gate_up_w, gate_up_b,
             down_w, down_b, wqkv1, wproj1, w1, b1, w2, b2, out):
    NT = ids.shape[1]
    VOCAB, KD = W0.shape
    D = out.shape[1]
    B = 2
    TB = NT // B
    T = TB * P
    KT = KD // P
    KC = D // P
    H, HD = 16, 16
    G = H // 4
    NG = B * G
    NE = router_w.shape[2]
    HC = w1.shape[1]
    QC = T // 512
    KR = 6 * HD
    Q_PARTS, K_PARTS = (0, 0, 0, 1, 1, 2), (0, 1, 2, 0, 1, 0)

    STRIPS = [(qc, i, 512 - P * max(0, i - 4 * qc)) for qc in range(QC) for i in range(4 * qc + 4)]
    NS = len(STRIPS)
    UNITS = [(m, pair) for m in range(NS) for pair in range(2)]
    NU = len(UNITS)
    LAST = {qc: max(m for m, s in enumerate(STRIPS) if s[0] == qc) for qc in range(QC)}

    scratch = nc.dram_tensor("qk_parts", (2, 2, 3, B * D, T), BF16, kind="Internal").ap()

    with ExitStack() as ctx:
        semaphores = []

        def sem(name):
            semaphores.append(ctx.enter_context(nc.semaphore(name)))
            return semaphores[-1]

        waited = sem("waited")

        def plain(eng):
            eng.sem_inc(waited, 1)

        def sb(name, shape, dt=F32):
            return ctx.enter_context(nc.sbuf_tensor(name, shape, dt))

        ps = ctx.enter_context(nc.psum_tensor("ps", [P, 8, 512], F32))

        h = sb("h", [P, NT, D])
        xT = sb("xT", [P, KC, T])
        attnT = sb("attnT", [P, NG, T])
        region = sb("region", [P, 12 * 1024])
        stacks = region[:, 0:8192].bitcast(BF16).rearrange("p (s q j t) -> p s q j t", s=2, q=2, j=4)
        v_all = region[:, 8192:12288].rearrange("p (n t c) -> p n t c", n=NG, t=TB)
        wgu_sb = region[:, 0:8192].rearrange("p (e k f) -> p e k f", e=NE, k=KC)
        wdn_sb = region[:, 8192:12288].rearrange("p (e k d) -> p e k d", e=NE, k=KC)
        raw_w1 = region[:, 0:2048].rearrange("p (c d) -> p c d", c=HC)
        raw_w2 = region[:, 2048:4096].rearrange("p (k f) -> p k f", k=KC)
        sgn_w1 = region[:, 4096:6144].rearrange("p (c d) -> p c d", c=HC)
        sgn_w2 = region[:, 6144:8192].rearrange("p (k f) -> p k f", k=KC)
        arena = sb("arena", [P, 10 * 1024])

        vg = sb("vg", [P, TB, 4, 32])
        oT = sb("oT", [P, 512])
        den = sb("den", [P, 512])
        rden = sb("rden", [P, 512])

        w1t_sb = sb("w1t_sb", [P, KT, D])
        wqkv_sb = [sb(f"wqkv_sb{n}", [P, KC, 3 * D]) for n in range(2)]
        wproj_sb = [sb(f"wproj_sb{n}", [P, G, D]) for n in range(2)]
        bproj_sb = sb("bproj_sb", [P, D])
        rw_sb = sb("rw_sb", [P, KC, NE])
        rb_sb = sb("rb_sb", [P, NE])
        gub_sb = sb("gub_sb", [P, NE, 4])
        sgb_sb = sb("sgb_sb", [P, NE, 4])
        upb_sb = sb("upb_sb", [P, NE, 4])
        dnb_sb = sb("dnb_sb", [NE, D])
        w1T_sb = sb("w1T_sb", [P, KC, HC * P])
        w2T_sb = sb("w2T_sb", [P, HC, D])
        b1_sb = sb("b1_sb", [P, HC])
        b2_sb = sb("b2_sb", [P, D])
        ids_sb = sb("ids_sb", [P, NT], I32)

        ident = sb("ident", [P, P])
        identb = sb("identb", [P, P], BF16)
        mask_qk = sb("mask_qk", [P, P], BF16)
        mask_kq = sb("mask_kq", [P, P], BF16)
        den_sel = sb("den_sel", [P, P])
        expert_no = sb("expert_no", [P, NE])
        eps_sb = sb("eps_sb", [P, 2])

        idf = sb("idf", [P, TB])
        idn = sb("idn", [P, TB])
        idc = sb("idc", [P, TB], U32)
        tok_scale = sb("tok_scale", [P, TB])
        stats = sb("stats", [P, TB, 6])
        mv = sb("mv", [P, TB, 2])
        sd = sb("sd", [P, TB])
        rsd = sb("rsd", [P, TB])

        w_in = {n: sem(f"w_in_{n}") for n in ("tok", "qkv0", "mlp", "rest", "ids", "experts")}
        const_made = sem("const_made")
        id_step, ids_ready = sem("id_step"), sem("ids_ready")
        gathered = [ctx.enter_context(nc.semaphore(f"gathered{t}")) for t in range(TB)]
        rows_T, rows_Tc = sem("rows_T"), sem("rows_Tc")
        emb_done, h_ready = sem("emb_done"), sem("h_ready")
        alpha_step, sign_done, eff_done, wT_ps, wT_done = (
            sem("alpha_step"), sem("sign_done"), sem("eff_done"), sem("wT_ps"), sem("wT_done"))

        rows = arena[:, 0:TB * KD].rearrange("p (t k) -> p t k", t=TB)
        rowsT = arena[:, TB * KD:TB * KD + 2 * KD].rearrange("p (s k) -> p s k", s=2)
        alpha = arena[:, 8192:8192 + HC + KC]
        N_CONST = 12
        N_REST = 12
        W_BLOCKS = [("w1", c, k) for k in range(KC) for c in range(HC)] + \
                   [("w2", k, c) for c in range(HC) for k in range(KC)]

        def embed_phase():
            with nc.Block() as block:
                @block.sync
                def _(sp):
                    sp.dma_start(ids_sb[:], ids).then_inc(w_in["ids"], 16)
                    sp.dma_start(w1t_sb[:], w1_tok).then_inc(w_in["tok"], 16)
                    sp.dma_start(raw_w1, w1).then_inc(w_in["mlp"], 16)
                    sp.dma_start(raw_w2, w2).then_inc(w_in["mlp"], 16)
                    sp.dma_start(wqkv_sb[0][:], wqkv0).then_inc(w_in["qkv0"], 16)
                    for dst, src in ((wqkv_sb[1], wqkv1), (wproj_sb[0], wproj0), (wproj_sb[1], wproj1),
                                     (rw_sb, router_w), (gub_sb, gate_up_b), (dnb_sb, down_b),
                                     (b1_sb, b1)):
                        sp.dma_start(dst[:], src).then_inc(w_in["rest"], 16)
                    for dst, src in ((bproj_sb, bproj0), (rb_sb, router_b), (b2_sb, b2)):
                        sp.dma_start(dst[:], src.to_broadcast((P, src.shape[1]))).then_inc(w_in["rest"], 16)

                @block.gpsimd
                def _(pool):
                    nc.gpsimd.memset(ident[:], 0.0).then_inc(const_made, 1)
                    nc.gpsimd.memset(identb[:], 0.0).then_inc(const_made, 1)
                    nc.gpsimd.memset(mask_qk[:], 0.0).then_inc(const_made, 1)
                    nc.gpsimd.memset(mask_kq[:], 0.0).then_inc(const_made, 1)
                    nc.gpsimd.memset(den_sel[:], 1.0).then_inc(const_made, 1)
                    nc.gpsimd.memset(vg[:], 0.0).then_inc(const_made, 1)
                    pool.wait_ge(const_made, 1 + 6)
                    for m in (ident, identb):
                        nc.gpsimd.affine_select(out=m[:], in_=m[:], compare_op=ALU.not_equal, fill=1.0, base=0,
                                                pattern=[[-1, P]], channel_multiplier=1).then_inc(const_made, 1)
                    nc.gpsimd.affine_select(out=mask_qk[:], in_=mask_qk[:], compare_op=ALU.is_ge, fill=NEG, base=0,
                                            pattern=[[-1, P]], channel_multiplier=1).then_inc(const_made, 1)
                    nc.gpsimd.affine_select(out=mask_kq[:], in_=mask_kq[:], compare_op=ALU.is_ge, fill=NEG, base=0,
                                            pattern=[[1, P]], channel_multiplier=-1).then_inc(const_made, 1)
                    nc.gpsimd.affine_select(out=den_sel[:].rearrange("p (j c) -> p j c", j=4),
                                            in_=den_sel[:].rearrange("p (j c) -> p j c", j=4),
                                            compare_op=ALU.is_equal, fill=0.0, base=-HD,
                                            pattern=[[-32, 4], [0, 32]], channel_multiplier=1).then_inc(const_made, 1)
                    nc.gpsimd.iota(expert_no[:], pattern=[[1, NE]], base=0, channel_multiplier=0,
                                   allow_small_or_imprecise_dtypes=True).then_inc(const_made, 1)
                    nc.gpsimd.memset(vg[:, :, :, HD:HD + 1], 1.0).then_inc(const_made, 1)
                    with pool.Fori(0, B) as b:
                        pool.wait_ge(ids_ready, 1 + b + 1)
                        pool.wait_ge(rows_T, 1 + TB * b)
                        plain(pool)
                        for t in range(TB):
                            nc.gpsimd.indirect_dma_start(
                                rows[:, t, :], None, W0, bass.IndirectOffsetOnAxis(ap=idc[:, t:t + 1], axis=0),
                            ).then_inc(gathered[t], 16)

                @block.vector
                def _(dve):
                    nc.vector.memset(eps_sb[:, 0:1], EPS)
                    nc.vector.memset(eps_sb[:, 1:2], 1e-9)
                    dve.wait_ge(w_in["ids"], 1 + 16)
                    with dve.Fori(0, B) as b:
                        dve.wait_ge(rows_T, 1 + TB * b)
                        dve.wait_ge(h_ready, 1 + TB * b)
                        nc.vector.tensor_copy(idf[:], ids_sb[:, bass.ds(b * TB, TB)]).then_inc(id_step, 1)
                        dve.wait_ge(id_step, 1 + 4 * b + 1)
                        nc.vector.tensor_scalar(idn[:], idf[:], 0.0, float(VOCAB), ALU.is_lt, ALU.mult).then_inc(id_step, 1)
                        nc.vector.tensor_scalar(tok_scale[:], idf[:], 0.0, 16.0, ALU.not_equal, ALU.mult).then_inc(id_step, 1)
                        dve.wait_ge(id_step, 1 + 4 * b + 3)
                        nc.vector.tensor_tensor(idn[:], idn[:], idf[:], ALU.add).then_inc(id_step, 1)
                        dve.wait_ge(id_step, 1 + 4 * b + 4)
                        nc.vector.tensor_scalar(idc[:], idn[:], float(VOCAB - 1), 0.0, ALU.min, ALU.max).then_inc(ids_ready, 1)
                        for t in range(TB):
                            dve.wait_ge(emb_done, 1 + TB * b + t + 1)
                            nc.vector.tensor_scalar(h[:, b * TB + t, :], ps[:, 2 + t % 2, 0:D], tok_scale[:, t:t + 1],
                                                    None, ALU.mult).then_inc(h_ready, 1)
                    dve.wait_ge(w_in["mlp"], 1 + 32)
                    nc.vector.tensor_reduce(alpha[:, 0:HC], raw_w1, AX.X, ALU.add,
                                            apply_absolute_value=True).then_inc(alpha_step, 1)
                    nc.vector.tensor_reduce(alpha[:, HC:HC + KC], raw_w2, AX.X, ALU.add,
                                            apply_absolute_value=True).then_inc(alpha_step, 1)
                    dve.wait_ge(alpha_step, 1 + 2)
                    nc.vector.tensor_scalar(alpha[:, 0:HC], alpha[:, 0:HC], 1.0 / D, None, ALU.mult).then_inc(alpha_step, 1)
                    nc.vector.tensor_scalar(alpha[:, HC:HC + KC], alpha[:, HC:HC + KC], 1.0 / (HC * P), None,
                                            ALU.mult).then_inc(alpha_step, 1)
                    dve.wait_ge(alpha_step, 1 + 4)
                    parts = [(sgn_w1[:, c, :], raw_w1[:, c, :], alpha[:, c:c + 1]) for c in range(HC)] + \
                            [(sgn_w2[:, k, :], raw_w2[:, k, :], alpha[:, HC + k:HC + k + 1]) for k in range(KC)]
                    for n, (s, w, a) in enumerate(parts):
                        dve.wait_ge(sign_done, 1 + (1 if n < HC else 2))
                        nc.vector.scalar_tensor_tensor(s, s, a, w, ALU.mult, ALU.subtract).then_inc(eff_done, 1)
                    for n, (s, w, a) in enumerate(parts):
                        dve.wait_ge(eff_done, 1 + n + 1)
                        nc.vector.tensor_tensor(s, s, w, ALU.add).then_inc(eff_done, 1)
                    dve.wait_ge(w_in["rest"], 1 + 16 * 10)
                    nc.vector.tensor_scalar(sgb_sb[:], gub_sb[:], 1.702, None, ALU.mult)
                    nc.vector.tensor_scalar(upb_sb[:], gub_sb[:], 1.0, None, ALU.add)

                @block.tensor
                def _(pe):
                    pe.wait_ge(const_made, 1 + 13)
                    pe.wait_ge(w_in["tok"], 1 + 16)
                    with pe.Fori(0, B) as b:
                        for t in range(TB + 1):
                            if t < TB:
                                pe.wait_ge(gathered[t], 16 * (b + 1))
                                if t >= 2:
                                    pe.wait_ge(rows_Tc, 1 + TB * b + t - 1)
                                else:
                                    pe.wait_ge(rows_Tc, 1 + TB * b)
                                for k in range(KT):
                                    last = nc.tensor.transpose(ps[:, t % 2, k * P:(k + 1) * P],
                                                               rows[:, t, k * P:(k + 1) * P], ident[:])
                                last.then_inc(rows_T, 1)
                            if t >= 1:
                                pe.wait_ge(rows_Tc, 1 + TB * b + t)
                                if t >= 3:
                                    pe.wait_ge(h_ready, 1 + TB * b + t - 2)
                                else:
                                    pe.wait_ge(h_ready, 1 + TB * b)
                                for k in range(KT):
                                    last = nc.tensor.matmul(ps[:, 2 + (t - 1) % 2, 0:D],
                                                            rowsT[:, (t - 1) % 2, k * P:(k + 1) * P],
                                                            w1t_sb[:, k, :], start=(k == 0), stop=(k == KT - 1))
                                last.then_inc(emb_done, 1)
                    for n in range(len(W_BLOCKS) // 4):
                        pe.wait_ge(eff_done, 1 + 2 * (HC + KC))
                        if n >= 4:
                            pe.wait_ge(wT_done, 1 + n - 3)
                        for i in range(4):
                            kind, r, c = W_BLOCKS[4 * n + i]
                            src = (sgn_w1 if kind == "w1" else sgn_w2)[:, r, c * P:(c + 1) * P]
                            last = nc.tensor.transpose(ps[:, 4 + n % 4, i * P:(i + 1) * P], src, ident[:])
                        last.then_inc(wT_ps, 1)

                @block.scalar
                def _(act):
                    with act.Fori(0, B) as b:
                        for t in range(TB):
                            act.wait_ge(rows_T, 1 + TB * b + t + 1)
                            act.wait_ge(emb_done, 1 + TB * b + max(t - 1, 0))
                            nc.scalar.activation(rowsT[:, t % 2, :], ps[:, t % 2, :], ACT.Copy).then_inc(rows_Tc, 1)
                    act.wait_ge(w_in["mlp"], 1 + 32)
                    nc.scalar.activation(sgn_w1, raw_w1, ACT.Sign).then_inc(sign_done, 1)
                    nc.scalar.activation(sgn_w2, raw_w2, ACT.Sign).then_inc(sign_done, 1)
                    for n in range(len(W_BLOCKS) // 4):
                        act.wait_ge(wT_ps, 1 + n + 1)
                        if n < 4:
                            dst = w1T_sb[:, n // 2, (n % 2) * 512:(n % 2) * 512 + 512]
                        else:
                            dst = w2T_sb[:, 2 * (n - 4):2 * (n - 4) + 2, :].rearrange("p c d -> p (c d)")
                        nc.scalar.activation(dst, ps[:, 4 + n % 4, :], ACT.Copy).then_inc(wT_done, 1)

        st_done, mv_done, sd_done, rsd_done, xn_done, xn_T, xT_done = (
            sem(n) for n in ("st_done", "mv_done", "sd_done", "rsd_done", "xn_done", "xn_T", "xT_done"))
        xn = arena[:, 0:TB * D].rearrange("p (t d) -> p t d", t=TB)

        def ln_vector(dve, n, b):
            for t in range(TB):
                nc.vector.bn_stats(stats[:, t, :], h[:, b * TB + t, :]).then_inc(st_done, 1)
            for t in range(TB):
                dve.wait_ge(st_done, 1 + TB * n + t + 1)
                plain(dve)
                nc.vector.bn_aggr(mv[:, t, :], stats[:, t, :]).then_inc(mv_done, 1)
            dve.wait_ge(sd_done, 1 + n + 1)
            nc.vector.reciprocal(rsd[:], sd[:]).then_inc(rsd_done, 1)
            dve.wait_ge(rsd_done, 1 + n + 1)
            for t in range(TB):
                nc.vector.tensor_scalar(xn[:, t, :], h[:, b * TB + t, :], mv[:, t, 0:1], rsd[:, t:t + 1],
                                        ALU.subtract, ALU.mult).then_inc(xn_done, 1)

        def ln_scalar(act, n, xT_free):
            act.wait_ge(mv_done, 1 + TB * (n + 1))
            nc.scalar.activation(sd[:], mv[:, :, 1], ACT.Sqrt, bias=eps_sb[:, 0:1]).then_inc(sd_done, 1)
            xT_free()
            for c in range(T // 512):
                for k in range(KC):
                    act.wait_ge(xn_T, 1 + 4 * n + KC * c + k + 1)
                    nc.scalar.activation(xT[:, k, c * 512:(c + 1) * 512], ps[:, KC * c + k, :],
                                         ACT.Copy).then_inc(xT_done, 1)

        def ln_tensor(pe, n, banks_free):
            banks_free()
            for c in range(T // 512):
                pe.wait_ge(xn_done, 1 + TB * n + 4 * c + 4)
                for k in range(KC):
                    for i in range(4):
                        last = nc.tensor.transpose(ps[:, KC * c + k, i * P:(i + 1) * P],
                                                   xn[:, 4 * c + i, k * P:(k + 1) * P], ident[:])
                    last.then_inc(xn_T, 1)

        qk_ps, qk_hi, qk_r, qk_mid, qk_lo, v_ps, v_done, res_bias = (
            sem(n) for n in ("qk_ps", "qk_hi", "qk_r", "qk_mid", "qk_lo", "v_ps", "v_done", "res_bias"))
        qk_out = [sem("qk_out0"), sem("qk_out1")]
        splits = arena[:, 2048:2048 + 2 * 768].bitcast(BF16).rearrange("p (s r t) -> p s r t", s=2, r=3)
        rest = arena[:, 4096:4096 + 2 * 512].rearrange("p (s t) -> p s t", s=2)
        NF = 2 * KC * (T // 512)

        def qkv_phase(layer):
            def blk(u):
                qk, f, c = u // 4, u // 2 % 2, u % 2
                return qk, f, c

            with nc.Block() as block:
                @block.vector
                def _(dve):
                    with dve.Fori(0, B) as b:
                        n = b + B * 2 * layer
                        m = b + B * layer
                        ln_vector(dve, n, b)
                        for u in range(NF):
                            dve.wait_ge(qk_hi, 1 + NF * m + u + 1)
                            nc.vector.tensor_tensor(rest[:, u % 2, :], ps[:, 4 + u % 2, :], splits[:, u % 2, 0, :],
                                                    ALU.subtract).then_inc(qk_r, 1)
                            dve.wait_ge(qk_r, 1 + NF * m + u + 1)
                            nc.vector.tensor_copy(splits[:, u % 2, 1, :], rest[:, u % 2, :]).then_inc(qk_mid, 1)
                            dve.wait_ge(qk_mid, 1 + NF * m + u + 1)
                            nc.vector.tensor_tensor(splits[:, u % 2, 2, :], rest[:, u % 2, :], splits[:, u % 2, 1, :],
                                                    ALU.subtract).then_inc(qk_lo, 1)

                @block.scalar
                def _(act):
                    with act.Fori(0, B) as b:
                        n = b + B * 2 * layer
                        m = b + B * layer

                        def xT_free():
                            act.wait_ge(v_ps, 1 + TB * m)
                        ln_scalar(act, n, xT_free)
                        for u in range(NF):
                            act.wait_ge(qk_ps, 1 + NF * m + u + 1)
                            act.wait_ge(qk_out[u % 2], 1 + 16 * (NF // 2 * m + u // 2))
                            nc.scalar.activation(splits[:, u % 2, 0, :], ps[:, 4 + u % 2, :], ACT.Copy).then_inc(qk_hi, 1)
                        for t in range(TB):
                            act.wait_ge(v_ps, 1 + TB * m + t + 1)
                            nc.scalar.activation(v_all[:, bass.ds(b * G, G), t, :],
                                                 ps[:, 6 + t % 2, 0:D].rearrange("p (g c) -> p g c", g=G),
                                                 ACT.Copy).then_inc(v_done, 1)

                @block.tensor
                def _(pe):
                    if layer == 0:
                        pe.wait_ge(w_in["qkv0"], 1 + 16)
                    else:
                        pe.wait_ge(w_in["rest"], 1 + 16 * 10)
                    with pe.Fori(0, B) as b:
                        n = b + B * 2 * layer
                        m = b + B * layer

                        def banks_free():
                            pe.wait_ge(xT_done, 1 + 4 * n)
                        ln_tensor(pe, n, banks_free)
                        pe.wait_ge(xT_done, 1 + 4 * (n + 1))
                        for u in range(NF):
                            qk, f, c = blk(u)
                            pe.wait_ge(qk_r, 1 + NF * m + max(u - 1, 0))
                            for k in range(KC):
                                last = nc.tensor.matmul(ps[:, 4 + u % 2, :],
                                                        wqkv_sb[layer][:, k, qk * D + f * P:qk * D + (f + 1) * P],
                                                        xT[:, k, c * 512:(c + 1) * 512],
                                                        start=(k == 0), stop=(k == KC - 1))
                            last.then_inc(qk_ps, 1)
                        for t in range(TB):
                            pe.wait_ge(v_done, 1 + TB * m + max(t - 1, 0))
                            for k in range(KC):
                                last = nc.tensor.matmul(ps[:, 6 + t % 2, 0:D], xT[:, k, t * P:(t + 1) * P],
                                                        wqkv_sb[layer][:, k, 2 * D:3 * D],
                                                        start=(k == 0), stop=(k == KC - 1))
                            last.then_inc(v_ps, 1)

                @block.sync
                def _(sp):
                    with sp.Fori(0, B) as b:
                        m = b + B * layer
                        for u in range(NF):
                            qk, f, c = blk(u)
                            sp.wait_ge(qk_lo, 1 + NF * m + u + 1)
                            dst = scratch[layer, qk, :, bass.ds(b * D + f * P, P), c * 512:(c + 1) * 512]
                            sp.dma_start(dst.rearrange("r p t -> p r t"), splits[:, u % 2, :, :]).then_inc(qk_out[u % 2], 16)
                    for s in range(2):
                        sp.wait_ge(qk_out[s], 1 + 16 * NF // 2 * B * (layer + 1))

                if layer == 0:
                    @block.gpsimd
                    def _(pool):
                        pool.wait_ge(w_in["rest"], 1 + 16 * 10)
                        with pool.Fori(0, B) as b:
                            pool.wait_ge(xn_done, 1 + TB * (b + 1))
                            for t in range(TB):
                                nc.gpsimd.tensor_tensor(h[:, b * TB + t, :], h[:, b * TB + t, :], bproj_sb[:],
                                                        ALU.add).then_inc(res_bias, 1)

        stack_in = [sem("stack_in0"), sem("stack_in1")]
        stack_free, vg_ready, vg_free = sem("stack_free"), sem("vg_ready"), sem("vg_free")
        pv_done, oT_done, den_ps, den_done, rden_done, attn_done, bank_pv_free = (
            sem(n) for n in ("pv_done", "oT_done", "den_ps", "den_done", "rden_done", "attn_done", "bank_pv_free"))
        NP = 4
        probs = arena[:, 0:4096].rearrange("p (s j q) -> p s j q", s=NP, j=2)
        NX = 4
        soft = arena[:, 4096:8192].rearrange("p (s j q) -> p s j q", s=NX, j=2)

        def turn(step, lag, after):
            return [qc for qc in range(QC - 1) if step == 2 * LAST[qc] + 1 + lag + after]

        def load_stacks(sp, layer, it, par):
            for qk, parts in ((0, Q_PARTS), (1, K_PARTS)):
                for r, part in enumerate(parts):
                    src = scratch[layer, qk, part, bass.ds(it * 4 * HD, 4 * HD), :]
                    sp.dma_start(stacks[r * HD:(r + 1) * HD, par, qk, :, :],
                                 src.rearrange("(j d) t -> d j t", d=HD)).then_inc(stack_in[par], 16)

        def copy_values(pool, n, it):
            pool.wait_ge(vg_free, 1 + n)
            nc.gpsimd.tensor_copy(vg[:, :, :, 0:HD],
                                  v_all[:, it, :, :].rearrange("p t (j d) -> p t j d", j=4)).then_inc(vg_ready, 1)

        def pe_scores(dst, par, m, j, rows_):
            qc, i, cols = STRIPS[m]
            diag = i >= 4 * qc
            q0 = qc * 512 + 512 - cols
            last = nc.tensor.matmul(dst[:, 0:cols], stacks[0:rows_, par, 1, j, i * P:(i + 1) * P],
                                    stacks[0:rows_, par, 0, j, q0:q0 + cols], start=True, stop=not diag)
            if diag:
                last = nc.tensor.matmul(dst[:, 0:P], identb[:], mask_kq[:], start=False, stop=True)
            return last

        def pe_values(pe, n, m, bank):
            qc, i, cols = STRIPS[m]
            if m == 0:
                pe.wait_ge(vg_ready, 1 + n + 1)
            if i == 0:
                pe.wait_ge(oT_done, 1 + QC * n + qc)
            for j in range(4):
                u = 2 * m + j // 2
                last = nc.tensor.matmul(ps[32 * j:32 * j + 32, bank, 512 - cols:512], vg[:, i, j, :],
                                        probs[:, u % NP, j % 2, 0:cols], start=(i == 0), stop=(m == LAST[qc]))
            last.then_inc(pv_done, 1)

        def pe_spread(pe, n, qc, bank):
            pe.wait_ge(oT_done, 1 + QC * n + qc + 1)
            pe.wait_ge(den_done, 1 + QC * n + qc)
            nc.tensor.matmul(ps[:, bank, :], den_sel[:], oT[:], start=True, stop=True).then_inc(den_ps, 1)

        def act_sums(act, n, qc, bank):
            act.wait_ge(pv_done, 1 + NS * n + LAST[qc] + 1)
            act.wait_ge(attn_done, 1 + QC * n + qc)
            nc.scalar.activation(oT[:], ps[:, bank, :], ACT.Copy).then_inc(oT_done, 1)

        def act_den(act, n, qc, bank, layer):
            act.wait_ge(den_ps, 1 + QC * n + qc + 1)
            act.wait_ge(rden_done, 1 + QC * n + qc)
            if layer == 0:
                nc.scalar.activation(den[:], ps[:, bank, :], ACT.Identity, bias=eps_sb[:, 1:2]).then_inc(den_done, 1)
            else:
                nc.scalar.activation(den[:], ps[:, bank, :], ACT.Copy).then_inc(den_done, 1)

        def dve_rden(dve, n, qc):
            dve.wait_ge(den_done, 1 + QC * n + qc + 1)
            dve.wait_ge(attn_done, 1 + QC * n + qc)
            nc.vector.reciprocal(rden[:], den[:]).then_inc(rden_done, 1)

        def pool_norm(pool, n, it, qc):
            pool.wait_ge(rden_done, 1 + QC * n + qc + 1)
            nc.gpsimd.tensor_tensor(attnT[:, it, qc * 512:(qc + 1) * 512], oT[:], rden[:],
                                    ALU.mult).then_inc(attn_done, 1)

        sc_ps, e_done, cap_done, ln_done, mx_done = (
            sem(n) for n in ("sc_ps", "e_done", "cap_done", "ln_done", "mx_done"))
        sq_done = {e: sem(f"sq_{e}") for e in ("pool", "dve", "act")}
        SQ = ["act" if u % 4 == 1 else "pool" for u in range(NU)]
        SQ_N = {e: SQ.count(e) for e in sq_done}

        def sq_count(e, u):
            return sum(1 for x in SQ[:u + 1] if x == e)

        def softplus_attention():
            LAG = 5
            with nc.Block() as block:
                @block.sync
                def _(sp):
                    with sp.Fori(0, NG // 2) as i2:
                        for par in range(2):
                            it = 2 * i2 + par
                            sp.wait_ge(stack_free, 1 + it + 1)
                            load_stacks(sp, 0, it, par)

                @block.tensor
                def _(pe):
                    pe.sem_inc(stack_free, 2)
                    with pe.Fori(0, NG // 2) as i2:
                        for par in range(2):
                            it = 2 * i2 + par
                            pe.wait_ge(stack_in[par], 1 + 16 * 12 * (i2 + 1))
                            for step in range(NU + LAG):
                                if step < NU:
                                    u = step
                                    m, pair = UNITS[u]
                                    pe.wait_ge(mx_done, 1 + NU * it + u + 1)
                                    for jj in range(2):
                                        last = pe_scores(ps[:, 2 * (u % 3) + jj, :], par, m, 2 * pair + jj, KR)
                                    last.then_inc(sc_ps, 1)
                                v = step - LAG
                                if v >= 0 and v % 2 == 1:
                                    m = v // 2
                                    for e in ("pool", "dve", "act"):
                                        if e in SQ[v - 1:v + 1]:
                                            pe.wait_ge(sq_done[e], 1 + SQ_N[e] * it + sq_count(e, v))
                                    pe_values(pe, it, m, 6)
                                for qc in turn(step, LAG, 2):
                                    pe_spread(pe, it, qc, 7)
                            pe_spread(pe, it, QC - 1, 7)
                            pe.sem_inc(stack_free, 1)
                            pe.sem_inc(vg_free, 1)

                @block.scalar
                def _(act):
                    with act.Fori(0, NG) as it:
                        for u in range(NU):
                            cols = STRIPS[UNITS[u][0]][2]
                            x = soft[:, u % NX, :, 0:cols]
                            act.wait_ge(cap_done, 1 + NU * it + u + 1)
                            nc.scalar.activation(x, x, ACT.Exp).then_inc(e_done, 1)
                            act.wait_ge(e_done, 1 + NU * it + u + 1)
                            nc.scalar.activation(x, x, ACT.Ln, bias=1.0).then_inc(ln_done, 1)
                            if u >= 2 and SQ[u - 2] == "act":
                                pr = probs[:, (u - 2) % NP, :, 0:STRIPS[UNITS[u - 2][0]][2]]
                                act.wait_ge(mx_done, 1 + 3 + NU * it + u - 1)
                                nc.scalar.activation(pr, pr, ACT.Square).then_inc(sq_done["act"], 1)
                            for qc in turn(u, LAG, 0):
                                act_sums(act, it, qc, 6)
                            for qc in turn(u, LAG, 2):
                                act_den(act, it, qc, 7, 0)
                        act_sums(act, it, QC - 1, 6)
                        act_den(act, it, QC - 1, 7, 0)

                @block.vector
                def _(dve):
                    dve.sem_inc(mx_done, 3)
                    with dve.Fori(0, NG) as it:
                        for u in range(NU + 1):
                            if u < NU:
                                cols = STRIPS[UNITS[u][0]][2]
                                dve.wait_ge(sc_ps, 1 + NU * it + u + 1)
                                dve.wait_ge(mx_done, 1 + 3 + NU * it + max(u - NX + 1, 0))
                                nc.vector.tensor_scalar(soft[:, u % NX, :, 0:cols],
                                                        ps[:, 2 * (u % 3):2 * (u % 3) + 2, 0:cols],
                                                        HD ** -0.5, CAP, ALU.mult, ALU.min).then_inc(cap_done, 1)
                            if u >= 1:
                                v = u - 1
                                cols = STRIPS[UNITS[v][0]][2]
                                pr = probs[:, v % NP, :, 0:cols]
                                dve.wait_ge(ln_done, 1 + NU * it + v + 1)
                                dve.wait_ge(pv_done, 1 + NS * it + max(v // 2 - 1, 0))
                                nc.vector.scalar_tensor_tensor(pr, ps[:, 2 * (v % 3):2 * (v % 3) + 2, 0:cols],
                                                               HD ** -0.5, soft[:, v % NX, :, 0:cols],
                                                               ALU.mult, ALU.max).then_inc(mx_done, 1)
                                if SQ[v] == "dve":
                                    dve.wait_ge(mx_done, 1 + 3 + NU * it + v + 1)
                                    nc.vector.tensor_tensor(pr, pr, pr, ALU.mult).then_inc(sq_done["dve"], 1)
                            for qc in turn(u, LAG, 3):
                                dve_rden(dve, it, qc)
                        dve_rden(dve, it, QC - 1)

                @block.gpsimd
                def _(pool):
                    with pool.Fori(0, NG) as it:
                        copy_values(pool, it, it)
                        for v in range(NU):
                            cols = STRIPS[UNITS[v][0]][2]
                            if SQ[v] == "pool":
                                pr = probs[:, v % NP, :, 0:cols]
                                pool.wait_ge(mx_done, 1 + 3 + NU * it + v + 1)
                                nc.gpsimd.tensor_tensor(pr, pr, pr, ALU.mult).then_inc(sq_done["pool"], 1)
                            for qc in turn(v, LAG, 4):
                                pool_norm(pool, it, it, qc)
                        pool_norm(pool, it, it, QC - 1)

        proj_ps, proj_done = sem("proj_ps"), sem("proj_done")

        def proj_phase(layer):
            with nc.Block() as block:
                @block.tensor
                def _(pe):
                    for t in range(NT):
                        if NT * layer + t >= 4:
                            pe.wait_ge(proj_done, 1 + NT * layer + t - 3)
                        for g in range(G):
                            last = nc.tensor.matmul(ps[:, t % 4, 0:D],
                                                    attnT[:, t // TB * G + g, t % TB * P:(t % TB + 1) * P],
                                                    wproj_sb[layer][:, g, :], start=(g == 0), stop=(g == G - 1))
                        last.then_inc(proj_ps, 1)

                @block.vector
                def _(dve):
                    for t in range(NT):
                        dve.wait_ge(proj_ps, 1 + NT * layer + t + 1)
                        nc.vector.tensor_tensor(h[:, t, :], h[:, t, :], ps[:, t % 4, 0:D], ALU.add).then_inc(proj_done, 1)

                if layer == 0:
                    @block.sync
                    def _(sp):
                        sp.dma_start(wgu_sb, gate_up_w).then_inc(w_in["experts"], 16)
                        sp.dma_start(wdn_sb, down_w).then_inc(w_in["experts"], 16)

        r_ps, r_step, top_done, cw_exp, cw_done, cwT_ps, cwT_done, db_ps, db_done = (
            sem(n) for n in ("r_ps", "r_step", "top_done", "cw_exp", "cw_done", "cwT_ps", "cwT_done", "db_ps", "db_done"))
        gu_ps, sig_done, up_done, g_done, ga_done, a_done, dn_ps, dn_done = (
            sem(n) for n in ("gu_ps", "sig_done", "up_done", "g_done", "ga_done", "a_done", "dn_ps", "dn_done"))
        rs = sb("rs", [P, NE])
        top_v = sb("top_v", [P, NE])
        top_i = sb("top_i", [P, NE], U32)
        top_f = sb("top_f", [P, NE])
        gap = sb("gap", [P, 4])
        pick = sb("pick", [P, NE])
        cw = sb("cw", [P, TB, NE])
        cwT = sb("cwT", [NE, TB, P])
        sig = arena[:, 2048:3072].rearrange("p (s t) -> p s t", s=2)
        upc = arena[:, 3072:4096].rearrange("p (s t) -> p s t", s=2)
        gc = arena[:, 4096:5120].rearrange("p (s t) -> p s t", s=2)
        aT = arena[:, 5120:7168].rearrange("p (s k t) -> p s k t", s=2, k=2)
        NC_ = T // 512
        EU = NC_ * NE * 2
        ROUTE = 12

        def experts_phase():
            with nc.Block() as block:
                @block.vector
                def _(dve):
                    with dve.Fori(0, B) as b:
                        ln_vector(dve, b + B, b)
                        for t in range(TB):
                            n = TB * b + t
                            s0 = ROUTE * n
                            dve.wait_ge(r_ps, 1 + n + 1)

                            def step(ins, k):
                                ins.then_inc(r_step, 1)
                                dve.wait_ge(r_step, 1 + s0 + k)
                                plain(dve)
                            step(nc.vector.tensor_tensor(rs[:], ps[:, 4, t * NE:(t + 1) * NE], rb_sb[:], ALU.add), 1)
                            step(nc.vector.max(top_v[:], rs[:]), 2)
                            step(nc.vector.max_index(top_i[:], top_v[:], rs[:]), 3)
                            step(nc.vector.tensor_copy(top_f[:], top_i[:]), 4)
                            nc.vector.tensor_tensor(gap[:, 0:1], top_v[:, 1:2], top_v[:, 0:1],
                                                    ALU.subtract).then_inc(top_done, 1)
                            dve.wait_ge(cw_exp, 1 + n + 1)
                            step(nc.vector.tensor_scalar(gap[:, 2:3], gap[:, 1:2], 1.0, None, ALU.add), 5)
                            step(nc.vector.reciprocal(gap[:, 2:3], gap[:, 2:3]), 6)
                            step(nc.vector.tensor_tensor(gap[:, 3:4], gap[:, 1:2], gap[:, 2:3], ALU.mult), 7)
                            step(nc.vector.tensor_scalar(cw[:, t, :], expert_no[:], top_f[:, 0:1], gap[:, 2:3],
                                                         ALU.is_equal, ALU.mult), 8)
                            step(nc.vector.tensor_scalar(pick[:], expert_no[:], top_f[:, 1:2], gap[:, 3:4],
                                                         ALU.is_equal, ALU.mult), 9)
                            nc.vector.tensor_tensor(cw[:, t, :], cw[:, t, :], pick[:], ALU.add).then_inc(cw_done, 1)
                            dve.wait_ge(cwT_ps, 1 + n + 1)
                            nc.vector.tensor_copy(cwT[:, t, :], ps[0:NE, 5, 0:P]).then_inc(cwT_done, 1)
                            dve.wait_ge(db_ps, 1 + n + 1)
                            step(nc.vector.tensor_tensor(h[:, b * TB + t, :], h[:, b * TB + t, :], ps[:, 6, 0:D],
                                                         ALU.add), 10)
                            step(nc.vector.tensor_copy(gap[:, 0:1], top_f[:, 0:1]), 11)
                            step(nc.vector.tensor_copy(gap[:, 0:1], top_f[:, 0:1]), 12)
                        with dve.Fori(0, NC_) as c:
                            eb = (b * NC_ + c) * NE
                            for e in range(NE + 1):
                                for hc in range(2):
                                    if e == NE:
                                        break
                                    w = 2 * (eb + e) + hc
                                    s = hc
                                    dve.wait_ge(gu_ps, 1 + w + 1)
                                    nc.vector.tensor_scalar(upc[:, s, :], ps[:, 2 * s + 1, :], upb_sb[:, e, 2 + hc:3 + hc],
                                                            -6.0, ALU.add, ALU.max).then_inc(up_done, 1)
                                    dve.wait_ge(sig_done, 1 + w + 1)
                                    nc.vector.tensor_scalar(gc[:, s, :], ps[:, 2 * s, :], gub_sb[:, e, hc:hc + 1],
                                                            -7.0, ALU.add, ALU.max).then_inc(g_done, 1)
                                    dve.wait_ge(g_done, 1 + w + 1)
                                    nc.vector.scalar_tensor_tensor(gc[:, s, :], gc[:, s, :], 7.0, sig[:, s, :],
                                                                   ALU.min, ALU.mult).then_inc(ga_done, 1)
                                    dve.wait_ge(ga_done, 1 + w + 1)
                                    dve.wait_ge(up_done, 1 + w + 1)
                                    dve.wait_ge(dn_ps, 1 + 4 * (eb + max(e - 1, 0)))
                                    nc.vector.scalar_tensor_tensor(aT[:, e % 2, hc, :], upc[:, s, :], 8.0, gc[:, s, :],
                                                                   ALU.min, ALU.mult).then_inc(a_done, 1)
                                if e >= 1:
                                    for t in range(4):
                                        w = 4 * (eb + e - 1) + t
                                        tile = b * TB + c * 4 + t
                                        dve.wait_ge(dn_ps, 1 + w + 1)
                                        dve.wait_ge(dn_done, 1 + 4 * (eb + e - 1))
                                        nc.vector.scalar_tensor_tensor(
                                            h[:, tile, :], ps[:, 4 + t, 0:D], cw[:, c * 4 + t, e - 1:e],
                                            h[:, tile, :], ALU.mult, ALU.add).then_inc(dn_done, 1)

                @block.scalar
                def _(act):
                    with act.Fori(0, B) as b:
                        def xT_free():
                            act.wait_ge(gu_ps, 1 + EU * b)
                        ln_scalar(act, b + B, xT_free)
                        for t in range(TB):
                            act.wait_ge(top_done, 1 + TB * b + t + 1)
                            nc.scalar.activation(gap[:, 1:2], gap[:, 0:1], ACT.Exp).then_inc(cw_exp, 1)
                        with act.Fori(0, NC_) as c:
                            for e in range(NE):
                                for hc in range(2):
                                    w = 2 * ((b * NC_ + c) * NE + e) + hc
                                    act.wait_ge(gu_ps, 1 + w + 1)
                                    act.wait_ge(ga_done, 1 + 2 * ((b * NC_ + c) * NE + max(e - 1, 0)) + (hc + 1 if e else 0))
                                    nc.scalar.activation(sig[:, hc, :], ps[:, 2 * hc, :], ACT.Sigmoid,
                                                         bias=sgb_sb[:, e, hc:hc + 1], scale=1.702).then_inc(sig_done, 1)

                @block.tensor
                def _(pe):
                    with pe.Fori(0, B) as b:
                        def banks_free():
                            pe.wait_ge(g_done, 1 + EU * b)
                        ln_tensor(pe, b + B, banks_free)
                        pe.wait_ge(xT_done, 1 + 4 * (b + B + 1))
                        pe.wait_ge(dn_done, 1 + EU * 2 * b)
                        for t in range(TB):
                            n = TB * b + t
                            if t >= 1:
                                pe.wait_ge(r_step, 1 + ROUTE * n)
                            for k in range(KC):
                                last = nc.tensor.matmul(ps[:, 4, t * NE:(t + 1) * NE], xT[:, k, t * P:(t + 1) * P],
                                                        rw_sb[:, k, :], start=(k == 0), stop=(k == KC - 1))
                            last.then_inc(r_ps, 1)
                            pe.wait_ge(cw_done, 1 + n + 1)
                            nc.tensor.transpose(ps[0:NE, 5, 0:P], cw[:, t, :], ident[:]).then_inc(cwT_ps, 1)
                            pe.wait_ge(cwT_done, 1 + n + 1)
                            nc.tensor.matmul(ps[:, 6, 0:D], cwT[:, t, :], dnb_sb[:], start=True, stop=True).then_inc(db_ps, 1)
                        pe.wait_ge(r_step, 1 + ROUTE * TB * (b + 1))
                        pe.wait_ge(w_in["experts"], 1 + 32)
                        plain(pe)
                        with pe.Fori(0, NC_) as c:
                            eb = (b * NC_ + c) * NE
                            for e in range(NE + 1):
                                if e < NE:
                                    for hc in range(2):
                                        if e >= 1:
                                            pe.wait_ge(g_done, 1 + 2 * (eb + e - 1) + hc + 1)
                                            pe.wait_ge(up_done, 1 + 2 * (eb + e - 1) + hc + 1)
                                        else:
                                            pe.wait_ge(g_done, 1 + 2 * eb)
                                            pe.wait_ge(up_done, 1 + 2 * eb)
                                        for gu in range(2):
                                            for k in range(KC):
                                                f = gu * 2 * P + hc * P
                                                last = nc.tensor.matmul(ps[:, 2 * hc + gu, :],
                                                                        wgu_sb[:, e, k, f:f + P],
                                                                        xT[:, k, bass.ds(c * 512, 512)],
                                                                        start=(k == 0), stop=(k == KC - 1))
                                        last.then_inc(gu_ps, 1)
                                if e >= 1:
                                    pe.wait_ge(a_done, 1 + 2 * (eb + e))
                                    for t in range(4):
                                        if e >= 2:
                                            pe.wait_ge(dn_done, 1 + 4 * (eb + e - 2) + t + 1)
                                        else:
                                            pe.wait_ge(dn_done, 1 + 4 * eb)
                                        for k in range(2):
                                            last = nc.tensor.matmul(ps[:, 4 + t, 0:D],
                                                                    aT[:, (e - 1) % 2, k, t * P:(t + 1) * P],
                                                                    wdn_sb[:, e - 1, k, :],
                                                                    start=(k == 0), stop=(k == 1))
                                        last.then_inc(dn_ps, 1)

        MAXES = [(j, t, k0, min(512, (t + 1) * P - k0)) for t in range(TB) for j in range(4)
                 for k0 in range(0, (t + 1) * P, 512)]
        NM = len(MAXES)
        am_ps, am_done, am_all, mT_ps, m_step, m_out = (
            sem(n) for n in ("am_ps", "am_done", "am_all", "mT_ps", "m_step", "m_out"))
        sb_ps, p_done, ones_done = sem("sb_ps"), sem("p_done"), sem("ones_done")
        mx1 = sb("mx1", [P, 4, TB])
        mx2 = sb("mx2", [P, 4, TB])
        m_rest = sb("m_rest", [4 * TB, P])
        m_parts = sb("m_parts", [4 * TB, 3, P], BF16)
        FIRST = 6

        def maxes_after(u):
            done = NM * max(u + 1 - FIRST, 0) // (NU - FIRST)
            before = NM * max(u - FIRST, 0) // (NU - FIRST)
            return range(before, done)

        def softmax_attention():
            LAG = 3

            def pe_max(pe, n, par, w):
                j, t, k0, keys = MAXES[w]
                diag = k0 + keys == (t + 1) * P
                pe.wait_ge(am_done, 1 + NM * n + w + 1)
                if w == 0:
                    pe.wait_ge(stack_in[par], 1 + 16 * 12 * (NG // 2 + n // 2 + 1)) if isinstance(n, int) else None
                bank = 4 + w % 2
                last = nc.tensor.matmul(ps[:, bank, 0:keys], stacks[0:KR, par, 0, j, t * P:(t + 1) * P],
                                        stacks[0:KR, par, 1, j, k0:k0 + keys], start=True, stop=not diag)
                if diag:
                    last = nc.tensor.matmul(ps[:, bank, keys - P:keys], identb[:], mask_qk[:], start=False, stop=True)
                last.then_inc(am_ps, 1)

            def pe_maxT(pe, n):
                pe.wait_ge(am_all, 1 + n + 1)
                pe.wait_ge(den_done, 1 + QC * (NG + n))
                nc.tensor.transpose(ps[0:4 * TB, 7, 0:P], mx1[:].rearrange("p j t -> p (j t)"),
                                    ident[:]).then_inc(mT_ps, 1)

            def dve_max(dve, n, w):
                j, t, k0, keys = MAXES[w]
                dve.wait_ge(am_ps, 1 + NM * n + w + 1)
                if w == 0:
                    dve.wait_ge(mT_ps, 1 + n)
                dst = (mx2 if k0 else mx1)[:, j, t:t + 1]
                nc.vector.reduce_max(dst, ps[:, 4 + w % 2, 0:keys], AX.X).then_inc(am_done, 1)

            def dve_max_parts(dve, n):
                dve.wait_ge(am_done, 1 + 2 + NM * (n + 1))
                nc.vector.tensor_tensor(mx1[:, :, 4:TB], mx1[:, :, 4:TB], mx2[:, :, 4:TB], ALU.max).then_inc(am_all, 1)
                dve.wait_ge(mT_ps, 1 + n + 1)
                dve.wait_ge(m_out, 1 + 48 * n)
                src = ps[0:4 * TB, 7, 0:P]
                nc.vector.tensor_scalar(m_parts[:, 0, :], src, -1.0, None, ALU.mult).then_inc(m_step, 1)
                dve.wait_ge(m_step, 1 + 4 * n + 1)
                nc.vector.scalar_tensor_tensor(m_rest[:], src, -1.0, m_parts[:, 0, :], ALU.mult,
                                               ALU.subtract).then_inc(m_step, 1)
                dve.wait_ge(m_step, 1 + 4 * n + 2)
                nc.vector.tensor_copy(m_parts[:, 1, :], m_rest[:]).then_inc(m_step, 1)
                dve.wait_ge(m_step, 1 + 4 * n + 3)
                nc.vector.tensor_tensor(m_parts[:, 2, :], m_rest[:], m_parts[:, 1, :], ALU.subtract).then_inc(m_step, 1)

            def sp_maxima(sp, n, par):
                sp.wait_ge(m_step, 1 + 4 * (n + 1))
                for s in range(3):
                    sp.dma_start(stacks[KR + s:KR + s + 1, par, 0, :, :].rearrange("o j (t q) -> o (j t) q", q=P),
                                 m_parts[:, s, :]).then_inc(m_out, 16)

            def pairs(eng, body, tail):
                with eng.Fori(0, NG // 2 - 1) as i2:
                    for par in range(2):
                        body(2 * i2 + par, i2, par, True)
                for par in range(2):
                    body(NG - 2 + par, NG // 2 - 1, par, par == 0)
                tail()

            with nc.Block() as block:
                @block.sync
                def _(sp):
                    for par in range(2):
                        sp.wait_ge(ones_done, 1 + 1)
                        load_stacks(sp, 1, par, par)
                    sp_maxima(sp, 0, 0)

                    def body(it, i2, par, more):
                        if more:
                            sp_maxima(sp, it + 1, 1 - par)

                    with sp.Fori(0, NG // 2 - 1) as i2:
                        for par in range(2):
                            it = 2 * i2 + par
                            sp_maxima(sp, it + 1, 1 - par)
                            sp.wait_ge(stack_free, 1 + 2 + NG + it + 1)
                            load_stacks(sp, 1, it + 2, par)
                    sp_maxima(sp, NG - 1, 1)

                @block.tensor
                def _(pe):
                    pe.wait_ge(stack_in[0], 1 + 16 * 12 * (NG // 2 + 1))
                    for w in range(NM):
                        pe_max(pe, 0, 0, w)
                    pe_maxT(pe, 0)

                    def body(it, i2, par, more):
                        n = NG + it
                        pe.wait_ge(m_out, 1 + 48 * (it + 1))
                        for step in range(NU + LAG):
                            if step < NU:
                                u = step
                                m, pair = UNITS[u]
                                pe.wait_ge(p_done, 1 + NU * it + u + 1)
                                for jj in range(2):
                                    last = pe_scores(ps[:, 2 * (u % 2) + jj, :], par, m, 2 * pair + jj, KR + 3)
                                last.then_inc(sb_ps, 1)
                                if more:
                                    for w in maxes_after(u):
                                        if w == 0:
                                            nxt = i2 + (1 if par == 1 else 0)
                                            pe.wait_ge(stack_in[1 - par], 1 + 16 * 12 * (NG // 2 + 1 + nxt))
                                        pe_max_units(pe, it + 1, 1 - par, w)
                            v = step - LAG
                            if v >= 0 and v % 2 == 1:
                                m = v // 2
                                pe.wait_ge(p_done, 1 + 2 + NU * it + v + 1)
                                pe_values(pe, n, m, 6)
                            for qc in turn(step, LAG, 2):
                                pe_spread(pe, n, qc, 7)
                        pe_spread(pe, n, QC - 1, 7)
                        pe.sem_inc(stack_free, 1)
                        pe.sem_inc(vg_free, 1)
                        if more:
                            pe_maxT(pe, it + 1)

                    def pe_max_units(pe, n, par, w):
                        j, t, k0, keys = MAXES[w]
                        diag = k0 + keys == (t + 1) * P
                        pe.wait_ge(am_done, 1 + NM * n + w + 1)
                        bank = 4 + w % 2
                        last = nc.tensor.matmul(ps[:, bank, 0:keys], stacks[0:KR, par, 0, j, t * P:(t + 1) * P],
                                                stacks[0:KR, par, 1, j, k0:k0 + keys], start=True, stop=not diag)
                        if diag:
                            last = nc.tensor.matmul(ps[:, bank, keys - P:keys], identb[:], mask_qk[:],
                                                    start=False, stop=True)
                        last.then_inc(am_ps, 1)

                    pairs(pe, body, lambda: None)

                @block.scalar
                def _(act):
                    act.sem_inc(p_done, 2)

                    def body(it, i2, par, more):
                        n = NG + it
                        for u in range(NU):
                            cols = STRIPS[UNITS[u][0]][2]
                            act.wait_ge(sb_ps, 1 + NU * it + u + 1)
                            act.wait_ge(pv_done, 1 + NS * n + max(u // 2 - 1, 0))
                            nc.scalar.activation(probs[:, u % NP, :, 0:cols],
                                                 ps[:, 2 * (u % 2):2 * (u % 2) + 2, 0:cols],
                                                 ACT.Exp, scale=HD ** -0.5).then_inc(p_done, 1)
                            for qc in turn(u, LAG, 0):
                                act_sums(act, n, qc, 6)
                            for qc in turn(u, LAG, 2):
                                act_den(act, n, qc, 7, 1)
                        act_sums(act, n, QC - 1, 6)
                        act_den(act, n, QC - 1, 7, 1)
                    with act.Fori(0, NG) as it:
                        body(it, None, None, True)

                @block.vector
                def _(dve):
                    dve.sem_inc(am_done, 2)
                    for w in range(NM):
                        dve_max(dve, 0, w)
                    dve_max_parts(dve, 0)

                    def body(it, more):
                        n = NG + it
                        for u in range(NU):
                            if more:
                                for w in maxes_after(u):
                                    dve_max(dve, it + 1, w)
                            for qc in turn(u, LAG, 3):
                                dve_rden(dve, n, qc)
                        dve_rden(dve, n, QC - 1)
                        if more:
                            dve_max_parts(dve, it + 1)
                    with dve.Fori(0, NG - 1) as it:
                        body(it, True)
                    body(NG - 1, False)

                @block.gpsimd
                def _(pool):
                    nc.gpsimd.memset(stacks[KR:KR + 3, :, 1, :, :], 1.0).then_inc(ones_done, 1)
                    pool.wait_ge(ones_done, 1 + 1)
                    with pool.Fori(0, NG) as it:
                        copy_values(pool, NG + it, it)
                        for qc in range(QC):
                            pool_norm(pool, NG + it, it, qc)

        hid_ps, hid_done, mo_ps, mo_done = sem("hid_ps"), sem("hid_done"), sem("mo_ps"), sem("mo_done")
        b2_done, stored = sem("b2_done"), sem("stored")
        hT = arena[:, 2048:2048 + 8192].rearrange("p (s c t) -> p s c t", s=2, c=HC)

        def mlp_phase():
            with nc.Block() as block:
                @block.vector
                def _(dve):
                    with dve.Fori(0, B) as b:
                        ln_vector(dve, b + 3 * B, b)
                        for c in range(NC_):
                            for t in range(4):
                                w = b * TB + c * 4 + t
                                dve.wait_ge(b2_done, 1 + TB * (b + 1))
                                dve.wait_ge(mo_ps, 1 + w + 1)
                                nc.vector.tensor_tensor(h[:, w, :], h[:, w, :], ps[:, 6 + t % 2, 0:D],
                                                        ALU.add).then_inc(mo_done, 1)

                @block.gpsimd
                def _(pool):
                    with pool.Fori(0, B) as b:
                        pool.wait_ge(xn_done, 1 + TB * (b + 3 * B + 1))
                        for t in range(TB):
                            nc.gpsimd.tensor_tensor(h[:, b * TB + t, :], h[:, b * TB + t, :], b2_sb[:],
                                                    ALU.add).then_inc(b2_done, 1)

                @block.scalar
                def _(act):
                    with act.Fori(0, B) as b:
                        def xT_free():
                            act.wait_ge(hid_ps, 1 + HC * NC_ * b)
                        ln_scalar(act, b + 3 * B, xT_free)
                        for c in range(NC_):
                            for f in range(HC):
                                w = (b * NC_ + c) * HC + f
                                act.wait_ge(hid_ps, 1 + w + 1)
                                act.wait_ge(mo_ps, 1 + TB * b)
                                nc.scalar.activation(hT[:, c, f, :], ps[:, 4 * (f // 2 % 2) // 4 * 0 + [0, 1, 4, 5][f % 4], :],
                                                     ACT.Gelu, bias=b1_sb[:, f:f + 1]).then_inc(hid_done, 1)

                @block.tensor
                def _(pe):
                    with pe.Fori(0, B) as b:
                        def banks_free():
                            pe.wait_ge(hid_done, 1 + HC * NC_ * b)
                        ln_tensor(pe, b + 3 * B, banks_free)
                        pe.wait_ge(xT_done, 1 + 4 * (b + 3 * B + 1))
                        for c in range(NC_ + 1):
                            if c < NC_:
                                for f in range(HC):
                                    w = (b * NC_ + c) * HC + f
                                    if c == 0 and f < 4:
                                        pe.wait_ge(hid_done, 1 + b * NC_ * HC)
                                    else:
                                        pe.wait_ge(hid_done, 1 + w - 3)
                                    for k in range(KC):
                                        last = nc.tensor.matmul(ps[:, [0, 1, 4, 5][f % 4], :],
                                                                w1T_sb[:, k, f * P:(f + 1) * P],
                                                                xT[:, k, c * 512:(c + 1) * 512],
                                                                start=(k == 0), stop=(k == KC - 1))
                                    last.then_inc(hid_ps, 1)
                            if c >= 1:
                                pe.wait_ge(hid_done, 1 + (b * NC_ + c) * HC)
                                for t in range(4):
                                    w = b * TB + (c - 1) * 4 + t
                                    if c == 1 and t < 2:
                                        pe.wait_ge(mo_done, 1 + b * TB)
                                    else:
                                        pe.wait_ge(mo_done, 1 + w - 1)
                                    for f in range(HC):
                                        last = nc.tensor.matmul(ps[:, 6 + t % 2, 0:D], hT[:, c - 1, f, t * P:(t + 1) * P],
                                                                w2T_sb[:, f, :], start=(f == 0), stop=(f == HC - 1))
                                    last.then_inc(mo_ps, 1)

                @block.sync
                def _(sp):
                    with sp.Fori(0, NT) as w:
                        sp.wait_ge(mo_done, 1 + w + 1)
                        sp.dma_start(out[bass.ds(w * P, P), :], h[:, w, :]).then_inc(stored, 16)
                    sp.wait_ge(stored, 1 + 16 * NT)

        with nc.Block() as block:
            @block.sync
            def _(sp):
                for s in semaphores[0::5]:
                    sp.sem_inc(s, 1)

            @block.vector
            def _(dve):
                for s in semaphores[1::5]:
                    dve.sem_inc(s, 1)

            @block.scalar
            def _(act):
                for s in semaphores[2::5]:
                    act.sem_inc(s, 1)

            @block.tensor
            def _(pe):
                for s in semaphores[3::5]:
                    pe.sem_inc(s, 1)

            @block.gpsimd
            def _(pool):
                for s in semaphores[4::5]:
                    pool.sem_inc(s, 1)

        embed_phase()
        qkv_phase(0)
        softplus_attention()
        proj_phase(0)
        experts_phase()
        qkv_phase(1)
        softmax_attention()
        proj_phase(1)
        mlp_phase()


def kernel(**inputs):
    import numpy as np
    import concourse.bacc as bacc
    from concourse.bass_utils import run_bass_kernel_spmd

    a = {k: np.asarray(v) for k, v in inputs.items()}
    D, G = 256, 4

    def chunks(w):
        return w.reshape(-1, P, w.shape[-1]).transpose(1, 0, 2)

    def padded(w):
        r = np.zeros((4, 32, G, D), np.float32)
        r[:, :16] = w.T.reshape(G, 4, 16, D).transpose(1, 2, 0, 3)
        return r.reshape(P, G, D)

    gu = a["L0_ffn_gate_up_w"]
    gub = a["L0_ffn_gate_up_b"]
    gu = np.concatenate([gu[:, 0::2], gu[:, 1::2]], 1)
    gub = np.concatenate([gub[:, 0::2], gub[:, 1::2]], 1)
    arrays = {
        "ids": a["x"].reshape(-1, P).T,
        "W0": a["L0_tok_W0"],
        "w1_tok": chunks(a["L0_tok_W1"]),
        "wqkv0": chunks(a["L0_attn_w_qkv"].T),
        "wproj0": padded(a["L0_attn_w_proj"]),
        "bproj0": a["L0_attn_b_proj"][None],
        "router_w": chunks(a["L0_ffn_router_w"].T),
        "router_b": a["L0_ffn_router_b"][None],
        "gate_up_w": gu.transpose(2, 0, 1).reshape(2, P, 8, 512).transpose(1, 2, 0, 3),
        "gate_up_b": gub.reshape(8, 4, P).transpose(2, 0, 1),
        "down_w": a["L0_ffn_down_w"].transpose(2, 0, 1).reshape(2, P, 8, D).transpose(1, 2, 0, 3),
        "down_b": a["L0_ffn_down_b"],
        "wqkv1": chunks(np.concatenate([a["L1_attn_Wq"], a["L1_attn_Wk"], a["L1_attn_Wv"]], 0).T),
        "wproj1": padded(a["L1_attn_Wo"]),
        "w1": chunks(a["L1_ffn_w1"]),
        "b1": a["L1_ffn_b1"].reshape(-1, P).T,
        "w2": chunks(a["L1_ffn_w2"]),
        "b2": a["L1_ffn_b2"][None],
    }
    arrays = {k: np.ascontiguousarray(v) for k, v in arrays.items()}
    nc = bacc.Bacc("TRN2", target_bir_lowering=False, num_devices=1)
    args = [nc.dram_tensor(f"in_{k}", v.shape, mybir.dt.from_np(v.dtype), kind="ExternalInput").ap()
            for k, v in arrays.items()]
    tokens = a["x"].size
    out = nc.dram_tensor("out", (tokens, D), F32, kind="ExternalOutput").ap()
    lm_tower(nc, *args, out)
    r = run_bass_kernel_spmd(nc, [{f"in_{k}": v for k, v in arrays.items()}], core_ids=[0])
    return r.results[0]["out"].reshape(*a["x"].shape, D)
```

```python
from contextlib import ExitStack

import concourse.bass as bass
from concourse import mybir

F32 = mybir.dt.float32
F32R = mybir.dt.float32r
BF16 = mybir.dt.bfloat16
I32 = mybir.dt.int32
U32 = mybir.dt.uint32
ALU = mybir.AluOpType
ACT = mybir.ActivationFunctionType
AX = mybir.AxisListType

P = 128
EPS = 1e-5
NEG = -1e30
CAP = 40.0


def lm_tower(nc, ids, W0, w1_tok, wqkv0, wproj0, bproj0, router_w, router_b, expert_w, gate_up_b,
             down_b, wqkv1, wproj1, w1, b1, w2, b2, out):
    NT = ids.shape[1]
    VOCAB, KD = W0.shape
    D = out.shape[1]
    B = 2
    TB = NT // B
    T = TB * P
    KT = KD // P
    KC = D // P
    H, HD = 16, 16
    G = H // 4
    NG = B * G
    NE = router_w.shape[2]
    HC = w1.shape[1]
    QC = T // 512
    CW = 4 * HD
    KR = 6 * HD
    Q_PARTS, K_PARTS = (0, 0, 0, 1, 1, 2), (0, 1, 2, 0, 1, 0)

    STRIPS = [(qc, i, 512 - P * max(0, i - 4 * qc)) for qc in range(QC) for n in range(2 * qc + 2)
              for i in (n, 4 * qc + 3 - n)]
    NC_ = T // 512
    NS = len(STRIPS)
    UNITS = [(m, heads) for m in range(NS) for heads in (((0, 1, 2, 3),) if STRIPS[m][2] <= 256 else ((0, 1), (2, 3)))]
    NU = len(UNITS)
    OF_STRIP = [[u for u in range(NU) if UNITS[u][0] == m] for m in range(NS)]
    LAST = {qc: max(m for m, s in enumerate(STRIPS) if s[0] == qc) for qc in range(QC)}

    scratch = nc.dram_tensor("qk_parts", (2, 2, 3, B * D, T), BF16, kind="Internal").ap()

    with ExitStack() as ctx:
        semaphores = []

        def sem(name):
            semaphores.append(ctx.enter_context(nc.semaphore(name)))
            return semaphores[-1]

        waited = sem("waited")

        def plain(eng):
            eng.sem_inc(waited, 1)

        def sb(name, shape, dt=F32, scope=ctx):
            return scope.enter_context(nc.sbuf_tensor(name, shape, dt))

        ps = ctx.enter_context(nc.psum_tensor("ps", [P, 8, 512], F32))

        h = sb("h", [P, NT, D])
        w1t_sb = sb("w1t_sb", [P, KT, D])
        wqkv_sb = [sb(f"wqkv_sb{n}", [P, KC, 3 * D]) for n in range(2)]
        wproj_sb = [sb(f"wproj_sb{n}", [P, KC, D]) for n in range(2)]
        bproj_sb = sb("bproj_sb", [P, D])
        rw_sb = sb("rw_sb", [P, KC, NE])
        rb_sb = sb("rb_sb", [P, NE])
        gub_sb = sb("gub_sb", [P, NE, 4])
        sgb_sb = sb("sgb_sb", [P, NE, 4])
        upb_sb = sb("upb_sb", [P, NE, 4])
        dnb_sb = sb("dnb_sb", [NE, D])
        w1T = [sb(f"w1T{n}", [P, KC, HC * P], F32R) for n in range(2)]
        w2T = [sb(f"w2T{n}", [P, HC, D], F32R) for n in range(2)]
        b1_sb = sb("b1_sb", [P, HC])
        b2_sb = sb("b2_sb", [P, D])
        ids_sb = sb("ids_sb", [P, NT], I32)

        ident = sb("ident", [P, P])
        identb = sb("identb", [P, P], BF16)
        mask_qk = sb("mask_qk", [P, P], BF16)
        mask_kq = sb("mask_kq", [P, P], BF16)
        expert_no = sb("expert_no", [P, NE])
        eps_sb = sb("eps_sb", [P, 1])

        stats = sb("stats", [P, TB, 6])
        mv = sb("mv", [P, TB, 2])
        sd = sb("sd", [P, TB])
        rsd = sb("rsd", [P, TB])

        w_in = {n: sem(f"w_in_{n}") for n in ("tok", "qkv0", "mlp", "rest", "ids")}
        const_made = sem("const_made")
        id_step, ids_ready = sem("id_step"), sem("ids_ready")
        gathered = [ctx.enter_context(nc.semaphore(f"gathered{t}")) for t in range(TB)]
        rows_T, rows_Tc = sem("rows_T"), sem("rows_Tc")
        emb_done, h_ready = sem("emb_done"), sem("h_ready")
        alpha_step, sign_done, eff_done, wT_ps, wT_hi, wT_lo = (
            sem(n) for n in ("alpha_step", "sign_done", "eff_done", "wT_ps", "wT_hi", "wT_lo"))

        W_BLOCKS = [("w1", c, k) for k in range(KC) for c in range(HC)] + \
                   [("w2", k, c) for c in range(HC) for k in range(KC)]

        def embed_phase():
            with ExitStack() as scope:
                rows = sb("rows", [P, TB, KD], scope=scope)
                rowsT = sb("rowsT", [P, 2, KD], scope=scope)
                raw_w1 = sb("raw_w1", [P, HC, D], scope=scope)
                raw_w2 = sb("raw_w2", [P, KC, HC * P], scope=scope)
                sgn_w1 = sb("sgn_w1", [P, HC, D], scope=scope)
                sgn_w2 = sb("sgn_w2", [P, KC, HC * P], scope=scope)
                alpha = sb("alpha", [P, HC + KC], scope=scope)
                idf = sb("idf", [P, TB], scope=scope)
                idn = sb("idn", [P, TB], scope=scope)
                idc = sb("idc", [P, TB], U32, scope=scope)
                tok_scale = sb("tok_scale", [P, TB], scope=scope)
                block = scope.enter_context(nc.Block())

                @block.sync
                def _(sp):
                    sp.dma_start(ids_sb[:], ids).then_inc(w_in["ids"], 16)
                    sp.dma_start(w1t_sb[:], w1_tok).then_inc(w_in["tok"], 16)
                    sp.dma_start(raw_w1[:], w1).then_inc(w_in["mlp"], 16)
                    sp.dma_start(raw_w2[:], w2).then_inc(w_in["mlp"], 16)
                    sp.dma_start(wqkv_sb[0][:], wqkv0).then_inc(w_in["qkv0"], 16)
                    for dst, src in ((wqkv_sb[1], wqkv1), (wproj_sb[0], wproj0), (wproj_sb[1], wproj1),
                                     (rw_sb, router_w), (gub_sb, gate_up_b), (dnb_sb, down_b),
                                     (b1_sb, b1)):
                        sp.dma_start(dst[:], src).then_inc(w_in["rest"], 16)
                    for dst, src in ((bproj_sb, bproj0), (rb_sb, router_b), (b2_sb, b2)):
                        sp.dma_start(dst[:], src.to_broadcast((P, src.shape[1]))).then_inc(w_in["rest"], 16)

                @block.gpsimd
                def _(pool):
                    for m in (ident, identb, mask_qk, mask_kq):
                        nc.gpsimd.memset(m[:], 0.0).then_inc(const_made, 1)
                    pool.wait_ge(const_made, 1 + 4)
                    for m in (ident, identb):
                        nc.gpsimd.affine_select(out=m[:], in_=m[:], compare_op=ALU.not_equal, fill=1.0, base=0,
                                                pattern=[[-1, P]], channel_multiplier=1).then_inc(const_made, 1)
                    nc.gpsimd.affine_select(out=mask_qk[:], in_=mask_qk[:], compare_op=ALU.is_ge, fill=NEG, base=0,
                                            pattern=[[-1, P]], channel_multiplier=1).then_inc(const_made, 1)
                    nc.gpsimd.affine_select(out=mask_kq[:], in_=mask_kq[:], compare_op=ALU.is_ge, fill=NEG, base=0,
                                            pattern=[[1, P]], channel_multiplier=-1).then_inc(const_made, 1)
                    nc.gpsimd.iota(expert_no[:], pattern=[[1, NE]], base=0, channel_multiplier=0,
                                   allow_small_or_imprecise_dtypes=True).then_inc(const_made, 1)
                    with pool.Fori(0, B) as b:
                        pool.wait_ge(ids_ready, 1 + b + 1)
                        pool.wait_ge(rows_T, 1 + TB * b)
                        plain(pool)
                        for t in range(TB):
                            nc.gpsimd.indirect_dma_start(
                                rows[:, t, :], None, W0, bass.IndirectOffsetOnAxis(ap=idc[:, t:t + 1], axis=0),
                            ).then_inc(gathered[t], 16)

                def w_dst(part, n):
                    if n < 4:
                        return w1T[part][:, n // 2, (n % 2) * 512:(n % 2) * 512 + 512]
                    return w2T[part][:, 2 * (n - 4):2 * (n - 4) + 2, :].rearrange("p c d -> p (c d)")

                @block.vector
                def _(dve):
                    nc.vector.memset(eps_sb[:], EPS)
                    dve.wait_ge(w_in["ids"], 1 + 16)
                    with dve.Fori(0, B) as b:
                        dve.wait_ge(rows_T, 1 + TB * b)
                        dve.wait_ge(h_ready, 1 + TB * b)
                        nc.vector.tensor_copy(idf[:], ids_sb[:, bass.ds(b * TB, TB)]).then_inc(id_step, 1)
                        dve.wait_ge(id_step, 1 + 4 * b + 1)
                        nc.vector.tensor_scalar(idn[:], idf[:], 0.0, float(VOCAB), ALU.is_lt,
                                                ALU.mult).then_inc(id_step, 1)
                        nc.vector.tensor_scalar(tok_scale[:], idf[:], 0.0, float(D) ** 0.5, ALU.not_equal,
                                                ALU.mult).then_inc(id_step, 1)
                        dve.wait_ge(id_step, 1 + 4 * b + 3)
                        nc.vector.tensor_tensor(idn[:], idn[:], idf[:], ALU.add).then_inc(id_step, 1)
                        dve.wait_ge(id_step, 1 + 4 * b + 4)
                        nc.vector.tensor_scalar(idc[:], idn[:], float(VOCAB - 1), 0.0, ALU.min,
                                                ALU.max).then_inc(ids_ready, 1)
                        for t in range(TB):
                            dve.wait_ge(emb_done, 1 + TB * b + t + 1)
                            nc.vector.tensor_scalar(h[:, b * TB + t, :], ps[:, 2 + t % 2, 0:D], tok_scale[:, t:t + 1],
                                                    None, ALU.mult).then_inc(h_ready, 1)
                    dve.wait_ge(w_in["mlp"], 1 + 32)
                    nc.vector.tensor_reduce(alpha[:, 0:HC], raw_w1[:], AX.X, ALU.add,
                                            apply_absolute_value=True).then_inc(alpha_step, 1)
                    nc.vector.tensor_reduce(alpha[:, HC:HC + KC], raw_w2[:], AX.X, ALU.add,
                                            apply_absolute_value=True).then_inc(alpha_step, 1)
                    dve.wait_ge(alpha_step, 1 + 2)
                    nc.vector.tensor_scalar(alpha[:, 0:HC], alpha[:, 0:HC], 1.0 / D, None,
                                            ALU.mult).then_inc(alpha_step, 1)
                    nc.vector.tensor_scalar(alpha[:, HC:HC + KC], alpha[:, HC:HC + KC], 1.0 / (HC * P), None,
                                            ALU.mult).then_inc(alpha_step, 1)
                    dve.wait_ge(alpha_step, 1 + 4)
                    parts = [(sgn_w1[:, c, :], raw_w1[:, c, :], alpha[:, c:c + 1]) for c in range(HC)] + \
                            [(sgn_w2[:, k, :], raw_w2[:, k, :], alpha[:, HC + k:HC + k + 1]) for k in range(KC)]
                    for n, (sg, w, al) in enumerate(parts):
                        dve.wait_ge(sign_done, 1 + (1 if n < HC else 2))
                        nc.vector.scalar_tensor_tensor(sg, sg, al, w, ALU.mult, ALU.subtract).then_inc(eff_done, 1)
                    for n, (sg, w, al) in enumerate(parts):
                        dve.wait_ge(eff_done, 1 + n + 1)
                        nc.vector.tensor_tensor(sg, sg, w, ALU.add).then_inc(eff_done, 1)
                    for n in range(len(W_BLOCKS) // 4):
                        dve.wait_ge(wT_hi, 1 + n + 1)
                        nc.vector.tensor_tensor(w_dst(1, n), ps[:, 4 + n % 4, :], w_dst(0, n).bitcast(F32),
                                                ALU.subtract).then_inc(wT_lo, 1)
                    dve.wait_ge(w_in["rest"], 1 + 16 * 10)
                    nc.vector.tensor_scalar(sgb_sb[:], gub_sb[:], 1.702, None, ALU.mult)
                    nc.vector.tensor_scalar(upb_sb[:], gub_sb[:], 1.0, None, ALU.add)

                @block.tensor
                def _(pe):
                    pe.wait_ge(const_made, 1 + 9)
                    pe.wait_ge(w_in["tok"], 1 + 16)
                    with pe.Fori(0, B) as b:
                        for t in range(TB + 1):
                            if t < TB:
                                pe.wait_ge(gathered[t], 16 * (b + 1))
                                pe.wait_ge(rows_Tc, 1 + TB * b + max(t - 1, 0))
                                for k in range(KT):
                                    last = nc.tensor.transpose(ps[:, t % 2, k * P:(k + 1) * P],
                                                               rows[:, t, k * P:(k + 1) * P], ident[:])
                                last.then_inc(rows_T, 1)
                            if t >= 1:
                                pe.wait_ge(rows_Tc, 1 + TB * b + t)
                                pe.wait_ge(h_ready, 1 + TB * b + max(t - 2, 0))
                                for k in range(KT):
                                    last = nc.tensor.matmul(ps[:, 2 + (t - 1) % 2, 0:D],
                                                            rowsT[:, (t - 1) % 2, k * P:(k + 1) * P],
                                                            w1t_sb[:, k, :], start=(k == 0), stop=(k == KT - 1))
                                last.then_inc(emb_done, 1)
                    pe.wait_ge(eff_done, 1 + 2 * (HC + KC))
                    for n in range(len(W_BLOCKS) // 4):
                        if n >= 4:
                            pe.wait_ge(wT_lo, 1 + n - 3)
                        for i in range(4):
                            kind, r, c = W_BLOCKS[4 * n + i]
                            src = (sgn_w1 if kind == "w1" else sgn_w2)[:, r, c * P:(c + 1) * P]
                            last = nc.tensor.transpose(ps[:, 4 + n % 4, i * P:(i + 1) * P], src, ident[:])
                        last.then_inc(wT_ps, 1)

                @block.scalar
                def _(act):
                    with act.Fori(0, B) as b:
                        for t in range(TB):
                            act.wait_ge(rows_T, 1 + TB * b + t + 1)
                            act.wait_ge(emb_done, 1 + TB * b + max(t - 1, 0))
                            nc.scalar.activation(rowsT[:, t % 2, :], ps[:, t % 2, :], ACT.Copy).then_inc(rows_Tc, 1)
                    act.wait_ge(w_in["mlp"], 1 + 32)
                    nc.scalar.activation(sgn_w1[:], raw_w1[:], ACT.Sign).then_inc(sign_done, 1)
                    nc.scalar.activation(sgn_w2[:], raw_w2[:], ACT.Sign).then_inc(sign_done, 1)
                    for n in range(len(W_BLOCKS) // 4):
                        act.wait_ge(wT_ps, 1 + n + 1)
                        nc.scalar.activation(w_dst(0, n), ps[:, 4 + n % 4, :], ACT.Copy).then_inc(wT_hi, 1)

        st_done, mv_done, sd_done, rsd_done, xn_done, xn_T, xT_done, xlo_done = (
            sem(n) for n in ("st_done", "mv_done", "sd_done", "rsd_done", "xn_done", "xn_T", "xT_done", "xlo_done"))

        def ln_vector(dve, n, b, xn):
            for t in range(TB):
                nc.vector.bn_stats(stats[:, t, :], h[:, b * TB + t, :]).then_inc(st_done, 1)
            for t in range(TB):
                dve.wait_ge(st_done, 1 + TB * n + t + 1)
                plain(dve)
                nc.vector.bn_aggr(mv[:, t, :], stats[:, t, :]).then_inc(mv_done, 1)
            dve.wait_ge(sd_done, 1 + n + 1)
            nc.vector.reciprocal(rsd[:], sd[:]).then_inc(rsd_done, 1)
            dve.wait_ge(rsd_done, 1 + n + 1)
            dve.wait_ge(xn_T, 1 + 4 * n)
            for t in range(TB):
                nc.vector.tensor_scalar(xn[:, t, :], h[:, b * TB + t, :], mv[:, t, 0:1], rsd[:, t:t + 1],
                                        ALU.subtract, ALU.mult).then_inc(xn_done, 1)

        def ln_scalar(act, n, dst):
            act.wait_ge(mv_done, 1 + TB * (n + 1))
            nc.scalar.activation(sd[:], mv[:, :, 1], ACT.Sqrt, bias=eps_sb[:]).then_inc(sd_done, 1)
            for c in range(NC_):
                for k in range(KC):
                    act.wait_ge(xn_T, 1 + 4 * n + KC * c + k + 1)
                    plain(act)
                    nc.scalar.activation(dst(k, c), ps[:, KC * c + k, :], ACT.Copy).then_inc(xT_done, 1)

        def ln_low_parts(dve, n, hi, lo):
            for c in range(NC_):
                for k in range(KC):
                    dve.wait_ge(xT_done, 1 + 4 * n + KC * c + k + 1)
                    nc.vector.tensor_tensor(lo(k, c), ps[:, KC * c + k, :], hi(k, c).bitcast(F32),
                                            ALU.subtract).then_inc(xlo_done, 1)

        def ln_tensor(pe, n, xn):
            for c in range(NC_):
                pe.wait_ge(xn_done, 1 + TB * n + 4 * c + 4)
                for k in range(KC):
                    for i in range(4):
                        last = nc.tensor.transpose(ps[:, KC * c + k, i * P:(i + 1) * P],
                                                   xn[:, 4 * c + i, k * P:(k + 1) * P], ident[:])
                    last.then_inc(xn_T, 1)

        qk_ps, qk_hi, qk_r, qk_mid, qk_lo, v_ps, v_done, res_bias = (
            sem(n) for n in ("qk_ps", "qk_hi", "qk_r", "qk_mid", "qk_lo", "v_ps", "v_done", "res_bias"))
        qk_out = [sem("qk_out0"), sem("qk_out1")]
        NF = 2 * KC * NC_
        SCALE = HD ** -0.5

        def qkv_phase(layer, v_all):
            with ExitStack() as scope:
                xn = sb(f"xn{layer}", [P, TB, D], scope=scope)
                xT = sb(f"xT{layer}", [P, KC, T], scope=scope)
                splits = sb(f"splits{layer}", [P, 2, 3, 512], BF16, scope=scope)
                rest = sb(f"rest{layer}", [P, 2, 512], scope=scope)
                block = scope.enter_context(nc.Block())

                def factor(u):
                    return SCALE if u < NF // 2 else 1.0

                @block.vector
                def _(dve):
                    with dve.Fori(0, B) as b:
                        n = b + B * 2 * layer
                        m = b + B * layer
                        ln_vector(dve, n, b, xn)
                        for u in range(NF):
                            dve.wait_ge(qk_hi, 1 + NF * m + u + 1)
                            nc.vector.scalar_tensor_tensor(rest[:, u % 2, :], ps[:, 4 + u % 2, :], factor(u),
                                                           splits[:, u % 2, 0, :], ALU.mult,
                                                           ALU.subtract).then_inc(qk_r, 1)
                            dve.wait_ge(qk_r, 1 + NF * m + u + 1)
                            nc.vector.tensor_copy(splits[:, u % 2, 1, :], rest[:, u % 2, :]).then_inc(qk_mid, 1)
                            dve.wait_ge(qk_mid, 1 + NF * m + u + 1)
                            nc.vector.tensor_tensor(splits[:, u % 2, 2, :], rest[:, u % 2, :], splits[:, u % 2, 1, :],
                                                    ALU.subtract).then_inc(qk_lo, 1)

                @block.scalar
                def _(act):
                    with act.Fori(0, B) as b:
                        n = b + B * 2 * layer
                        m = b + B * layer
                        act.wait_ge(v_ps, 1 + TB * m)
                        ln_scalar(act, n, lambda k, c: xT[:, k, c * 512:(c + 1) * 512])
                        for u in range(NF):
                            act.wait_ge(qk_ps, 1 + NF * m + u + 1)
                            act.wait_ge(qk_out[u % 2], 1 + 16 * (NF // 2 * m + u // 2))
                            nc.scalar.activation(splits[:, u % 2, 0, :], ps[:, 4 + u % 2, :], ACT.Copy,
                                                 scale=factor(u)).then_inc(qk_hi, 1)
                        for t in range(TB):
                            act.wait_ge(v_ps, 1 + TB * m + t + 1)
                            plain(act)
                            nc.scalar.activation(v_all[:, t, bass.ds(b * D, D)], ps[:, 6 + t % 2, 0:D],
                                                 ACT.Copy).then_inc(v_done, 1)

                @block.tensor
                def _(pe):
                    if layer == 0:
                        pe.wait_ge(w_in["qkv0"], 1 + 16)
                    else:
                        pe.wait_ge(w_in["rest"], 1 + 16 * 10)
                    with pe.Fori(0, B) as b:
                        n = b + B * 2 * layer
                        m = b + B * layer
                        pe.wait_ge(xT_done, 1 + 4 * n)
                        ln_tensor(pe, n, xn)
                        pe.wait_ge(xT_done, 1 + 4 * (n + 1))
                        for u in range(NF):
                            qk, f, c = u // 4, u // 2 % 2, u % 2
                            pe.wait_ge(qk_r, 1 + NF * m + max(u - 1, 0))
                            for k in range(KC):
                                last = nc.tensor.matmul(ps[:, 4 + u % 2, :],
                                                        wqkv_sb[layer][:, k, qk * D + f * P:qk * D + (f + 1) * P],
                                                        xT[:, k, c * 512:(c + 1) * 512],
                                                        start=(k == 0), stop=(k == KC - 1))
                            last.then_inc(qk_ps, 1)
                        for t in range(TB):
                            pe.wait_ge(v_done, 1 + TB * m + max(t - 1, 0))
                            for k in range(KC):
                                last = nc.tensor.matmul(ps[:, 6 + t % 2, 0:D], xT[:, k, t * P:(t + 1) * P],
                                                        wqkv_sb[layer][:, k, 2 * D:3 * D],
                                                        start=(k == 0), stop=(k == KC - 1))
                            last.then_inc(v_ps, 1)

                @block.sync
                def _(sp):
                    with sp.Fori(0, B) as b:
                        m = b + B * layer
                        for u in range(NF):
                            qk, f, c = u // 4, u // 2 % 2, u % 2
                            sp.wait_ge(qk_lo, 1 + NF * m + u + 1)
                            dst = scratch[layer, qk, :, bass.ds(b * D + f * P, P), c * 512:(c + 1) * 512]
                            sp.dma_start(dst.rearrange("r p t -> p r t"),
                                         splits[:, u % 2, :, :]).then_inc(qk_out[u % 2], 16)
                    for x in range(2):
                        sp.wait_ge(qk_out[x], 1 + 16 * NF // 2 * B * (layer + 1))

                if layer == 0:
                    @block.gpsimd
                    def _(pool):
                        pool.wait_ge(w_in["rest"], 1 + 16 * 10)
                        with pool.Fori(0, B) as b:
                            pool.wait_ge(xn_done, 1 + TB * (b + 1))
                            for t in range(TB):
                                nc.gpsimd.tensor_tensor(h[:, b * TB + t, :], h[:, b * TB + t, :], bproj_sb[:],
                                                        ALU.add).then_inc(res_bias, 1)

        stack_in = [[sem(f"stack_in{n}{i}") for i in range(3)] for n in range(2)]
        vg_made, vg_ready = sem("vg_made"), sem("vg_ready")
        pv_done, oT_done, o_ps, dsum_done, rden_done, attn_done = (
            sem(n) for n in ("pv_done", "oT_done", "o_ps", "dsum_done", "rden_done", "attn_done"))

        def load_stack(sp, layer, it, i, stacks):
            for qk, parts in ((0, Q_PARTS), (1, K_PARTS)):
                for r, part in enumerate(parts):
                    src = scratch[layer, qk, part, bass.ds(it * CW, CW), :]
                    sp.dma_start(stacks[r * HD:(r + 1) * HD, i, qk, :, :],
                                 src.rearrange("(j d) t -> d j t", d=HD)).then_inc(stack_in[layer][i], 16)

        def make_vg(pool, layer, vg):
            nc.gpsimd.memset(vg[:], 0.0).then_inc(vg_made, 1)
            pool.wait_ge(vg_made, 1 + 2 * layer + 1)
            nc.gpsimd.memset(vg[:, :, :, :, HD:HD + 1], 1.0).then_inc(vg_made, 1)
            pool.wait_ge(vg_made, 1 + 2 * layer + 2)

        def copy_values(it, i, vg, v_all):
            nc.gpsimd.tensor_copy(vg[:, i, :, :, 0:HD], v_all[:, :, bass.ds(it * CW, CW)].rearrange(
                "p t (j d) -> p t j d", j=4)).then_inc(vg_ready, 1)

        def place(u, j):
            m, heads = UNITS[u]
            col = heads.index(j) * (STRIPS[m][2] if len(heads) == 4 else 512)
            return col // 512, col % 512

        def filled(buf, u):
            m, heads = UNITS[u]
            cols = STRIPS[m][2]
            return buf[:, 0:2, 0:cols] if len(heads) == 2 else buf[:, 0:4 * cols // 512, :]

        def pe_scores(first_bank, u, stack, rows_):
            m, heads = UNITS[u]
            qc, i, cols = STRIPS[m]
            diag = i >= 4 * qc
            q0 = qc * 512 + 512 - cols
            for j in heads:
                bank, col = place(u, j)
                last = nc.tensor.matmul(ps[:, first_bank + bank, col:col + cols],
                                        stack[0:rows_, 1, j, i * P:(i + 1) * P], stack[0:rows_, 0, j, q0:q0 + cols],
                                        start=True, stop=not diag)
                if diag:
                    last = nc.tensor.matmul(ps[:, first_bank + bank, col:col + P], identb[:], mask_kq[:],
                                            start=False, stop=True)
            return last

        def ready_strip(u):
            return [m for m in range(NS) if u == OF_STRIP[m][-1]]

        def pe_values(pe, n, m, bank, vg, prob):
            qc, i, cols = STRIPS[m]
            if m == 0:
                pe.wait_ge(vg_ready, 1 + n + 1)
            if i == 0:
                pe.wait_ge(oT_done, 1 + QC * n + qc)
            for j in range(4):
                u = [u for u in OF_STRIP[m] if j in UNITS[u][1]][0]
                half, col = place(u, j)
                last = nc.tensor.matmul(ps[32 * j:32 * j + 32, bank, 512 - cols:512], vg[:, i, j, :],
                                        prob(u)[:, half, col:col + cols], start=(i == 0), stop=(m == LAST[qc]))
            last.then_inc(pv_done, 1)

        def act_sums(act, n, qc, bank, oT):
            act.wait_ge(pv_done, 1 + NS * n + LAST[qc] + 1)
            act.wait_ge(o_ps, 1 + QC * n + qc)
            nc.scalar.activation(oT[:], ps[:, bank, :], ACT.Copy).then_inc(oT_done, 1)

        def pe_token_major(pe, n, qc, bank, oT):
            pe.wait_ge(oT_done, 1 + QC * n + qc + 1)
            pe.wait_ge(attn_done, 1 + QC * n + qc)
            for i in range(4):
                last = nc.tensor.transpose(ps[:, bank, i * P:(i + 1) * P], oT[:, i * P:(i + 1) * P], ident[:])
            last.then_inc(o_ps, 1)

        def dve_norm(dve, layer, n, it, qc, bank, dsum, rden, attn):
            o = ps[:, bank, :].rearrange("p (i j c) -> p i j c", i=4, j=4)
            dve.wait_ge(o_ps, 1 + QC * n + qc + 1)
            nc.vector.tensor_scalar(dsum[:], o[:, :, :, HD], 1e-9 if layer == 0 else 0.0, None,
                                    ALU.add).then_inc(dsum_done, 1)
            dve.wait_ge(dsum_done, 1 + QC * n + qc + 1)
            nc.vector.reciprocal(rden[:], dsum[:]).then_inc(rden_done, 1)
            dve.wait_ge(rden_done, 1 + QC * n + qc + 1)
            nc.vector.tensor_tensor(
                attn[:, qc * 4:qc * 4 + 4, bass.ds(it * CW, CW)].rearrange("p i (j d) -> p i j d", j=4), o[:, :, :, 0:HD],
                rden[:].rearrange("p i (j o) -> p i j o", o=1).to_broadcast((P, 4, 4, HD)),
                ALU.mult).then_inc(attn_done, 1)

        def turn(step, lag, after):
            return [qc for qc in range(QC) if step == OF_STRIP[LAST[qc]][-1] + lag + after]

        def reach(n):
            return 1 + (max(n, 0) if isinstance(n, int) else n)

        def values_used(n, u, size):
            if u >= size:
                return NS * n + UNITS[u - size][0] + 1
            return 0 if isinstance(n, int) and n == 0 else NS * (n - 1) + UNITS[u - size + NU][0] + 1

        def over_groups(eng, per, tail, step):
            def rest(it, rnd, i, last):
                for s in range(tail, NU):
                    step(it, rnd, i, s)
                for s in range(tail):
                    if not last:
                        step(it + 1, rnd + (i + 1) // per, (i + 1) % per, s)
                    step(it, rnd, i, NU + s)
            for s in range(tail):
                step(0, 0, 0, s)
            rounds = (NG - 2) // per
            with eng.Fori(0, rounds) as rnd:
                for i in range(per):
                    rest(per * rnd + i, rnd, i, False)
            for it in range(per * rounds, NG):
                rest(it, it // per, it % per, it == NG - 1)

        sc_ps, cap_done, e_done, ln_done, mx_done = (
            sem(n) for n in ("sc_ps", "cap_done", "e_done", "ln_done", "mx_done"))
        sq_done = {e: sem(f"sq_{e}") for e in ("pool", "dve", "act")}
        SQ = ["pool" for u in range(NU)]

        def count(flags, u=NU - 1):
            return sum(1 for x in flags[:u + 1] if x)

        def softplus_attention(v_all, stacks, attn):
            LAG, NP = 7, 10
            TAIL = NP + 1
            with ExitStack() as scope:
                probs = sb("soft_probs", [P, NP, 2, 512], scope=scope)
                soft = sb("soft", [P, 3, 2, 512], scope=scope)
                vg = sb("vg0", [P, 3, TB, 4, 32], scope=scope)
                oT = sb("oT0", [P, 512], scope=scope)
                dsum = sb("dsum0", [P, 4, 4], scope=scope)
                rden = sb("rden0", [P, 4, 4], scope=scope)
                block = scope.enter_context(nc.Block())

                def ring(i, u):
                    return (NU * i + u) % 3

                def sc(i, u):
                    return filled(ps[:, 2 * ring(i, u):2 * ring(i, u) + 2, :], u)

                @block.sync
                def _(sp):
                    for it in range(NG):
                        if it >= 3:
                            sp.wait_ge(sc_ps, 1 + NU * (it - 2))
                        load_stack(sp, 0, it, it % 3, stacks)

                @block.tensor
                def _(pe):
                    def step(it, rnd, i, s):
                        if s == 0:
                            pe.wait_ge(stack_in[0][i], 1 + 16 * 12 * (rnd + 1))
                        if s < NU:
                            pe.wait_ge(mx_done, reach(NU * it + s - 2))
                            pe_scores(2 * ring(i, s), s, stacks[:, i], KR).then_inc(sc_ps, 1)
                        v = s - LAG
                        for m in ready_strip(v):
                            for e in ("pool", "dve", "act"):
                                if e in [SQ[u] for u in OF_STRIP[m]]:
                                    own = [x == e for x in SQ]
                                    pe.wait_ge(sq_done[e], 1 + count(own) * it + count(own, v))
                            pe_values(pe, it, m, 6, vg[:, i], lambda u: probs[:, u % NP])
                        for qc in turn(s, LAG, 2):
                            pe_token_major(pe, it, qc, 7, oT)
                    over_groups(pe, 3, TAIL, step)

                @block.scalar
                def _(act):
                    act.preload_act_table_set("natural_log_exp_and_others")

                    def step(it, rnd, i, s):
                        if s < NU:
                            x = filled(soft[:, ring(i, s)], s)
                            act.wait_ge(cap_done, 1 + NU * it + s + 1)
                            nc.scalar.activation(x, x, ACT.Exp).then_inc(e_done, 1)
                            act.wait_ge(e_done, 1 + NU * it + s + 1)
                            nc.scalar.activation(x, x, ACT.Ln, bias=1.0).then_inc(ln_done, 1)
                        v = s - 4
                        if 0 <= v < NU and SQ[v] == "act":
                            pr = filled(probs[:, v % NP], v)
                            act.wait_ge(mx_done, 1 + NU * it + v + 1)
                            nc.scalar.activation(pr, pr, ACT.Square).then_inc(sq_done["act"], 1)
                        for qc in turn(s, LAG, 0):
                            act_sums(act, it, qc, 6, oT)
                    over_groups(act, 3, TAIL, step)

                @block.vector
                def _(dve):
                    def step(it, rnd, i, s):
                        if s < NU:
                            dve.wait_ge(sc_ps, 1 + NU * it + s + 1)
                            nc.vector.tensor_scalar(filled(soft[:, ring(i, s)], s), sc(i, s), CAP, None,
                                                    ALU.min).then_inc(cap_done, 1)
                        v = s - 1
                        if 0 <= v < NU:
                            pr = filled(probs[:, v % NP], v)
                            x = filled(soft[:, ring(i, v)], v)
                            dve.wait_ge(ln_done, 1 + NU * it + v + 1)
                            dve.wait_ge(pv_done, 1 + values_used(it, v, NP))
                            nc.vector.tensor_tensor(pr, sc(i, v), x, ALU.max).then_inc(mx_done, 1)
                            if SQ[v] == "dve":
                                dve.wait_ge(mx_done, 1 + NU * it + v + 1)
                                nc.vector.tensor_tensor(pr, pr, pr, ALU.mult).then_inc(sq_done["dve"], 1)
                        for qc in turn(s, LAG, 3):
                            dve_norm(dve, 0, it, it, qc, 7, dsum, rden, attn)
                    over_groups(dve, 3, TAIL, step)

                @block.gpsimd
                def _(pool):
                    make_vg(pool, 0, vg)
                    for i in range(2):
                        copy_values(i, i, vg, v_all)

                    def step(it, rnd, i, s):
                        if s < NU and SQ[s] == "pool":
                            pr = filled(probs[:, s % NP], s)
                            pool.wait_ge(mx_done, 1 + NU * it + s + 1)
                            nc.gpsimd.tensor_tensor(pr, pr, pr, ALU.mult).then_inc(sq_done["pool"], 1)
                        if s == TAIL and not (isinstance(it, int) and it >= NG - 2):
                            pool.wait_ge(pv_done, 1 + NS * it)
                            copy_values(it + 2, (i + 2) % 3, vg, v_all)
                    over_groups(pool, 3, TAIL, step)

        at_ps, at_done, proj_ps, proj_done = sem("at_ps"), sem("at_done"), sem("proj_ps"), sem("proj_done")

        def proj_phase(layer, attn):
            with ExitStack() as scope:
                attnT = sb(f"attnT{layer}", [P, 2, KC, 512], scope=scope)
                block = scope.enter_context(nc.Block())
                NQ = NT // 4

                @block.tensor
                def _(pe):
                    for n in range(NQ + 1):
                        if n < NQ:
                            for k in range(KC):
                                pe.wait_ge(at_done, 1 + KC * (NQ * layer + max(n - 1, 0)))
                                for i in range(4):
                                    b, t = n * 4 // TB, n * 4 % TB + i
                                    src = attn[:, t, b * D + k * P:b * D + (k + 1) * P]
                                    last = nc.tensor.transpose(ps[:, KC * (n % 2) + k, i * P:(i + 1) * P], src, ident[:])
                                last.then_inc(at_ps, 1)
                        if n >= 1:
                            pe.wait_ge(at_done, 1 + KC * (NQ * layer + n))
                            for i in range(4):
                                t = (n - 1) * 4 + i
                                pe.wait_ge(proj_done, 1 + NT * layer + max(t - 3, 0))
                                for k in range(KC):
                                    last = nc.tensor.matmul(ps[:, 4 + t % 4, 0:D],
                                                            attnT[:, (n - 1) % 2, k, i * P:(i + 1) * P],
                                                            wproj_sb[layer][:, k, :], start=(k == 0), stop=(k == KC - 1))
                                last.then_inc(proj_ps, 1)

                @block.scalar
                def _(act):
                    for n in range(NQ):
                        for k in range(KC):
                            act.wait_ge(at_ps, 1 + KC * (NQ * layer + n) + k + 1)
                            act.wait_ge(proj_ps, 1 + NT * layer + 4 * max(n - 1, 0))
                            nc.scalar.activation(attnT[:, n % 2, k, :], ps[:, KC * (n % 2) + k, :],
                                                 ACT.Copy).then_inc(at_done, 1)

                @block.vector
                def _(dve):
                    for t in range(NT):
                        dve.wait_ge(proj_ps, 1 + NT * layer + t + 1)
                        nc.vector.tensor_tensor(h[:, t, :], h[:, t, :], ps[:, 4 + t % 4, 0:D],
                                                ALU.add).then_inc(proj_done, 1)

        rw_split, r_ps, r_step, top_done, cw_exp, cw_done, cwT_ps, cwT_done, db_ps, db_done = (
            sem(n) for n in ("rw_split", "r_ps", "r_step", "top_done", "cw_exp", "cw_done", "cwT_ps", "cwT_done",
                             "db_ps", "db_done"))
        gu_ps, sig_done, up_done, g_done, ga_done, a_done, ah_done, al_done, dn_ps, dn_done = (
            sem(n) for n in ("gu_ps", "sig_done", "up_done", "g_done", "ga_done", "a_done", "ah_done", "al_done",
                             "dn_ps", "dn_done"))
        rT_ps, rT_done = sem("rT_ps"), sem("rT_done")
        wh_done, wl_done = sem("wh_done"), sem("wl_done")
        ew_in = [sem("ew_in0"), sem("ew_in1")]
        NCH = NT // 4
        GUC = KC * 2 * KC * P
        WC = GUC + 2 * D

        def products(dst, lhs, rhs, n_k, stop=True):
            terms = [(k, a, b) for k in range(n_k) for a, b in ((0, 0), (1, 0), (0, 1))]
            for n, (k, a, b) in enumerate(terms):
                last = nc.tensor.matmul(dst, lhs(a, k), rhs(b, k), start=(n == 0), stop=(n == len(terms) - 1))
            return last

        def over_experts(eng, hidden, down, split):
            def expert(e, rnd, par, last):
                for c in range(NCH):
                    if c < NCH - 1:
                        hidden(e, par, c + 1)
                    elif not last:
                        hidden(e + 1, 1 - par, 0)
                    if c == 1 and not last:
                        split(e + 1, rnd + par, 1 - par)
                    down(e, par, c)
            with eng.Fori(0, NE // 2 - 1) as rnd:
                for par in range(2):
                    expert(2 * rnd + par, rnd, par, False)
            expert(NE - 2, NE // 2 - 1, 0, False)
            expert(NE - 1, NE // 2 - 1, 1, True)

        def nothing(*_):
            pass

        def experts_phase():
            with ExitStack() as scope:
                xn = sb("ffn_xn", [P, TB, D], scope=scope)
                x_hl = [sb(f"ffn_x{n}", [P, KC, NT * P], F32R, scope=scope) for n in range(2)]
                rw_hl = [sb(f"rw{n}", [P, KC, NE], F32R, scope=scope) for n in range(2)]
                raw = sb("expert_raw", [P, 2, WC], scope=scope)
                w_hl = [sb(f"expert_w{n}", [P, 2, WC], F32R, scope=scope) for n in range(2)]
                a_hl = [sb(f"expert_a{n}", [P, 2, 2, 512], F32R, scope=scope) for n in range(2)]
                a_sb = sb("expert_a", [P, 2, 512], scope=scope)
                sig = sb("sig", [P, 2, 512], scope=scope)
                upc = sb("upc", [P, 2, 512], scope=scope)
                gc = sb("gc", [P, 2, 512], scope=scope)
                rs = sb("rs", [P, NT, NE], scope=scope)
                top_v = sb("top_v", [P, NT, NE], scope=scope)
                top_i = sb("top_i", [P, NT, NE], U32, scope=scope)
                top_f = sb("top_f", [P, NT, NE], scope=scope)
                gap = sb("gap", [P, 4, NT], scope=scope)
                pick = sb("pick", [P, NT, NE], scope=scope)
                cw = sb("cw", [P, NT, NE], scope=scope)
                cwT = sb("cwT", [NE, NCH, 512], scope=scope)
                rT = sb("rT", [NE, NCH, 512], scope=scope)
                block = scope.enter_context(nc.Block())
                guw = [w[:, :, 0:GUC].rearrange("p s (k f) -> p s k f", k=KC) for w in w_hl]
                dnw = [w[:, :, GUC:WC].rearrange("p s (k d) -> p s k d", k=2) for w in w_hl]

                def rows_bc(ap):
                    return ap.rearrange("p (t o) -> p t o", o=1).to_broadcast((P, NT, NE))

                @block.sync
                def _(sp):
                    for e in range(2):
                        sp.dma_start(raw[:, e, :], expert_w[e, :, :]).then_inc(ew_in[e], 16)
                    with sp.Fori(0, NE // 2 - 1) as rnd:
                        for par in range(2):
                            sp.wait_ge(wl_done, 1 + 2 * rnd + par + 1)
                            sp.dma_start(raw[:, par, :], expert_w[2 * rnd + par + 2, :, :]).then_inc(ew_in[par], 16)

                @block.gpsimd
                def _(pool):
                    def split(e, rnd, par):
                        pool.wait_ge(wh_done, 1 + e + 1)
                        nc.gpsimd.tensor_tensor(w_hl[1][:, par, :], raw[:, par, :],
                                                w_hl[0][:, par, :].bitcast(F32), ALU.subtract).then_inc(wl_done, 1)

                    def hidden(e, par, c):
                        for hc in range(2):
                            pool.wait_ge(ah_done, 1 + 2 * (NCH * e + c) + hc + 1)
                            nc.gpsimd.tensor_tensor(a_hl[1][:, c % 2, hc, :], a_sb[:, hc, :],
                                                    a_hl[0][:, c % 2, hc, :].bitcast(F32),
                                                    ALU.subtract).then_inc(al_done, 1)
                    split(0, 0, 0)
                    hidden(0, 0, 0)
                    over_experts(pool, hidden, nothing, split)

                @block.vector
                def _(dve):
                    with dve.Fori(0, B) as b:
                        ln_vector(dve, b + B, b, xn)
                        ln_low_parts(dve, b + B, lambda k, c: x_hl[0][:, k, bass.ds(b * T + c * 512, 512)],
                                     lambda k, c: x_hl[1][:, k, bass.ds(b * T + c * 512, 512)])
                    dve.wait_ge(rw_split, 1 + 1)
                    nc.vector.tensor_tensor(rw_hl[1][:], rw_sb[:], rw_hl[0][:].bitcast(F32),
                                            ALU.subtract).then_inc(rw_split, 1)

                    def step(ins, k):
                        ins.then_inc(r_step, 1)
                        dve.wait_ge(r_step, 1 + k)
                    dve.wait_ge(r_ps, 1 + NCH)
                    step(nc.vector.tensor_tensor(
                        rs[:], ps[:, 7, 0:NT * NE].rearrange("p (t e) -> p t e", e=NE),
                        rb_sb[:].rearrange("p (o e) -> p o e", o=1).to_broadcast((P, NT, NE)), ALU.add), 1)
                    for t in range(NT):
                        nc.vector.max(top_v[:, t, :], rs[:, t, :]).then_inc(r_step, 1)
                    dve.wait_ge(r_step, 1 + 1 + NT)
                    nc.vector.tensor_tensor(gap[:, 0, :], top_v[:, :, 1], top_v[:, :, 0],
                                            ALU.subtract).then_inc(top_done, 1)
                    for t in range(NT):
                        nc.vector.max_index(top_i[:, t, :], top_v[:, t, :], rs[:, t, :]).then_inc(r_step, 1)
                    dve.wait_ge(r_step, 1 + 1 + 2 * NT)
                    k = 1 + 2 * NT
                    step(nc.vector.tensor_copy(top_f[:], top_i[:]), k + 1)
                    dve.wait_ge(cw_exp, 1 + 1)
                    step(nc.vector.tensor_scalar(gap[:, 2, :], gap[:, 1, :], 1.0, None, ALU.add), k + 2)
                    step(nc.vector.reciprocal(gap[:, 2, :], gap[:, 2, :]), k + 3)
                    step(nc.vector.tensor_tensor(gap[:, 3, :], gap[:, 1, :], gap[:, 2, :], ALU.mult), k + 4)
                    numbers = expert_no[:].rearrange("p (o e) -> p o e", o=1).to_broadcast((P, NT, NE))
                    step(nc.vector.tensor_tensor(cw[:], numbers, rows_bc(top_f[:, :, 0]), ALU.is_equal), k + 5)
                    step(nc.vector.tensor_tensor(pick[:], numbers, rows_bc(top_f[:, :, 1]), ALU.is_equal), k + 6)
                    step(nc.vector.tensor_tensor(cw[:], cw[:], rows_bc(gap[:, 2, :]), ALU.mult), k + 7)
                    step(nc.vector.tensor_tensor(pick[:], pick[:], rows_bc(gap[:, 3, :]), ALU.mult), k + 8)
                    nc.vector.tensor_tensor(cw[:], cw[:], pick[:], ALU.add).then_inc(cw_done, 1)
                    def hidden(e, par, c):
                        for hc in range(2):
                            w = 2 * (NCH * e + c) + hc
                            dve.wait_ge(gu_ps, 1 + w + 1)
                            nc.vector.tensor_scalar(upc[:, hc, :], ps[:, 2 * hc + 1, :], upb_sb[:, e, 2 + hc:3 + hc],
                                                    -6.0, ALU.add, ALU.max).then_inc(up_done, 1)
                            dve.wait_ge(sig_done, 1 + w + 1)
                            nc.vector.tensor_scalar(gc[:, hc, :], ps[:, 2 * hc, :], gub_sb[:, e, hc:hc + 1],
                                                    -7.0, ALU.add, ALU.max).then_inc(g_done, 1)
                            dve.wait_ge(g_done, 1 + w + 1)
                            nc.vector.scalar_tensor_tensor(gc[:, hc, :], gc[:, hc, :], 7.0, sig[:, hc, :],
                                                           ALU.min, ALU.mult).then_inc(ga_done, 1)
                            dve.wait_ge(ga_done, 1 + w + 1)
                            dve.wait_ge(up_done, 1 + w + 1)
                            dve.wait_ge(al_done, reach(w - 1))
                            nc.vector.scalar_tensor_tensor(a_sb[:, hc, :], upc[:, hc, :], 8.0, gc[:, hc, :],
                                                           ALU.min, ALU.mult).then_inc(a_done, 1)

                    def down(e, par, c):
                        for t in range(4):
                            tile = 4 * c + t
                            dve.wait_ge(dn_ps, 1 + 4 * (NCH * e + c) + t + 1)
                            nc.vector.scalar_tensor_tensor(h[:, tile, :], ps[:, 4 + t, 0:D],
                                                           cw[:, tile, e:e + 1] if isinstance(e, int) else
                                                           cw[:, tile, bass.ds(e, 1)],
                                                           h[:, tile, :], ALU.mult, ALU.add).then_inc(dn_done, 1)
                    hidden(0, 0, 0)
                    for w in range(NT // 2):
                        dve.wait_ge(db_ps, 1 + w + 1)
                        nc.vector.tensor_tensor(h[:, 2 * w:2 * w + 2, :], h[:, 2 * w:2 * w + 2, :],
                                                ps[:, 4 + w % 4, :].rearrange("p (t d) -> p t d", t=2),
                                                ALU.add).then_inc(db_done, 1)
                    over_experts(dve, hidden, down, nothing)

                @block.scalar
                def _(act):
                    with act.Fori(0, B) as b:
                        ln_scalar(act, b + B, lambda k, c: x_hl[0][:, k, bass.ds(b * T + c * 512, 512)])
                    nc.scalar.activation(rw_hl[0][:], rw_sb[:], ACT.Copy).then_inc(rw_split, 1)
                    def split(e, rnd, par):
                        act.wait_ge(ew_in[par], 1 + 16 * (rnd + 1))
                        if not isinstance(e, int) or e > 0:
                            act.wait_ge(dn_ps, 1 + 4 * NCH * (e - 1))
                        nc.scalar.activation(w_hl[0][:, par, :], raw[:, par, :], ACT.Copy).then_inc(wh_done, 1)

                    def hidden(e, par, c):
                        for hc in range(2):
                            w = 2 * (NCH * e + c) + hc
                            act.wait_ge(gu_ps, 1 + w + 1)
                            act.wait_ge(ga_done, reach(w - 1))
                            plain(act)
                            nc.scalar.activation(sig[:, hc, :], ps[:, 2 * hc, :], ACT.Sigmoid,
                                                 bias=sgb_sb[:, e, hc:hc + 1], scale=1.702).then_inc(sig_done, 1)
                            act.wait_ge(a_done, 1 + w + 1)
                            act.wait_ge(dn_ps, reach(4 * (NCH * e + c - 1)))
                            nc.scalar.activation(a_hl[0][:, c % 2, hc, :], a_sb[:, hc, :],
                                                 ACT.Copy).then_inc(ah_done, 1)
                    split(0, 0, 0)
                    for n in range(NCH):
                        act.wait_ge(rT_ps, 1 + n + 1)
                        nc.scalar.activation(rT[:, n, :], ps[0:NE, 4 + n % 3, :], ACT.Copy).then_inc(rT_done, 1)
                    act.wait_ge(top_done, 1 + 1)
                    nc.scalar.activation(gap[:, 1, :], gap[:, 0, :], ACT.Exp).then_inc(cw_exp, 1)
                    for n in range(NCH):
                        act.wait_ge(cwT_ps, 1 + n + 1)
                        nc.scalar.activation(cwT[:, n, :], ps[0:NE, 4 + n, :], ACT.Copy).then_inc(cwT_done, 1)
                    hidden(0, 0, 0)
                    over_experts(act, hidden, nothing, split)

                @block.tensor
                def _(pe):
                    with pe.Fori(0, B) as b:
                        pe.wait_ge(xlo_done, 1 + 4 * b)
                        ln_tensor(pe, b + B, xn)
                    pe.wait_ge(xlo_done, 1 + 8)
                    pe.wait_ge(rw_split, 1 + 2)
                    for n in range(NCH + 1):
                        if n < NCH:
                            pe.wait_ge(rT_done, 1 + max(n - 2, 0))
                            products(ps[0:NE, 4 + n % 3, :], lambda x, k: rw_hl[x][:, k, :],
                                     lambda x, k: x_hl[x][:, k, n * 512:(n + 1) * 512], KC).then_inc(rT_ps, 1)
                        if n >= 1:
                            pe.wait_ge(rT_done, 1 + n)
                            for t in range(4 * n - 4, 4 * n):
                                last = nc.tensor.transpose(ps[:, 7, t * NE:(t + 1) * NE],
                                                           rT[:, n - 1, t % 4 * P:(t % 4 + 1) * P], ident[0:NE, 0:NE])
                            last.then_inc(r_ps, 1)

                    def hidden(e, par, c):
                        if c == 0:
                            pe.wait_ge(wh_done, 1 + e + 1)
                            pe.wait_ge(wl_done, 1 + e + 1)
                        for hc in range(2):
                            pe.wait_ge(g_done, reach(2 * (NCH * e + c) + hc - 1))
                            for gu in range(2):
                                f = gu * 2 * P + hc * P
                                last = products(ps[:, 2 * hc + gu, :], lambda x, k: guw[x][:, par, k, f:f + P],
                                                lambda x, k: x_hl[x][:, k, c * 512:(c + 1) * 512], KC)
                            last.then_inc(gu_ps, 1)

                    def down(e, par, c):
                        pe.wait_ge(al_done, 1 + 2 * (NCH * e + c) + 2)
                        for t in range(4):
                            pe.wait_ge(dn_done, 1 + 4 * (NCH * e + c) + t + 1)
                            products(ps[:, 4 + t, 0:D], lambda x, k: a_hl[x][:, c % 2, k, t * P:(t + 1) * P],
                                     lambda x, k: dnw[x][:, par, k, :], 2).then_inc(dn_ps, 1)
                    hidden(0, 0, 0)
                    pe.wait_ge(cw_done, 1 + 1)
                    for n in range(NCH):
                        for t in range(4):
                            last = nc.tensor.transpose(ps[0:NE, 4 + n, t * P:(t + 1) * P], cw[:, 4 * n + t, :], ident[:])
                        last.then_inc(cwT_ps, 1)
                    for w in range(NT // 2):
                        pe.wait_ge(cwT_done, 1 + (NCH if w < 4 else w // 2 + 1))
                        pe.wait_ge(db_done, 1 + max(w - 3, 0))
                        for t in range(2):
                            last = nc.tensor.matmul(ps[:, 4 + w % 4, t * D:(t + 1) * D],
                                                    cwT[:, w // 2, (2 * (w % 2) + t) * P:(2 * (w % 2) + t + 1) * P],
                                                    dnb_sb[:], start=True, stop=True)
                        last.then_inc(db_ps, 1)
                    pe.wait_ge(db_done, 1 + NT // 2)
                    pe.sem_inc(dn_done, 4)
                    over_experts(pe, hidden, down, nothing)

        MAXES = [(j, t, k0, min(512, (t + 1) * P - k0)) for n in range(TB // 2) for j in range(4)
                 for t in (n, TB - 1 - n) for k0 in range(0, (t + 1) * P, 512)]
        NM = len(MAXES)
        M_END = 14

        def maxes_after(u):
            return range(NM * min(u, M_END) // M_END, NM * min(u + 1, M_END) // M_END)

        am_ps, am_done, am_all, mT_ps, m_step, m_out = (
            sem(n) for n in ("am_ps", "am_done", "am_all", "mT_ps", "m_step", "m_out"))
        sb_ps, p_done, ones_done = sem("sb_ps"), sem("p_done"), sem("ones_done")

        def softmax_attention(v_all, stacks, attn):
            LAG, NP = 8, 10
            MAX_BANKS = (4, 5, 7)
            TAIL = NP + 1
            with ExitStack() as scope:
                probs = sb("probs", [P, NP, 2, 512], scope=scope)
                vg = sb("vg1", [P, 3, TB, 4, 32], scope=scope)
                oT = sb("oT1", [P, 512], scope=scope)
                dsum = sb("dsum1", [P, 4, 4], scope=scope)
                rden = sb("rden1", [P, 4, 4], scope=scope)
                mx1 = sb("mx1", [P, 4, TB], scope=scope)
                mx2 = sb("mx2", [P, 4, TB], scope=scope)
                m_rest = sb("m_rest", [4 * TB, P], scope=scope)
                m_parts = sb("m_parts", [4 * TB, 3, P], BF16, scope=scope)
                block = scope.enter_context(nc.Block())

                def last(it):
                    return isinstance(it, int) and it == NG - 1

                @block.sync
                def _(sp):
                    def send_maxima(n, i):
                        sp.wait_ge(m_step, 1 + 4 * (n + 1))
                        for x in range(3):
                            sp.dma_start(stacks[KR + x:KR + x + 1, i, 0, :, :].rearrange("o j (t q) -> o (j t) q", q=P),
                                         m_parts[:, x, :]).then_inc(m_out, 16)
                    sp.wait_ge(ones_done, 1 + 1)
                    for i in range(3):
                        load_stack(sp, 1, i, i, stacks)
                    send_maxima(0, 0)
                    for it in range(NG - 1):
                        send_maxima(it + 1, (it + 1) % 3)
                        if it + 3 < NG:
                            sp.wait_ge(sb_ps, 1 + NU * (it + 1))
                            load_stack(sp, 1, it + 3, it % 3, stacks)

                @block.tensor
                def _(pe):
                    def maxes(n, i, units):
                        for w in units:
                            j, t, k0, keys = MAXES[w]
                            diag = k0 + keys == (t + 1) * P
                            if w == 0 and not (isinstance(n, int) and n == 0):
                                pe.wait_ge(m_step, 1 + 4 * (n - 1) + 2)
                            pe.wait_ge(am_done, reach(NM * n + w - 2))
                            bank = MAX_BANKS[w % 3]
                            scores = nc.tensor.matmul(ps[:, bank, 0:keys], stacks[0:KR, i, 0, j, t * P:(t + 1) * P],
                                                      stacks[0:KR, i, 1, j, k0:k0 + keys], start=True, stop=not diag)
                            if diag:
                                scores = nc.tensor.matmul(ps[:, bank, keys - P:keys], identb[:], mask_qk[:],
                                                          start=False, stop=True)
                            scores.then_inc(am_ps, 1)

                    def max_rows(n):
                        pe.wait_ge(am_all, 1 + n + 1)
                        nc.tensor.transpose(ps[0:4 * TB, MAX_BANKS[0], 0:P], mx1[:].rearrange("p j t -> p (j t)"),
                                            ident[:]).then_inc(mT_ps, 1)
                    pe.wait_ge(stack_in[1][0], 1 + 16 * 12)
                    maxes(0, 0, range(NM))
                    max_rows(0)

                    def step(it, rnd, i, s):
                        n = NG + it
                        if s == 0:
                            pe.wait_ge(m_out, 1 + 48 * (it + 1))
                        for qc in turn(s, LAG, 1):
                            pe_token_major(pe, n, qc, 6, oT)
                        if s < NU:
                            pe.wait_ge(p_done, reach(NU * it + s - 1))
                            pe_scores(2 * (s % 2), s, stacks[:, i], KR + 3).then_inc(sb_ps, 1)
                            if not last(it):
                                if s == 0:
                                    pe.wait_ge(stack_in[1][(i + 1) % 3], 1 + 16 * 12 * (rnd + (i + 1) // 3 + 1))
                                maxes(it + 1, (i + 1) % 3, maxes_after(s))
                        v = s - LAG
                        for m in ready_strip(v):
                            pe.wait_ge(p_done, 1 + NU * it + v + 1)
                            if STRIPS[m][1] == 0:
                                pe.wait_ge(attn_done, 1 + QC * n + STRIPS[m][0])
                            pe_values(pe, n, m, 6, vg[:, i], lambda u: probs[:, u % NP])
                        if s == M_END + 1 and not last(it):
                            max_rows(it + 1)
                    over_groups(pe, 3, TAIL, step)

                @block.scalar
                def _(act):
                    def step(it, rnd, i, s):
                        n = NG + it
                        if s < NU:
                            act.wait_ge(sb_ps, 1 + NU * it + s + 1)
                            act.wait_ge(pv_done, 1 + values_used(n, s, NP))
                            nc.scalar.activation(filled(probs[:, s % NP], s),
                                                 filled(ps[:, 2 * (s % 2):2 * (s % 2) + 2, :], s),
                                                 ACT.Exp).then_inc(p_done, 1)
                        for qc in turn(s, LAG, 0):
                            act_sums(act, n, qc, 6, oT)
                    over_groups(act, 1, TAIL, step)

                @block.vector
                def _(dve):
                    def maxes(n, units):
                        for w in units:
                            j, t, k0, keys = MAXES[w]
                            dve.wait_ge(am_ps, 1 + NM * n + w + 1)
                            if w == 0:
                                dve.wait_ge(mT_ps, 1 + n)
                            dst = (mx2 if k0 else mx1)[:, j, t:t + 1]
                            nc.vector.reduce_max(dst, ps[:, MAX_BANKS[w % 3], 0:keys], AX.X).then_inc(am_done, 1)

                    def join(n):
                        dve.wait_ge(am_done, 1 + NM * (n + 1))
                        nc.vector.tensor_tensor(mx1[:, :, 4:TB], mx1[:, :, 4:TB], mx2[:, :, 4:TB],
                                                ALU.max).then_inc(am_all, 1)

                    def parts(n):
                        dve.wait_ge(mT_ps, 1 + n + 1)
                        dve.wait_ge(m_out, 1 + 48 * n)
                        src = ps[0:4 * TB, MAX_BANKS[0], 0:P]
                        nc.vector.tensor_scalar(m_parts[:, 0, :], src, -1.0, None, ALU.mult).then_inc(m_step, 1)
                        dve.wait_ge(m_step, 1 + 4 * n + 1)
                        nc.vector.scalar_tensor_tensor(m_rest[:], src, -1.0, m_parts[:, 0, :], ALU.mult,
                                                       ALU.subtract).then_inc(m_step, 1)
                        dve.wait_ge(m_step, 1 + 4 * n + 2)
                        nc.vector.tensor_copy(m_parts[:, 1, :], m_rest[:]).then_inc(m_step, 1)
                        dve.wait_ge(m_step, 1 + 4 * n + 3)
                        nc.vector.tensor_tensor(m_parts[:, 2, :], m_rest[:], m_parts[:, 1, :],
                                                ALU.subtract).then_inc(m_step, 1)
                    maxes(0, range(NM))
                    join(0)
                    parts(0)

                    def step(it, rnd, i, s):
                        n = NG + it
                        if s < NU and not last(it):
                            maxes(it + 1, maxes_after(s))
                            if s == M_END:
                                join(it + 1)
                            if s == M_END + 1:
                                parts(it + 1)
                        for qc in turn(s, LAG, 1):
                            dve_norm(dve, 1, n, it, qc, 6, dsum, rden, attn)
                    over_groups(dve, 1, TAIL, step)

                @block.gpsimd
                def _(pool):
                    nc.gpsimd.memset(stacks[KR:KR + 3, :, 1, :, :], 1.0).then_inc(ones_done, 1)
                    pool.wait_ge(ones_done, 1 + 1)
                    make_vg(pool, 1, vg)
                    for it in range(NG):
                        pool.wait_ge(pv_done, 1 + NS * (NG + max(it - 2, 0)))
                        copy_values(it, it % 3, vg, v_all)

        hid_ps, hid_f, hid_hi, hid_lo, mo_ps, mo_done, b2_done, stored = (
            sem(n) for n in ("hid_ps", "hid_f", "hid_hi", "hid_lo", "mo_ps", "mo_done", "b2_done", "stored"))
        HB_ = (0, 1, 4, 5)

        def mlp_phase():
            with ExitStack() as scope:
                xn = sb("mlp_xn", [P, TB, D], scope=scope)
                x_hl = [sb(f"mlp_x{n}", [P, KC, T], F32R, scope=scope) for n in range(2)]
                hid = sb("hid", [P, 4, 512], scope=scope)
                hT = [sb(f"hT{n}", [P, 2, HC, 512], F32R, scope=scope) for n in range(2)]
                block = scope.enter_context(nc.Block())

                @block.vector
                def _(dve):
                    with dve.Fori(0, B) as b:
                        ln_vector(dve, b + 3 * B, b, xn)
                        dve.wait_ge(hid_ps, 1 + HC * NC_ * b)
                        ln_low_parts(dve, b + 3 * B, lambda k, c: x_hl[0][:, k, c * 512:(c + 1) * 512],
                                     lambda k, c: x_hl[1][:, k, c * 512:(c + 1) * 512])
                        for c in range(NC_ + 1):
                            if c < NC_:
                                for f in range(HC):
                                    w = (b * NC_ + c) * HC + f
                                    dve.wait_ge(hid_hi, 1 + w + 1)
                                    nc.vector.tensor_tensor(hT[1][:, c, f, :], hid[:, f % 4, :],
                                                            hT[0][:, c, f, :].bitcast(F32),
                                                            ALU.subtract).then_inc(hid_lo, 1)
                            if c >= 1:
                                for t in range(4):
                                    w = b * TB + (c - 1) * 4 + t
                                    dve.wait_ge(b2_done, 1 + TB * (b + 1))
                                    dve.wait_ge(mo_ps, 1 + w + 1)
                                    nc.vector.tensor_tensor(h[:, w, :], h[:, w, :], ps[:, 6 + t % 2, 0:D],
                                                            ALU.add).then_inc(mo_done, 1)

                @block.gpsimd
                def _(pool):
                    with pool.Fori(0, B) as b:
                        pool.wait_ge(xn_done, 1 + TB * (b + 3 * B + 1))
                        for t in range(TB):
                            nc.gpsimd.tensor_tensor(h[:, b * TB + t, :], h[:, b * TB + t, :], b2_sb[:],
                                                    ALU.add).then_inc(b2_done, 1)

                @block.scalar
                def _(act):
                    with act.Fori(0, B) as b:
                        act.wait_ge(hid_ps, 1 + HC * NC_ * b)
                        ln_scalar(act, b + 3 * B, lambda k, c: x_hl[0][:, k, c * 512:(c + 1) * 512])
                        for c in range(NC_):
                            for f in range(HC):
                                w = (b * NC_ + c) * HC + f
                                act.wait_ge(hid_ps, 1 + w + 1)
                                act.wait_ge(hid_lo, 1 + b * NC_ * HC + max(c * HC + f - 3, 0))
                                nc.scalar.activation(hid[:, f % 4, :], ps[:, HB_[f % 4], :],
                                                     ACT.Gelu, bias=b1_sb[:, f:f + 1]).then_inc(hid_f, 1)
                                act.wait_ge(hid_f, 1 + w + 1)
                                act.wait_ge(mo_ps, 1 + TB * b)
                                nc.scalar.activation(hT[0][:, c, f, :], hid[:, f % 4, :], ACT.Copy).then_inc(hid_hi, 1)

                @block.tensor
                def _(pe):
                    with pe.Fori(0, B) as b:
                        pe.wait_ge(xlo_done, 1 + 4 * (b + B))
                        pe.wait_ge(hid_f, 1 + HC * NC_ * b)
                        ln_tensor(pe, b + 3 * B, xn)
                        pe.wait_ge(xlo_done, 1 + 4 * (b + B + 1))
                        for c in range(NC_ + 1):
                            if c < NC_:
                                for f in range(HC):
                                    pe.wait_ge(hid_f, 1 + b * NC_ * HC + max(c * HC + f - 3, 0))
                                    products(ps[:, HB_[f % 4], :], lambda x, k: w1T[x][:, k, f * P:(f + 1) * P],
                                             lambda x, k: x_hl[x][:, k, c * 512:(c + 1) * 512], KC).then_inc(hid_ps, 1)
                            if c >= 1:
                                pe.wait_ge(hid_lo, 1 + (b * NC_ + c) * HC)
                                for t in range(4):
                                    pe.wait_ge(mo_done, 1 + b * TB + max(4 * (c - 1) + t - 1, 0))
                                    products(ps[:, 6 + t % 2, 0:D], lambda x, f: hT[x][:, c - 1, f, t * P:(t + 1) * P],
                                             lambda x, f: w2T[x][:, f, :], HC).then_inc(mo_ps, 1)

                @block.sync
                def _(sp):
                    with sp.Fori(0, NT) as w:
                        sp.wait_ge(mo_done, 1 + w + 1)
                        sp.dma_start(out[bass.ds(w * P, P), :], h[:, w, :]).then_inc(stored, 16)
                    sp.wait_ge(stored, 1 + 16 * NT)

        with nc.Block() as block:
            @block.sync
            def _(sp):
                for s in semaphores[0::5]:
                    sp.sem_inc(s, 1)

            @block.vector
            def _(dve):
                for s in semaphores[1::5]:
                    dve.sem_inc(s, 1)

            @block.scalar
            def _(act):
                for s in semaphores[2::5]:
                    act.sem_inc(s, 1)

            @block.tensor
            def _(pe):
                for s in semaphores[3::5]:
                    pe.sem_inc(s, 1)

            @block.gpsimd
            def _(pool):
                for s in semaphores[4::5]:
                    pool.sem_inc(s, 1)

        embed_phase()
        for layer in range(2):
            with ExitStack() as scope:
                v_all = attn = sb(f"v_attn{layer}", [P, TB, B * D], scope=scope)
                stacks = sb(f"stacks{layer}", [P, 3, 2, 4, T], BF16, scope=scope)
                qkv_phase(layer, v_all)
                if layer == 0:
                    softplus_attention(v_all, stacks, attn)
                else:
                    softmax_attention(v_all, stacks, attn)
                proj_phase(layer, attn)
            if layer == 0:
                experts_phase()
            else:
                mlp_phase()


def kernel(**inputs):
    import numpy as np
    import concourse.bacc as bacc
    from concourse.bass_utils import run_bass_kernel_spmd

    a = {k: np.asarray(v) for k, v in inputs.items()}
    D = 256

    def chunks(w):
        return w.reshape(-1, P, w.shape[-1]).transpose(1, 0, 2)

    gu = a["L0_ffn_gate_up_w"]
    gub = a["L0_ffn_gate_up_b"]
    gu = np.concatenate([gu[:, 0::2], gu[:, 1::2]], 1)
    gub = np.concatenate([gub[:, 0::2], gub[:, 1::2]], 1)
    gu = gu.transpose(0, 2, 1).reshape(8, 2, P, 512).transpose(0, 2, 1, 3).reshape(8, P, 1024)
    dn = a["L0_ffn_down_w"].transpose(0, 2, 1).reshape(8, 2, P, D).transpose(0, 2, 1, 3).reshape(8, P, 512)
    expert_w = np.concatenate([gu, dn], 2)
    arrays = {
        "ids": a["x"].reshape(-1, P).T,
        "W0": a["L0_tok_W0"],
        "w1_tok": chunks(a["L0_tok_W1"]),
        "wqkv0": chunks(a["L0_attn_w_qkv"].T),
        "wproj0": chunks(a["L0_attn_w_proj"].T),
        "bproj0": a["L0_attn_b_proj"][None],
        "router_w": chunks(a["L0_ffn_router_w"].T),
        "router_b": a["L0_ffn_router_b"][None],
        "expert_w": expert_w,
        "gate_up_b": gub.reshape(8, 4, P).transpose(2, 0, 1),
        "down_b": a["L0_ffn_down_b"],
        "wqkv1": chunks(np.concatenate([a["L1_attn_Wq"], a["L1_attn_Wk"], a["L1_attn_Wv"]], 0).T),
        "wproj1": chunks(a["L1_attn_Wo"].T),
        "w1": chunks(a["L1_ffn_w1"]),
        "b1": a["L1_ffn_b1"].reshape(-1, P).T,
        "w2": chunks(a["L1_ffn_w2"]),
        "b2": a["L1_ffn_b2"][None],
    }
    arrays = {k: np.ascontiguousarray(v) for k, v in arrays.items()}
    nc = bacc.Bacc("TRN2", target_bir_lowering=False, num_devices=1)
    args = [nc.dram_tensor(f"in_{k}", v.shape, mybir.dt.from_np(v.dtype), kind="ExternalInput").ap()
            for k, v in arrays.items()]
    tokens = a["x"].size
    out = nc.dram_tensor("out", (tokens, D), F32, kind="ExternalOutput").ap()
    lm_tower(nc, *args, out)
    r = run_bass_kernel_spmd(nc, [{f"in_{k}": v for k, v in arrays.items()}], core_ids=[0])
    return r.results[0]["out"].reshape(*a["x"].shape, D)
```

```python
from contextlib import ExitStack

import concourse.bass as bass
from concourse import mybir

F32 = mybir.dt.float32
F32R = mybir.dt.float32r
BF16 = mybir.dt.bfloat16
I32 = mybir.dt.int32
U32 = mybir.dt.uint32
ALU = mybir.AluOpType
ACT = mybir.ActivationFunctionType
AX = mybir.AxisListType

P = 128
EPS = 1e-5
NEG = -1e30
CAP = 40.0


def lm_tower(nc, ids, W0, w1_tok, wqkv0, wproj0, bproj0, router_w, router_b, expert_w, gate_up_b,
             down_b, wqkv1, wproj1, w1, b1, w2, b2, out):
    NT = ids.shape[1]
    VOCAB, KD = W0.shape
    D = out.shape[1]
    B = 2
    TB = NT // B
    T = TB * P
    KT = KD // P
    KC = D // P
    H, HD = 16, 16
    G = H // 4
    NG = B * G
    NE = router_w.shape[2]
    HC = w1.shape[1]
    QC = T // 512
    CW = 4 * HD
    KR = 6 * HD
    Q_PARTS, K_PARTS = (0, 0, 0, 1, 1, 2), (0, 1, 2, 0, 1, 0)

    STRIPS = [(qc, i, 512 - P * max(0, i - 4 * qc)) for qc in range(QC) for n in range(2 * qc + 2)
              for i in (n, 4 * qc + 3 - n)]
    NC_ = T // 512
    NS = len(STRIPS)
    UNITS = [(m, heads) for m in range(NS) for heads in (((0, 1, 2, 3),) if STRIPS[m][2] <= 256 else ((0, 1), (2, 3)))]
    NU = len(UNITS)
    OF_STRIP = [[u for u in range(NU) if UNITS[u][0] == m] for m in range(NS)]
    LAST = {qc: max(m for m, s in enumerate(STRIPS) if s[0] == qc) for qc in range(QC)}

    scratch = nc.dram_tensor("qk_parts", (2, 2, 3, B * D, T), BF16, kind="Internal").ap()

    with ExitStack() as ctx:
        semaphores = []

        def sem(name):
            semaphores.append(ctx.enter_context(nc.semaphore(name)))
            return semaphores[-1]

        waited = sem("waited")

        def plain(eng):
            eng.sem_inc(waited, 1)

        def sb(name, shape, dt=F32, scope=ctx):
            return scope.enter_context(nc.sbuf_tensor(name, shape, dt))

        ps = ctx.enter_context(nc.psum_tensor("ps", [P, 8, 512], F32))

        h = sb("h", [P, NT, D])
        w1t_sb = sb("w1t_sb", [P, KT, D])
        wqkv_sb = [sb(f"wqkv_sb{n}", [P, KC, 3 * D]) for n in range(2)]
        wproj_sb = [sb(f"wproj_sb{n}", [P, KC, D]) for n in range(2)]
        bproj_sb = sb("bproj_sb", [P, D])
        rw_sb = sb("rw_sb", [P, KC, NE])
        rb_sb = sb("rb_sb", [P, NE])
        gub_sb = sb("gub_sb", [P, NE, 4])
        sgb_sb = sb("sgb_sb", [P, NE, 4])
        upb_sb = sb("upb_sb", [P, NE, 4])
        dnb_sb = sb("dnb_sb", [NE, D])
        w1T = [sb(f"w1T{n}", [P, KC, HC * P], F32R) for n in range(2)]
        w2T = [sb(f"w2T{n}", [P, HC, D], F32R) for n in range(2)]
        b1_sb = sb("b1_sb", [P, HC])
        b2_sb = sb("b2_sb", [P, D])
        ids_sb = sb("ids_sb", [P, NT], I32)

        ident = sb("ident", [P, P])
        identb = sb("identb", [P, P], BF16)
        mask_qk = sb("mask_qk", [P, P], BF16)
        mask_kq = sb("mask_kq", [P, P], BF16)
        expert_no = sb("expert_no", [P, NE])
        eps_sb = sb("eps_sb", [P, 1])

        stats = sb("stats", [P, NT, 6])
        mv = sb("mv", [P, TB, 2])
        sd = sb("sd", [P, TB])
        rsd = sb("rsd", [P, TB])

        w_in = {n: sem(f"w_in_{n}") for n in ("tok", "qkv0", "mlp", "rest", "ids")}
        const_made = sem("const_made")
        id_step, ids_ready = sem("id_step"), sem("ids_ready")
        gathered = [ctx.enter_context(nc.semaphore(f"gathered{t}")) for t in range(TB)]
        rows_T, rows_Tc = sem("rows_T"), sem("rows_Tc")
        emb_done, h_ready = sem("emb_done"), sem("h_ready")
        alpha_step, sign_done, eff_done, wT_ps, wT_hi, wT_lo = (
            sem(n) for n in ("alpha_step", "sign_done", "eff_done", "wT_ps", "wT_hi", "wT_lo"))

        W_BLOCKS = [("w1", c, k) for k in range(KC) for c in range(HC)] + \
                   [("w2", k, c) for c in range(HC) for k in range(KC)]

        def embed_phase():
            with ExitStack() as scope:
                rows = sb("rows", [P, TB, KD], scope=scope)
                rowsT = sb("rowsT", [P, 2, KD], scope=scope)
                raw_w1 = sb("raw_w1", [P, HC, D], scope=scope)
                raw_w2 = sb("raw_w2", [P, KC, HC * P], scope=scope)
                sgn_w1 = sb("sgn_w1", [P, HC, D], scope=scope)
                sgn_w2 = sb("sgn_w2", [P, KC, HC * P], scope=scope)
                alpha = sb("alpha", [P, HC + KC], scope=scope)
                idf = sb("idf", [P, NT], scope=scope)
                idn = sb("idn", [P, NT], scope=scope)
                idc = sb("idc", [P, NT], U32, scope=scope)
                tok_scale = sb("tok_scale", [P, NT], scope=scope)
                block = scope.enter_context(nc.Block())

                @block.sync
                def _(sp):
                    sp.dma_start(ids_sb[:], ids).then_inc(w_in["ids"], 16)
                    sp.dma_start(w1t_sb[:], w1_tok).then_inc(w_in["tok"], 16)
                    sp.dma_start(raw_w1[:], w1).then_inc(w_in["mlp"], 16)
                    sp.dma_start(raw_w2[:], w2).then_inc(w_in["mlp"], 16)
                    sp.dma_start(wqkv_sb[0][:], wqkv0).then_inc(w_in["qkv0"], 16)
                    for dst, src in ((wqkv_sb[1], wqkv1), (wproj_sb[0], wproj0), (wproj_sb[1], wproj1),
                                     (rw_sb, router_w), (gub_sb, gate_up_b), (dnb_sb, down_b),
                                     (b1_sb, b1)):
                        sp.dma_start(dst[:], src).then_inc(w_in["rest"], 16)
                    for dst, src in ((bproj_sb, bproj0), (rb_sb, router_b), (b2_sb, b2)):
                        sp.dma_start(dst[:], src.to_broadcast((P, src.shape[1]))).then_inc(w_in["rest"], 16)

                @block.gpsimd
                def _(pool):
                    for m in (ident, identb, mask_qk, mask_kq):
                        nc.gpsimd.memset(m[:], 0.0).then_inc(const_made, 1)
                    pool.wait_ge(const_made, 1 + 4)
                    for m in (ident, identb):
                        nc.gpsimd.affine_select(out=m[:], in_=m[:], compare_op=ALU.not_equal, fill=1.0, base=0,
                                                pattern=[[-1, P]], channel_multiplier=1).then_inc(const_made, 1)
                    nc.gpsimd.affine_select(out=mask_qk[:], in_=mask_qk[:], compare_op=ALU.is_ge, fill=NEG, base=0,
                                            pattern=[[-1, P]], channel_multiplier=1).then_inc(const_made, 1)
                    nc.gpsimd.affine_select(out=mask_kq[:], in_=mask_kq[:], compare_op=ALU.is_ge, fill=NEG, base=0,
                                            pattern=[[1, P]], channel_multiplier=-1).then_inc(const_made, 1)
                    nc.gpsimd.iota(expert_no[:], pattern=[[1, NE]], base=0, channel_multiplier=0,
                                   allow_small_or_imprecise_dtypes=True).then_inc(const_made, 1)
                    pool.wait_ge(ids_ready, 1 + 1)
                    for b in range(B):
                        for t in range(TB):
                            pool.wait_ge(rows_T, 1 + b * (t + 1))
                            nc.gpsimd.indirect_dma_start(
                                rows[:, t, :], None, W0,
                                bass.IndirectOffsetOnAxis(ap=idc[:, b * TB + t:b * TB + t + 1], axis=0),
                            ).then_inc(gathered[t], 16)

                def w_dst(part, n):
                    if n < 4:
                        return w1T[part][:, n // 2, (n % 2) * 512:(n % 2) * 512 + 512]
                    return w2T[part][:, 2 * (n - 4):2 * (n - 4) + 2, :].rearrange("p c d -> p (c d)")

                @block.vector
                def _(dve):
                    nc.vector.memset(eps_sb[:], EPS)
                    dve.wait_ge(w_in["ids"], 1 + 16)
                    nc.vector.tensor_copy(idf[:], ids_sb[:]).then_inc(id_step, 1)
                    dve.wait_ge(id_step, 1 + 1)
                    nc.vector.tensor_scalar(idn[:], idf[:], 0.0, float(VOCAB), ALU.is_lt,
                                            ALU.mult).then_inc(id_step, 1)
                    nc.vector.tensor_scalar(tok_scale[:], idf[:], 0.0, float(D) ** 0.5, ALU.not_equal,
                                            ALU.mult).then_inc(id_step, 1)
                    dve.wait_ge(id_step, 1 + 3)
                    nc.vector.tensor_tensor(idn[:], idn[:], idf[:], ALU.add).then_inc(id_step, 1)
                    dve.wait_ge(id_step, 1 + 4)
                    nc.vector.tensor_scalar(idc[:], idn[:], float(VOCAB - 1), 0.0, ALU.min,
                                            ALU.max).then_inc(ids_ready, 1)
                    dve.wait_ge(w_in["mlp"], 1 + 32)
                    nc.vector.tensor_reduce(alpha[:, 0:HC], raw_w1[:], AX.X, ALU.add,
                                            apply_absolute_value=True).then_inc(alpha_step, 1)
                    nc.vector.tensor_reduce(alpha[:, HC:HC + KC], raw_w2[:], AX.X, ALU.add,
                                            apply_absolute_value=True).then_inc(alpha_step, 1)
                    dve.wait_ge(alpha_step, 1 + 2)
                    nc.vector.tensor_scalar(alpha[:, 0:HC], alpha[:, 0:HC], 1.0 / D, None,
                                            ALU.mult).then_inc(alpha_step, 1)
                    nc.vector.tensor_scalar(alpha[:, HC:HC + KC], alpha[:, HC:HC + KC], 1.0 / (HC * P), None,
                                            ALU.mult).then_inc(alpha_step, 1)
                    both = ((sgn_w1, raw_w1), (sgn_w2, raw_w2))
                    for sg, w in both:
                        nc.vector.tensor_scalar(sg[:], w[:], 0.0, None, ALU.is_gt).then_inc(sign_done, 1)
                    for n, (sg, w) in enumerate(both):
                        dve.wait_ge(sign_done, 1 + n + 1)
                        nc.vector.scalar_tensor_tensor(sg[:], w[:], 0.0, sg[:], ALU.is_lt,
                                                       ALU.subtract).then_inc(sign_done, 1)
                    dve.wait_ge(alpha_step, 1 + 4)
                    parts = [(sgn_w1[:, c, :], raw_w1[:, c, :], alpha[:, c:c + 1]) for c in range(HC)] + \
                            [(sgn_w2[:, k, :], raw_w2[:, k, :], alpha[:, HC + k:HC + k + 1]) for k in range(KC)]
                    for n, (sg, w, al) in enumerate(parts):
                        dve.wait_ge(sign_done, 1 + 2 + (1 if n < HC else 2))
                        nc.vector.scalar_tensor_tensor(sg, sg, al, w, ALU.mult, ALU.add).then_inc(eff_done, 1)
                    for n, (sg, w) in enumerate(both):
                        dve.wait_ge(eff_done, 1 + (HC + KC if n else HC))
                        nc.vector.tensor_tensor(sg[:], w[:], sg[:], ALU.subtract).then_inc(eff_done, 1)
                    for n in range(len(W_BLOCKS) // 4):
                        dve.wait_ge(wT_hi, 1 + n + 1)
                        nc.vector.tensor_tensor(w_dst(1, n), ps[:, 4 + n % 4, :], w_dst(0, n).bitcast(F32),
                                                ALU.subtract).then_inc(wT_lo, 1)
                    dve.wait_ge(w_in["rest"], 1 + 16 * 10)
                    nc.vector.tensor_scalar(sgb_sb[:], gub_sb[:], 1.702, None, ALU.mult)
                    nc.vector.tensor_scalar(upb_sb[:], gub_sb[:], 1.0, None, ALU.add)

                @block.tensor
                def _(pe):
                    pe.wait_ge(const_made, 1 + 9)
                    pe.wait_ge(w_in["tok"], 1 + 16)
                    with pe.Fori(0, B) as b:
                        for t in range(TB + 1):
                            if t < TB:
                                pe.wait_ge(gathered[t], 16 * (b + 1))
                                pe.wait_ge(rows_Tc, 1 + TB * b + max(t - 1, 0))
                                for k in range(KT):
                                    last = nc.tensor.transpose(ps[:, t % 2, k * P:(k + 1) * P],
                                                               rows[:, t, k * P:(k + 1) * P], ident[:])
                                last.then_inc(rows_T, 1)
                            if t >= 1:
                                pe.wait_ge(rows_Tc, 1 + TB * b + t)
                                pe.wait_ge(h_ready, 1 + TB * b + max(t - 2, 0))
                                for k in range(KT):
                                    last = nc.tensor.matmul(ps[:, 2 + (t - 1) % 2, 0:D],
                                                            rowsT[:, (t - 1) % 2, k * P:(k + 1) * P],
                                                            w1t_sb[:, k, :], start=(k == 0), stop=(k == KT - 1))
                                last.then_inc(emb_done, 1)
                    pe.wait_ge(eff_done, 1 + HC + KC + 2)
                    for n in range(len(W_BLOCKS) // 4):
                        if n >= 4:
                            pe.wait_ge(wT_lo, 1 + n - 3)
                        for i in range(4):
                            kind, r, c = W_BLOCKS[4 * n + i]
                            src = (sgn_w1 if kind == "w1" else sgn_w2)[:, r, c * P:(c + 1) * P]
                            last = nc.tensor.transpose(ps[:, 4 + n % 4, i * P:(i + 1) * P], src, ident[:])
                        last.then_inc(wT_ps, 1)

                @block.scalar
                def _(act):
                    act.wait_ge(ids_ready, 1 + 1)
                    with act.Fori(0, B) as b:
                        for t in range(TB + 1):
                            if t < TB:
                                act.wait_ge(rows_T, 1 + TB * b + t + 1)
                                act.wait_ge(emb_done, 1 + TB * b + max(t - 1, 0))
                                nc.scalar.activation(rowsT[:, t % 2, :], ps[:, t % 2, :],
                                                     ACT.Copy).then_inc(rows_Tc, 1)
                            if t >= 1:
                                act.wait_ge(emb_done, 1 + TB * b + t)
                                plain(act)
                                nc.scalar.activation(h[:, b * TB + t - 1, :], ps[:, 2 + (t - 1) % 2, 0:D], ACT.Copy,
                                                     scale=tok_scale[:, bass.ds(b * TB + t - 1, 1)]).then_inc(h_ready, 1)
                    for n in range(len(W_BLOCKS) // 4):
                        act.wait_ge(wT_ps, 1 + n + 1)
                        nc.scalar.activation(w_dst(0, n), ps[:, 4 + n % 4, :], ACT.Copy).then_inc(wT_hi, 1)

        st_done, mv_done, sd_done, rsd_done, xn_done, xn_T, xT_done, xlo_done = (
            sem(n) for n in ("st_done", "mv_done", "sd_done", "rsd_done", "xn_done", "xn_T", "xT_done", "xlo_done"))

        def ln_vector(dve, n, b, xn, known=False):
            for t in range(TB):
                if not known:
                    nc.vector.bn_stats(stats[:, b * TB + t, :], h[:, b * TB + t, :]).then_inc(st_done, 1)
            for t in range(TB):
                dve.wait_ge(st_done, 1 + TB * n + t + 1)
                nc.vector.bn_aggr(mv[:, t, :], stats[:, b * TB + t, :]).then_inc(mv_done, 1)
            dve.wait_ge(sd_done, 1 + n + 1)
            nc.vector.reciprocal(rsd[:], sd[:]).then_inc(rsd_done, 1)
            dve.wait_ge(rsd_done, 1 + n + 1)
            dve.wait_ge(xn_T, 1 + 4 * n)
            for t in range(TB):
                nc.vector.tensor_scalar(xn[:, t, :], h[:, b * TB + t, :], mv[:, t, 0:1], rsd[:, t:t + 1],
                                        ALU.subtract, ALU.mult).then_inc(xn_done, 1)

        def ln_deviation(act, n):
            act.wait_ge(mv_done, 1 + TB * (n + 1))
            nc.scalar.activation(sd[:], mv[:, :, 1], ACT.Sqrt, bias=eps_sb[:]).then_inc(sd_done, 1)

        def ln_scalar(act, n, dst, banks=(0, 1, 2, 3)):
            for c in range(NC_):
                for k in range(KC):
                    act.wait_ge(xn_T, 1 + 4 * n + KC * c + k + 1)
                    nc.scalar.activation(dst(k, c), ps[:, banks[KC * c + k], :], ACT.Copy).then_inc(xT_done, 1)

        def ln_low_parts(dve, n, x_hl, b, banks=(0, 1, 2, 3)):
            for c in range(NC_):
                for k in range(KC):
                    dve.wait_ge(xT_done, 1 + 4 * n + KC * c + k + 1)
                    cols = slice(b * T + c * 512, b * T + (c + 1) * 512)
                    nc.vector.tensor_tensor(x_hl[1][:, k, cols], ps[:, banks[KC * c + k], :],
                                            x_hl[0][:, k, cols].bitcast(F32), ALU.subtract).then_inc(xlo_done, 1)

        def ln_tensor(pe, n, xn, banks=(0, 1, 2, 3)):
            for c in range(NC_):
                pe.wait_ge(xn_done, 1 + TB * n + 4 * c + 4)
                for k in range(KC):
                    for i in range(4):
                        last = nc.tensor.transpose(ps[:, banks[KC * c + k], i * P:(i + 1) * P],
                                                   xn[:, 4 * c + i, k * P:(k + 1) * P], ident[:])
                    last.then_inc(xn_T, 1)

        qk_ps, qk_hi, qk_r, qk_mid, qk_lo, v_ps, v_done, res_bias = (
            sem(n) for n in ("qk_ps", "qk_hi", "qk_r", "qk_mid", "qk_lo", "v_ps", "v_done", "res_bias"))
        qk_out = [sem("qk_out0"), sem("qk_out1")]
        NF = 2 * KC * NC_
        SCALE = HD ** -0.5

        def qkv_phase(layer, v_all, stacks):
            with ExitStack() as scope:
                xn = sb(f"xn{layer}", [P, TB, D], scope=scope)
                xT = sb(f"xT{layer}", [P, B, KC, T], scope=scope)
                splits = sb(f"splits{layer}", [P, 2, 3, 512], BF16, scope=scope)
                rest = sb(f"rest{layer}", [P, 2, 512], scope=scope)
                block = scope.enter_context(nc.Block())

                def factor(u):
                    return SCALE if u < NF // 2 else 1.0

                n0, m0 = B * 2 * layer, B * layer

                @block.vector
                def _(dve):
                    for b in range(B):
                        ln_vector(dve, n0 + b, b, xn)
                    with dve.Fori(0, B) as b:
                        m = b + m0
                        for u in range(NF):
                            dve.wait_ge(qk_hi, 1 + NF * m + u + 1)
                            nc.vector.scalar_tensor_tensor(rest[:, u % 2, :], ps[:, 4 + u % 2, :], factor(u),
                                                           splits[:, u % 2, 0, :], ALU.mult,
                                                           ALU.subtract).then_inc(qk_r, 1)
                            dve.wait_ge(qk_r, 1 + NF * m + u + 1)
                            nc.vector.tensor_copy(splits[:, u % 2, 1, :], rest[:, u % 2, :]).then_inc(qk_mid, 1)
                            dve.wait_ge(qk_mid, 1 + NF * m + u + 1)
                            nc.vector.tensor_tensor(splits[:, u % 2, 2, :], rest[:, u % 2, :], splits[:, u % 2, 1, :],
                                                    ALU.subtract).then_inc(qk_lo, 1)

                @block.scalar
                def _(act):
                    def transposed(b):
                        ln_scalar(act, n0 + b, lambda k, c: xT[:, b, k, c * 512:(c + 1) * 512])

                    def qk_high(b):
                        m = m0 + b
                        for u in range(NF):
                            act.wait_ge(qk_ps, 1 + NF * m + u + 1)
                            act.wait_ge(qk_out[u % 2], 1 + 16 * (NF // 2 * m + u // 2))
                            nc.scalar.activation(splits[:, u % 2, 0, :], ps[:, 4 + u % 2, :], ACT.Copy,
                                                 scale=factor(u)).then_inc(qk_hi, 1)

                    def v_out(b):
                        for t in range(TB):
                            act.wait_ge(v_ps, 1 + TB * (m0 + b) + t + 1)
                            nc.scalar.activation(v_all[:, t, b * D:(b + 1) * D], ps[:, 6 + t % 2, 0:D],
                                                 ACT.Copy).then_inc(v_done, 1)
                    ln_deviation(act, n0)
                    transposed(0)
                    ln_deviation(act, n0 + 1)
                    qk_high(0)
                    transposed(1)
                    v_out(0)
                    qk_high(1)
                    v_out(1)

                @block.tensor
                def _(pe):
                    def qk(b):
                        m = m0 + b
                        pe.wait_ge(xT_done, 1 + 4 * (n0 + b + 1))
                        for u in range(NF):
                            qk, f, c = u // 4, u // 2 % 2, u % 2
                            pe.wait_ge(qk_r, 1 + max(NF * m + u - 1, 0))
                            for k in range(KC):
                                last = nc.tensor.matmul(ps[:, 4 + u % 2, :],
                                                        wqkv_sb[layer][:, k, qk * D + f * P:qk * D + (f + 1) * P],
                                                        xT[:, b, k, c * 512:(c + 1) * 512],
                                                        start=(k == 0), stop=(k == KC - 1))
                            last.then_inc(qk_ps, 1)

                    def v(b):
                        for t in range(TB):
                            pe.wait_ge(v_done, 1 + max(TB * (m0 + b) + t - 1, 0))
                            for k in range(KC):
                                last = nc.tensor.matmul(ps[:, 6 + t % 2, 0:D], xT[:, b, k, t * P:(t + 1) * P],
                                                        wqkv_sb[layer][:, k, 2 * D:3 * D],
                                                        start=(k == 0), stop=(k == KC - 1))
                            last.then_inc(v_ps, 1)
                    if layer == 0:
                        pe.wait_ge(w_in["qkv0"], 1 + 16)
                    else:
                        pe.wait_ge(w_in["rest"], 1 + 16 * 10)
                    ln_tensor(pe, n0, xn)
                    qk(0)
                    ln_tensor(pe, n0 + 1, xn)
                    v(0)
                    qk(1)
                    v(1)

                @block.sync
                def _(sp):
                    for b in range(B):
                        m = m0 + b
                        for u in range(NF):
                            qk, f, c = u // 4, u // 2 % 2, u % 2
                            sp.wait_ge(qk_lo, 1 + NF * m + u + 1)
                            dst = scratch[layer, qk, :, b * D + f * P:b * D + (f + 1) * P, c * 512:(c + 1) * 512]
                            sp.dma_start(dst.rearrange("r p t -> p r t"),
                                         splits[:, u % 2, :, :]).then_inc(qk_out[u % 2], 16)
                        for x in range(2):
                            sp.wait_ge(qk_out[x], 1 + 16 * NF // 2 * (m + 1))
                        if b == 0:
                            load_stack(sp, layer, 0, 0, stacks)

                if layer == 0:
                    @block.gpsimd
                    def _(pool):
                        pool.wait_ge(w_in["rest"], 1 + 16 * 10)
                        with pool.Fori(0, B) as b:
                            pool.wait_ge(xn_done, 1 + TB * (b + 1))
                            for t in range(TB):
                                nc.gpsimd.tensor_tensor(h[:, b * TB + t, :], h[:, b * TB + t, :], bproj_sb[:],
                                                        ALU.add).then_inc(res_bias, 1)

        stack_in = [[sem(f"stack_in{n}{i}") for i in range(3)] for n in range(2)]
        vg_made, vg_ready = sem("vg_made"), sem("vg_ready")
        pv_done, oT_done, o_ps, dsum_done, rden_done, attn_done = (
            sem(n) for n in ("pv_done", "oT_done", "o_ps", "dsum_done", "rden_done", "attn_done"))

        def load_stack(sp, layer, it, i, stacks):
            for qk, parts in ((0, Q_PARTS), (1, K_PARTS)):
                for r, part in enumerate(parts):
                    src = scratch[layer, qk, part, bass.ds(it * CW, CW), :]
                    sp.dma_start(stacks[r * HD:(r + 1) * HD, i, qk, :, :],
                                 src.rearrange("(j d) t -> d j t", d=HD)).then_inc(stack_in[layer][i], 16)

        def make_vg(pool, layer, vg):
            nc.gpsimd.memset(vg[:], 0.0).then_inc(vg_made, 1)
            pool.wait_ge(vg_made, 1 + 2 * layer + 1)
            nc.gpsimd.memset(vg[:, :, :, :, HD:HD + 1], 1.0).then_inc(vg_made, 1)
            pool.wait_ge(vg_made, 1 + 2 * layer + 2)

        def copy_values(it, i, vg, v_all):
            nc.gpsimd.tensor_copy(vg[:, i, :, :, 0:HD], v_all[:, :, bass.ds(it * CW, CW)].rearrange(
                "p t (j d) -> p t j d", j=4)).then_inc(vg_ready, 1)

        def place(u, j):
            m, heads = UNITS[u]
            col = heads.index(j) * (STRIPS[m][2] if len(heads) == 4 else 512)
            return col // 512, col % 512

        def filled(buf, u):
            m, heads = UNITS[u]
            cols = STRIPS[m][2]
            return buf[:, 0:2, 0:cols] if len(heads) == 2 else buf[:, 0:4 * cols // 512, :]

        def pe_scores(first_bank, u, stack, rows_):
            m, heads = UNITS[u]
            qc, i, cols = STRIPS[m]
            diag = i >= 4 * qc
            q0 = qc * 512 + 512 - cols
            for j in heads:
                bank, col = place(u, j)
                last = nc.tensor.matmul(ps[:, first_bank + bank, col:col + cols],
                                        stack[0:rows_, 1, j, i * P:(i + 1) * P], stack[0:rows_, 0, j, q0:q0 + cols],
                                        start=True, stop=not diag)
                if diag:
                    last = nc.tensor.matmul(ps[:, first_bank + bank, col:col + P], identb[:], mask_kq[:],
                                            start=False, stop=True)
            return last

        def ready_strip(u):
            return [m for m in range(NS) if u == OF_STRIP[m][-1]]

        def pe_values(pe, n, m, bank, vg, prob):
            qc, i, cols = STRIPS[m]
            if m == 0:
                pe.wait_ge(vg_ready, 1 + n + 1)
            if i == 0:
                pe.wait_ge(oT_done, 1 + QC * n + qc)
            for j in range(4):
                u = [u for u in OF_STRIP[m] if j in UNITS[u][1]][0]
                half, col = place(u, j)
                last = nc.tensor.matmul(ps[32 * j:32 * j + 32, bank, 512 - cols:512], vg[:, i, j, :],
                                        prob(u)[:, half, col:col + cols], start=(i == 0), stop=(m == LAST[qc]))
            last.then_inc(pv_done, 1)

        def act_sums(act, n, qc, bank, oT):
            act.wait_ge(pv_done, 1 + NS * n + LAST[qc] + 1)
            act.wait_ge(o_ps, 1 + QC * n + qc)
            nc.scalar.activation(oT[:], ps[:, bank, :], ACT.Copy).then_inc(oT_done, 1)

        def pe_token_major(pe, n, qc, bank, oT):
            pe.wait_ge(oT_done, 1 + QC * n + qc + 1)
            pe.wait_ge(attn_done, 1 + QC * n + qc)
            for i in range(4):
                last = nc.tensor.transpose(ps[:, bank, i * P:(i + 1) * P], oT[:, i * P:(i + 1) * P], ident[:])
            last.then_inc(o_ps, 1)

        def dve_norm(dve, layer, n, it, qc, bank, dsum, rden, attn):
            o = ps[:, bank, :].rearrange("p (i j c) -> p i j c", i=4, j=4)
            dve.wait_ge(o_ps, 1 + QC * n + qc + 1)
            nc.vector.tensor_scalar(dsum[:], o[:, :, :, HD], 1e-9 if layer == 0 else 0.0, None,
                                    ALU.add).then_inc(dsum_done, 1)
            dve.wait_ge(dsum_done, 1 + QC * n + qc + 1)
            nc.vector.reciprocal(rden[:], dsum[:]).then_inc(rden_done, 1)
            dve.wait_ge(rden_done, 1 + QC * n + qc + 1)
            nc.vector.tensor_tensor(
                attn[:, qc * 4:qc * 4 + 4, bass.ds(it * CW, CW)].rearrange("p i (j d) -> p i j d", j=4), o[:, :, :, 0:HD],
                rden[:].rearrange("p i (j o) -> p i j o", o=1).to_broadcast((P, 4, 4, HD)),
                ALU.mult).then_inc(attn_done, 1)

        def turn(step, lag, after):
            return [qc for qc in range(QC) if step == OF_STRIP[LAST[qc]][-1] + lag + after]

        def reach(n):
            return 1 + (max(n, 0) if isinstance(n, int) else n)

        def values_used(n, u, size):
            if u >= size:
                return NS * n + UNITS[u - size][0] + 1
            return 0 if isinstance(n, int) and n == 0 else NS * (n - 1) + UNITS[u - size + NU][0] + 1

        def over_groups(eng, per, tail, step):
            def rest(it, rnd, i, last):
                for s in range(tail, NU):
                    step(it, rnd, i, s)
                for s in range(tail):
                    if not last:
                        step(it + 1, rnd + (i + 1) // per, (i + 1) % per, s)
                    step(it, rnd, i, NU + s)
            for s in range(tail):
                step(0, 0, 0, s)
            rounds = (NG - 2) // per
            with eng.Fori(0, rounds) as rnd:
                for i in range(per):
                    rest(per * rnd + i, rnd, i, False)
            for it in range(per * rounds, NG):
                rest(it, it // per, it % per, it == NG - 1)

        sc_ps, cap_done, e_done, ln_done, mx_done = (
            sem(n) for n in ("sc_ps", "cap_done", "e_done", "ln_done", "mx_done"))
        sq_done = sem("sq_done")

        def softplus_attention(v_all, stacks, attn):
            LAG, NP = 5, 10
            TAIL = NP + 1
            assert NU % NP == 0
            with ExitStack() as scope:
                probs = sb("soft_probs", [P, NP, 2, 512], scope=scope)
                soft = sb("soft", [P, 3, 2, 512], scope=scope)
                vg = sb("vg0", [P, 3, TB, 4, 32], scope=scope)
                oT = sb("oT0", [P, 512], scope=scope)
                dsum = sb("dsum0", [P, 4, 4], scope=scope)
                rden = sb("rden0", [P, 4, 4], scope=scope)
                block = scope.enter_context(nc.Block())

                def ring(i, u):
                    return (NU * i + u) % 3

                def sc(i, u):
                    return filled(ps[:, 2 * ring(i, u):2 * ring(i, u) + 2, :], u)

                @block.sync
                def _(sp):
                    for it in range(1, NG):
                        if it >= 3:
                            sp.wait_ge(sc_ps, 1 + NU * (it - 2))
                        load_stack(sp, 0, it, it % 3, stacks)

                @block.tensor
                def _(pe):
                    def step(it, rnd, i, s):
                        if s == 0:
                            pe.wait_ge(stack_in[0][i], 1 + 16 * 12 * (rnd + 1))
                        if s < NU:
                            pe.wait_ge(mx_done, reach(NU * it + s - 2))
                            pe_scores(2 * ring(i, s), s, stacks[:, i], KR).then_inc(sc_ps, 1)
                        v = s - LAG
                        for m in ready_strip(v):
                            pe.wait_ge(sq_done, 1 + NU * it + v + 1)
                            pe_values(pe, it, m, 6, vg[:, i], lambda u: probs[:, u % NP])
                        for qc in turn(s, LAG, 2):
                            pe_token_major(pe, it, qc, 7, oT)
                    over_groups(pe, 3, TAIL, step)

                @block.scalar
                def _(act):
                    act.preload_act_table_set("natural_log_exp_and_others")

                    def step(it, rnd, i, s):
                        if s < NU:
                            x = filled(soft[:, ring(i, s)], s)
                            act.wait_ge(cap_done, 1 + NU * it + s + 1)
                            nc.scalar.activation(x, x, ACT.Exp).then_inc(e_done, 1)
                            act.wait_ge(e_done, 1 + NU * it + s + 1)
                            nc.scalar.activation(x, x, ACT.Ln, bias=1.0).then_inc(ln_done, 1)
                        for qc in turn(s, LAG, 0):
                            act_sums(act, it, qc, 6, oT)
                    over_groups(act, 3, TAIL, step)

                @block.vector
                def _(dve):
                    def step(it, rnd, i, s):
                        if s < NU:
                            dve.wait_ge(sc_ps, 1 + NU * it + s + 1)
                            nc.vector.tensor_scalar(filled(soft[:, ring(i, s)], s), sc(i, s), CAP, None,
                                                    ALU.min).then_inc(cap_done, 1)
                        v = s - 1
                        if 0 <= v < NU:
                            pr = filled(probs[:, v % NP], v)
                            x = filled(soft[:, ring(i, v)], v)
                            dve.wait_ge(ln_done, 1 + NU * it + v + 1)
                            dve.wait_ge(pv_done, 1 + values_used(it, v, NP))
                            nc.vector.tensor_tensor(pr, sc(i, v), x, ALU.max).then_inc(mx_done, 1)
                        for qc in turn(s, LAG, 3):
                            dve_norm(dve, 0, it, it, qc, 7, dsum, rden, attn)
                    over_groups(dve, 3, TAIL, step)

                @block.gpsimd
                def _(pool):
                    make_vg(pool, 0, vg)
                    for i in range(2):
                        copy_values(i, i, vg, v_all)

                    def step(it, rnd, i, s):
                        if s < NU:
                            pr = filled(probs[:, s % NP], s)
                            pool.wait_ge(mx_done, 1 + NU * it + s + 1)
                            nc.gpsimd.tensor_tensor(pr, pr, pr, ALU.mult).then_inc(sq_done, 1)
                        if s == TAIL and not (isinstance(it, int) and it >= NG - 2):
                            pool.wait_ge(pv_done, 1 + NS * it)
                            copy_values(it + 2, (i + 2) % 3, vg, v_all)
                    over_groups(pool, 3, TAIL, step)

        at_ps, at_done, proj_ps, proj_done = sem("at_ps"), sem("at_done"), sem("proj_ps"), sem("proj_done")

        def proj_phase(layer, attn):
            with ExitStack() as scope:
                attnT = sb(f"attnT{layer}", [P, 2, KC, 512], scope=scope)
                block = scope.enter_context(nc.Block())
                NQ = NT // 4

                @block.tensor
                def _(pe):
                    for n in range(NQ + 1):
                        if n < NQ:
                            for k in range(KC):
                                pe.wait_ge(at_done, 1 + KC * (NQ * layer + max(n - 1, 0)))
                                for i in range(4):
                                    b, t = n * 4 // TB, n * 4 % TB + i
                                    src = attn[:, t, b * D + k * P:b * D + (k + 1) * P]
                                    last = nc.tensor.transpose(ps[:, KC * (n % 2) + k, i * P:(i + 1) * P], src, ident[:])
                                last.then_inc(at_ps, 1)
                        if n >= 1:
                            pe.wait_ge(at_done, 1 + KC * (NQ * layer + n))
                            for i in range(4):
                                t = (n - 1) * 4 + i
                                pe.wait_ge(proj_done, 1 + NT * layer + max(t - 3, 0))
                                for k in range(KC):
                                    last = nc.tensor.matmul(ps[:, 4 + t % 4, 0:D],
                                                            attnT[:, (n - 1) % 2, k, i * P:(i + 1) * P],
                                                            wproj_sb[layer][:, k, :], start=(k == 0), stop=(k == KC - 1))
                                last.then_inc(proj_ps, 1)

                @block.scalar
                def _(act):
                    for n in range(NQ):
                        for k in range(KC):
                            act.wait_ge(at_ps, 1 + KC * (NQ * layer + n) + k + 1)
                            act.wait_ge(proj_ps, 1 + NT * layer + 4 * max(n - 1, 0))
                            nc.scalar.activation(attnT[:, n % 2, k, :], ps[:, KC * (n % 2) + k, :],
                                                 ACT.Copy).then_inc(at_done, 1)

                @block.vector
                def _(dve):
                    for t in range(NT + 1):
                        if t < NT:
                            dve.wait_ge(proj_ps, 1 + NT * layer + t + 1)
                            nc.vector.tensor_tensor(h[:, t, :], h[:, t, :], ps[:, 4 + t % 4, 0:D],
                                                    ALU.add).then_inc(proj_done, 1)
                        if t >= 1:
                            dve.wait_ge(proj_done, 1 + NT * layer + t)
                            nc.vector.bn_stats(stats[:, t - 1, :], h[:, t - 1, :]).then_inc(st_done, 1)

        rw_split, r_ps, r_step, top_done, cw_exp, cw_done, cwT_ps, cwT_done, db_ps, db_done = (
            sem(n) for n in ("rw_split", "r_ps", "r_step", "top_done", "cw_exp", "cw_done", "cwT_ps", "cwT_done",
                             "db_ps", "db_done"))
        gu_ps, sig_done, up_done, g_done, ga_done, a_done, ah_done, al_done, dn_ps, dn_done = (
            sem(n) for n in ("gu_ps", "sig_done", "up_done", "g_done", "ga_done", "a_done", "ah_done", "al_done",
                             "dn_ps", "dn_done"))
        rT_ps, rT_done = sem("rT_ps"), sem("rT_done")
        wh_done, wl_done = sem("wh_done"), sem("wl_done")
        ew_in = [sem("ew_in0"), sem("ew_in1")]
        NCH = NT // 4
        GUC = KC * 2 * KC * P
        WC = GUC + 2 * D

        def products(dst, lhs, rhs, n_k, stop=True):
            terms = [(k, a, b) for k in range(n_k) for a, b in ((0, 0), (1, 0), (0, 1))]
            for n, (k, a, b) in enumerate(terms):
                last = nc.tensor.matmul(dst, lhs(a, k), rhs(b, k), start=(n == 0), stop=(n == len(terms) - 1))
            return last

        def over_experts(eng, hidden, down, split):
            def expert(e, rnd, par, last):
                for c in range(NCH):
                    if c < NCH - 1:
                        hidden(e, par, c + 1)
                    elif not last:
                        hidden(e + 1, 1 - par, 0)
                    if c == 1 and not last:
                        split(e + 1, rnd + par, 1 - par)
                    down(e, par, c)
            with eng.Fori(0, NE // 2 - 1) as rnd:
                for par in range(2):
                    expert(2 * rnd + par, rnd, par, False)
            expert(NE - 2, NE // 2 - 1, 0, False)
            expert(NE - 1, NE // 2 - 1, 1, True)

        def nothing(*_):
            pass

        def experts_phase():
            with ExitStack() as scope:
                xn = sb("ffn_xn", [P, TB, D], scope=scope)
                x_hl = [sb(f"ffn_x{n}", [P, KC, NT * P], F32R, scope=scope) for n in range(2)]
                rw_hl = [sb(f"rw{n}", [P, KC, NE], F32R, scope=scope) for n in range(2)]
                raw = sb("expert_raw", [P, 2, WC], scope=scope)
                w_hl = [sb(f"expert_w{n}", [P, 2, WC], F32R, scope=scope) for n in range(2)]
                a_hl = [sb(f"expert_a{n}", [P, 2, 2, 512], F32R, scope=scope) for n in range(2)]
                a_sb = sb("expert_a", [P, 2, 512], scope=scope)
                sig = sb("sig", [P, 2, 512], scope=scope)
                upc = sb("upc", [P, 2, 512], scope=scope)
                gc = sb("gc", [P, 2, 512], scope=scope)
                rs = sb("rs", [P, NT, NE], scope=scope)
                top_v = sb("top_v", [P, NT, NE], scope=scope)
                top_i = sb("top_i", [P, NT, NE], U32, scope=scope)
                top_f = sb("top_f", [P, NT, NE], scope=scope)
                gap = sb("gap", [P, 4, NT], scope=scope)
                pick = sb("pick", [P, NT, NE], scope=scope)
                cw = sb("cw", [P, NT, NE], scope=scope)
                cwT = sb("cwT", [NE, NCH, 512], scope=scope)
                rT = sb("rT", [NE, NCH, 512], scope=scope)
                block = scope.enter_context(nc.Block())
                LN_BANKS = ((0, 1, 2, 3), (4, 5, 6, 7))
                guw = [w[:, :, 0:GUC].rearrange("p s (k f) -> p s k f", k=KC) for w in w_hl]
                dnw = [w[:, :, GUC:WC].rearrange("p s (k d) -> p s k d", k=2) for w in w_hl]

                def rows_bc(ap):
                    return ap.rearrange("p (t o) -> p t o", o=1).to_broadcast((P, NT, NE))

                @block.sync
                def _(sp):
                    for e in range(2):
                        sp.dma_start(raw[:, e, :], expert_w[e, :, :]).then_inc(ew_in[e], 16)
                    with sp.Fori(0, NE // 2 - 1) as rnd:
                        for par in range(2):
                            sp.wait_ge(wl_done, 1 + 2 * rnd + par + 1)
                            sp.dma_start(raw[:, par, :], expert_w[2 * rnd + par + 2, :, :]).then_inc(ew_in[par], 16)

                @block.gpsimd
                def _(pool):
                    def split(e, rnd, par):
                        pool.wait_ge(wh_done, 1 + e + 1)
                        nc.gpsimd.tensor_tensor(w_hl[1][:, par, :], raw[:, par, :],
                                                w_hl[0][:, par, :].bitcast(F32), ALU.subtract).then_inc(wl_done, 1)

                    def hidden(e, par, c):
                        for hc in range(2):
                            pool.wait_ge(ah_done, 1 + 2 * (NCH * e + c) + hc + 1)
                            nc.gpsimd.tensor_tensor(a_hl[1][:, c % 2, hc, :], a_sb[:, hc, :],
                                                    a_hl[0][:, c % 2, hc, :].bitcast(F32),
                                                    ALU.subtract).then_inc(al_done, 1)
                    split(0, 0, 0)
                    hidden(0, 0, 0)
                    over_experts(pool, hidden, nothing, split)

                @block.vector
                def _(dve):
                    def hidden(e, par, c):
                        for hc in range(2):
                            w = 2 * (NCH * e + c) + hc
                            dve.wait_ge(gu_ps, 1 + w + 1)
                            nc.vector.tensor_scalar(upc[:, hc, :], ps[:, 2 * hc + 1, :], upb_sb[:, e, 2 + hc:3 + hc],
                                                    -6.0, ALU.add, ALU.max).then_inc(up_done, 1)
                            dve.wait_ge(sig_done, 1 + w + 1)
                            nc.vector.tensor_scalar(gc[:, hc, :], ps[:, 2 * hc, :], gub_sb[:, e, hc:hc + 1],
                                                    -7.0, ALU.add, ALU.max).then_inc(g_done, 1)
                            dve.wait_ge(g_done, 1 + w + 1)
                            nc.vector.scalar_tensor_tensor(gc[:, hc, :], gc[:, hc, :], 7.0, sig[:, hc, :],
                                                           ALU.min, ALU.mult).then_inc(ga_done, 1)
                            dve.wait_ge(ga_done, 1 + w + 1)
                            dve.wait_ge(up_done, 1 + w + 1)
                            dve.wait_ge(al_done, reach(w - 1))
                            nc.vector.scalar_tensor_tensor(a_sb[:, hc, :], upc[:, hc, :], 8.0, gc[:, hc, :],
                                                           ALU.min, ALU.mult).then_inc(a_done, 1)

                    def biases():
                        dve.wait_ge(dn_done, 1 + 4 + 4 * (NCH * NE - 1))
                        for w in range(NT // 2):
                            dve.wait_ge(db_ps, 1 + w + 1)
                            nc.vector.tensor_tensor(h[:, 2 * w:2 * w + 2, :], h[:, 2 * w:2 * w + 2, :],
                                                    ps[:, w % 4, :].rearrange("p (t d) -> p t d", t=2),
                                                    ALU.add).then_inc(db_done, 1)
                        dve.wait_ge(db_done, 1 + NT // 2)

                    def down(e, par, c):
                        if isinstance(e, int) and (e, c) == (NE - 1, NCH - 1):
                            biases()
                        for t in range(4):
                            tile = 4 * c + t
                            dve.wait_ge(dn_ps, 1 + 4 * (NCH * e + c) + t + 1)
                            nc.vector.scalar_tensor_tensor(h[:, tile, :], ps[:, 4 + t, 0:D],
                                                           cw[:, tile, e:e + 1] if isinstance(e, int) else
                                                           cw[:, tile, bass.ds(e, 1)],
                                                           h[:, tile, :], ALU.mult, ALU.add).then_inc(dn_done, 1)
                    ln_vector(dve, B, 0, xn, known=True)
                    ln_low_parts(dve, B, x_hl, 0, LN_BANKS[0])
                    ln_vector(dve, B + 1, 1, xn, known=True)
                    hidden(0, 0, 0)
                    ln_low_parts(dve, B + 1, x_hl, 1, LN_BANKS[1])
                    dve.wait_ge(rw_split, 1 + 1)
                    nc.vector.tensor_tensor(rw_hl[1][:], rw_sb[:], rw_hl[0][:].bitcast(F32),
                                            ALU.subtract).then_inc(rw_split, 1)

                    def step(ins, k):
                        ins.then_inc(r_step, 1)
                        dve.wait_ge(r_step, 1 + k)
                    dve.wait_ge(r_ps, 1 + NCH)
                    step(nc.vector.tensor_tensor(
                        rs[:], ps[:, 7, 0:NT * NE].rearrange("p (t e) -> p t e", e=NE),
                        rb_sb[:].rearrange("p (o e) -> p o e", o=1).to_broadcast((P, NT, NE)), ALU.add), 1)
                    dve.sem_inc(dn_done, 4)
                    for t in range(NT):
                        nc.vector.max(top_v[:, t, :], rs[:, t, :]).then_inc(r_step, 1)
                    dve.wait_ge(r_step, 1 + 1 + NT)
                    nc.vector.tensor_tensor(gap[:, 0, :], top_v[:, :, 1], top_v[:, :, 0],
                                            ALU.subtract).then_inc(top_done, 1)
                    for t in range(NT):
                        nc.vector.max_index(top_i[:, t, :], top_v[:, t, :], rs[:, t, :]).then_inc(r_step, 1)
                    dve.wait_ge(r_step, 1 + 1 + 2 * NT)
                    k = 1 + 2 * NT
                    step(nc.vector.tensor_copy(top_f[:], top_i[:]), k + 1)
                    dve.wait_ge(cw_exp, 1 + 1)
                    step(nc.vector.tensor_scalar(gap[:, 2, :], gap[:, 1, :], 1.0, None, ALU.add), k + 2)
                    step(nc.vector.reciprocal(gap[:, 2, :], gap[:, 2, :]), k + 3)
                    step(nc.vector.tensor_tensor(gap[:, 3, :], gap[:, 1, :], gap[:, 2, :], ALU.mult), k + 4)
                    numbers = expert_no[:].rearrange("p (o e) -> p o e", o=1).to_broadcast((P, NT, NE))
                    step(nc.vector.tensor_tensor(cw[:], numbers, rows_bc(top_f[:, :, 0]), ALU.is_equal), k + 5)
                    step(nc.vector.tensor_tensor(pick[:], numbers, rows_bc(top_f[:, :, 1]), ALU.is_equal), k + 6)
                    step(nc.vector.tensor_tensor(cw[:], cw[:], rows_bc(gap[:, 2, :]), ALU.mult), k + 7)
                    step(nc.vector.tensor_tensor(pick[:], pick[:], rows_bc(gap[:, 3, :]), ALU.mult), k + 8)
                    nc.vector.tensor_tensor(cw[:], cw[:], pick[:], ALU.add).then_inc(cw_done, 1)
                    over_experts(dve, hidden, down, nothing)

                @block.scalar
                def _(act):
                    def split(e, rnd, par):
                        act.wait_ge(ew_in[par], 1 + 16 * (rnd + 1))
                        if not isinstance(e, int) or e > 0:
                            act.wait_ge(dn_ps, 1 + 4 * NCH * (e - 1))
                        nc.scalar.activation(w_hl[0][:, par, :], raw[:, par, :], ACT.Copy).then_inc(wh_done, 1)

                    def hidden(e, par, c):
                        for hc in range(2):
                            w = 2 * (NCH * e + c) + hc
                            act.wait_ge(gu_ps, 1 + w + 1)
                            act.wait_ge(ga_done, reach(w - 1))
                            plain(act)
                            nc.scalar.activation(sig[:, hc, :], ps[:, 2 * hc, :], ACT.Sigmoid,
                                                 bias=sgb_sb[:, e, hc:hc + 1], scale=1.702).then_inc(sig_done, 1)
                            act.wait_ge(a_done, 1 + w + 1)
                            act.wait_ge(dn_ps, reach(4 * (NCH * e + c - 1)))
                            nc.scalar.activation(a_hl[0][:, c % 2, hc, :], a_sb[:, hc, :],
                                                 ACT.Copy).then_inc(ah_done, 1)
                    nc.scalar.activation(rw_hl[0][:], rw_sb[:], ACT.Copy).then_inc(rw_split, 1)

                    def transposed(b):
                        ln_scalar(act, B + b, lambda k, c: x_hl[0][:, k, b * T + c * 512:b * T + (c + 1) * 512],
                                  LN_BANKS[b])
                    ln_deviation(act, B)
                    transposed(0)
                    split(0, 0, 0)
                    ln_deviation(act, B + 1)
                    hidden(0, 0, 0)
                    transposed(1)
                    for n in range(NCH):
                        act.wait_ge(rT_ps, 1 + n + 1)
                        nc.scalar.activation(rT[:, n, :], ps[0:NE, 4 + n % 3, :], ACT.Copy).then_inc(rT_done, 1)
                    act.wait_ge(top_done, 1 + 1)
                    nc.scalar.activation(gap[:, 1, :], gap[:, 0, :], ACT.Exp).then_inc(cw_exp, 1)
                    over_experts(act, hidden, nothing, split)
                    for n in range(NCH):
                        act.wait_ge(cwT_ps, 1 + n + 1)
                        nc.scalar.activation(cwT[:, n, :], ps[0:NE, n, :], ACT.Copy).then_inc(cwT_done, 1)

                @block.tensor
                def _(pe):
                    def hidden(e, par, c):
                        if c == 0:
                            pe.wait_ge(wh_done, 1 + e + 1)
                            pe.wait_ge(wl_done, 1 + e + 1)
                        for hc in range(2):
                            pe.wait_ge(g_done, reach(2 * (NCH * e + c) + hc - 1))
                            for gu in range(2):
                                f = gu * 2 * P + hc * P
                                last = products(ps[:, 2 * hc + gu, :], lambda x, k: guw[x][:, par, k, f:f + P],
                                                lambda x, k: x_hl[x][:, k, c * 512:(c + 1) * 512], KC)
                            last.then_inc(gu_ps, 1)

                    def biases():
                        pe.wait_ge(cw_done, 1 + 1)
                        pe.wait_ge(g_done, 1 + 2 * NCH * NE)
                        for n in range(NCH):
                            for t in range(4):
                                last = nc.tensor.transpose(ps[0:NE, n, t * P:(t + 1) * P], cw[:, 4 * n + t, :], ident[:])
                            last.then_inc(cwT_ps, 1)
                        for w in range(NT // 2):
                            pe.wait_ge(cwT_done, 1 + NCH)
                            pe.wait_ge(db_done, 1 + max(w - 3, 0))
                            for t in range(2):
                                last = nc.tensor.matmul(ps[:, w % 4, t * D:(t + 1) * D],
                                                        cwT[:, w // 2, (2 * (w % 2) + t) * P:(2 * (w % 2) + t + 1) * P],
                                                        dnb_sb[:], start=True, stop=True)
                            last.then_inc(db_ps, 1)

                    def down(e, par, c):
                        if isinstance(e, int) and (e, c) == (NE - 1, NCH - 1):
                            biases()
                        pe.wait_ge(al_done, 1 + 2 * (NCH * e + c) + 2)
                        for t in range(4):
                            pe.wait_ge(dn_done, 1 + 4 * (NCH * e + c) + t + 1)
                            products(ps[:, 4 + t, 0:D], lambda x, k: a_hl[x][:, c % 2, k, t * P:(t + 1) * P],
                                     lambda x, k: dnw[x][:, par, k, :], 2).then_inc(dn_ps, 1)
                    ln_tensor(pe, B, xn, LN_BANKS[0])
                    pe.wait_ge(xlo_done, 1 + 4)
                    hidden(0, 0, 0)
                    ln_tensor(pe, B + 1, xn, LN_BANKS[1])
                    pe.wait_ge(xlo_done, 1 + 8)
                    pe.wait_ge(rw_split, 1 + 2)
                    for n in range(NCH + 1):
                        if n < NCH:
                            pe.wait_ge(rT_done, 1 + max(n - 2, 0))
                            products(ps[0:NE, 4 + n % 3, :], lambda x, k: rw_hl[x][:, k, :],
                                     lambda x, k: x_hl[x][:, k, n * 512:(n + 1) * 512], KC).then_inc(rT_ps, 1)
                        if n >= 1:
                            pe.wait_ge(rT_done, 1 + n)
                            for t in range(4 * n - 4, 4 * n):
                                last = nc.tensor.transpose(ps[:, 7, t * NE:(t + 1) * NE],
                                                           rT[:, n - 1, t % 4 * P:(t % 4 + 1) * P], ident[0:NE, 0:NE])
                            last.then_inc(r_ps, 1)

                    over_experts(pe, hidden, down, nothing)

        MAXES = [(j, t, k0, min(512, (t + 1) * P - k0)) for n in range(TB // 2) for j in range(4)
                 for t in (n, TB - 1 - n) for k0 in range(0, (t + 1) * P, 512)]
        NM = len(MAXES)
        assert NM % 3 == 0 and NU % 2 == 0
        M_END = 14

        def maxes_after(u):
            return range(NM * min(u, M_END) // M_END, NM * min(u + 1, M_END) // M_END)

        am_ps, am_done, am_all, mT_ps, m_step, m_out = (
            sem(n) for n in ("am_ps", "am_done", "am_all", "mT_ps", "m_step", "m_out"))
        sb_ps, p_done, ones_done = sem("sb_ps"), sem("p_done"), sem("ones_done")

        def softmax_attention(v_all, stacks, attn):
            LAG, NP = 8, 10
            MAX_BANKS = (4, 5, 7)
            TAIL = NP + 1
            assert NU % NP == 0
            with ExitStack() as scope:
                probs = sb("probs", [P, NP, 2, 512], scope=scope)
                vg = sb("vg1", [P, 3, TB, 4, 32], scope=scope)
                oT = sb("oT1", [P, 512], scope=scope)
                dsum = sb("dsum1", [P, 4, 4], scope=scope)
                rden = sb("rden1", [P, 4, 4], scope=scope)
                mx1 = sb("mx1", [P, 4, TB], scope=scope)
                mx2 = sb("mx2", [P, 4, TB], scope=scope)
                m_rest = sb("m_rest", [4 * TB, P], scope=scope)
                m_parts = sb("m_parts", [4 * TB, 3, P], BF16, scope=scope)
                block = scope.enter_context(nc.Block())

                def last(it):
                    return isinstance(it, int) and it == NG - 1

                @block.sync
                def _(sp):
                    def send_maxima(n, i):
                        sp.wait_ge(m_step, 1 + 4 * (n + 1))
                        for x in range(3):
                            sp.dma_start(stacks[KR + x:KR + x + 1, i, 0, :, :].rearrange("o j (t q) -> o (j t) q", q=P),
                                         m_parts[:, x, :]).then_inc(m_out, 16)
                    for it in range(1, 3):
                        load_stack(sp, 1, it, it, stacks)
                    sp.wait_ge(ones_done, 1 + 1)
                    send_maxima(0, 0)
                    for it in range(NG - 1):
                        send_maxima(it + 1, (it + 1) % 3)
                        if it + 3 < NG:
                            sp.wait_ge(sb_ps, 1 + NU * (it + 1))
                            load_stack(sp, 1, it + 3, it % 3, stacks)

                @block.tensor
                def _(pe):
                    def maxes(n, i, units):
                        for w in units:
                            j, t, k0, keys = MAXES[w]
                            diag = k0 + keys == (t + 1) * P
                            if w == 0 and not (isinstance(n, int) and n == 0):
                                pe.wait_ge(m_step, 1 + 4 * (n - 1) + 2)
                            pe.wait_ge(am_done, reach(NM * n + w - 2))
                            bank = MAX_BANKS[w % 3]
                            scores = nc.tensor.matmul(ps[:, bank, 0:keys], stacks[0:KR, i, 0, j, t * P:(t + 1) * P],
                                                      stacks[0:KR, i, 1, j, k0:k0 + keys], start=True, stop=not diag)
                            if diag:
                                scores = nc.tensor.matmul(ps[:, bank, keys - P:keys], identb[:], mask_qk[:],
                                                          start=False, stop=True)
                            scores.then_inc(am_ps, 1)

                    def max_rows(n):
                        pe.wait_ge(am_all, 1 + n + 1)
                        nc.tensor.transpose(ps[0:4 * TB, MAX_BANKS[0], 0:P], mx1[:].rearrange("p j t -> p (j t)"),
                                            ident[:]).then_inc(mT_ps, 1)
                    pe.wait_ge(stack_in[1][0], 1 + 16 * 12)
                    maxes(0, 0, range(NM))
                    max_rows(0)

                    def step(it, rnd, i, s):
                        n = NG + it
                        if s == 0:
                            pe.wait_ge(m_out, 1 + 48 * (it + 1))
                        for qc in turn(s, LAG, 1):
                            pe_token_major(pe, n, qc, 6, oT)
                        if s < NU:
                            pe.wait_ge(p_done, reach(NU * it + s - 1))
                            pe_scores(2 * (s % 2), s, stacks[:, i], KR + 3).then_inc(sb_ps, 1)
                            if not last(it):
                                if s == 0:
                                    pe.wait_ge(stack_in[1][(i + 1) % 3], 1 + 16 * 12 * (rnd + (i + 1) // 3 + 1))
                                maxes(it + 1, (i + 1) % 3, maxes_after(s))
                        v = s - LAG
                        for m in ready_strip(v):
                            pe.wait_ge(p_done, 1 + NU * it + v + 1)
                            if STRIPS[m][1] == 0:
                                pe.wait_ge(attn_done, 1 + QC * n + STRIPS[m][0])
                            pe_values(pe, n, m, 6, vg[:, i], lambda u: probs[:, u % NP])
                        if s == M_END + 1 and not last(it):
                            max_rows(it + 1)
                    over_groups(pe, 3, TAIL, step)

                @block.scalar
                def _(act):
                    def step(it, rnd, i, s):
                        n = NG + it
                        if s < NU:
                            act.wait_ge(sb_ps, 1 + NU * it + s + 1)
                            act.wait_ge(pv_done, 1 + values_used(n, s, NP))
                            nc.scalar.activation(filled(probs[:, s % NP], s),
                                                 filled(ps[:, 2 * (s % 2):2 * (s % 2) + 2, :], s),
                                                 ACT.Exp).then_inc(p_done, 1)
                        for qc in turn(s, LAG, 0):
                            act_sums(act, n, qc, 6, oT)
                    over_groups(act, 1, TAIL, step)

                @block.vector
                def _(dve):
                    def maxes(n, units):
                        for w in units:
                            j, t, k0, keys = MAXES[w]
                            dve.wait_ge(am_ps, 1 + NM * n + w + 1)
                            if w == 0:
                                dve.wait_ge(mT_ps, 1 + n)
                            dst = (mx2 if k0 else mx1)[:, j, t:t + 1]
                            nc.vector.reduce_max(dst, ps[:, MAX_BANKS[w % 3], 0:keys], AX.X).then_inc(am_done, 1)

                    def join(n):
                        dve.wait_ge(am_done, 1 + NM * (n + 1))
                        nc.vector.tensor_tensor(mx1[:, :, 4:TB], mx1[:, :, 4:TB], mx2[:, :, 4:TB],
                                                ALU.max).then_inc(am_all, 1)

                    def parts(n):
                        dve.wait_ge(mT_ps, 1 + n + 1)
                        dve.wait_ge(m_out, 1 + 48 * n)
                        src = ps[0:4 * TB, MAX_BANKS[0], 0:P]
                        nc.vector.tensor_scalar(m_parts[:, 0, :], src, -1.0, None, ALU.mult).then_inc(m_step, 1)
                        dve.wait_ge(m_step, 1 + 4 * n + 1)
                        nc.vector.scalar_tensor_tensor(m_rest[:], src, -1.0, m_parts[:, 0, :], ALU.mult,
                                                       ALU.subtract).then_inc(m_step, 1)
                        dve.wait_ge(m_step, 1 + 4 * n + 2)
                        nc.vector.tensor_copy(m_parts[:, 1, :], m_rest[:]).then_inc(m_step, 1)
                        dve.wait_ge(m_step, 1 + 4 * n + 3)
                        nc.vector.tensor_tensor(m_parts[:, 2, :], m_rest[:], m_parts[:, 1, :],
                                                ALU.subtract).then_inc(m_step, 1)
                    maxes(0, range(NM))
                    join(0)
                    parts(0)

                    def step(it, rnd, i, s):
                        n = NG + it
                        if s < NU and not last(it):
                            maxes(it + 1, maxes_after(s))
                            if s == M_END:
                                join(it + 1)
                            if s == M_END + 1:
                                parts(it + 1)
                        for qc in turn(s, LAG, 1):
                            dve_norm(dve, 1, n, it, qc, 6, dsum, rden, attn)
                    over_groups(dve, 1, TAIL, step)

                @block.gpsimd
                def _(pool):
                    nc.gpsimd.memset(stacks[KR:KR + 3, :, 1, :, :], 1.0).then_inc(ones_done, 1)
                    pool.wait_ge(ones_done, 1 + 1)
                    make_vg(pool, 1, vg)
                    for it in range(NG):
                        pool.wait_ge(pv_done, 1 + NS * (NG + max(it - 2, 0)))
                        copy_values(it, it % 3, vg, v_all)

        hid_ps, hid_f, hid_hi, hid_lo, mo_ps, mo_done, b2_done, stored = (
            sem(n) for n in ("hid_ps", "hid_f", "hid_hi", "hid_lo", "mo_ps", "mo_done", "b2_done", "stored"))
        HB_ = (0, 1, 4, 5)

        def mlp_phase():
            with ExitStack() as scope:
                xn = sb("mlp_xn", [P, TB, D], scope=scope)
                x_hl = [sb(f"mlp_x{n}", [P, KC, NT * P], F32R, scope=scope) for n in range(2)]
                hid = sb("hid", [P, 4, 512], scope=scope)
                hT = [sb(f"hT{n}", [P, 2, HC, 512], F32R, scope=scope) for n in range(2)]
                block = scope.enter_context(nc.Block())

                LN_BANKS = ((0, 1, 2, 3), (2, 3, 6, 7))
                n0 = 3 * B

                @block.vector
                def _(dve):
                    def hidden(c):
                        for f in range(HC):
                            dve.wait_ge(hid_hi, 1 + c * HC + f + 1)
                            nc.vector.tensor_tensor(hT[1][:, c % 2, f, :], hid[:, f % 4, :],
                                                    hT[0][:, c % 2, f, :].bitcast(F32), ALU.subtract).then_inc(hid_lo, 1)

                    def output(c):
                        dve.wait_ge(b2_done, 1 + NT)
                        for t in range(4):
                            w = 4 * c + t
                            dve.wait_ge(mo_ps, 1 + w + 1)
                            nc.vector.tensor_tensor(h[:, w, :], h[:, w, :], ps[:, 6 + t % 2, 0:D],
                                                    ALU.add).then_inc(mo_done, 1)
                    ln_vector(dve, n0, 0, xn, known=True)
                    ln_low_parts(dve, n0, x_hl, 0, LN_BANKS[0])
                    ln_vector(dve, n0 + 1, 1, xn, known=True)
                    hidden(0)
                    ln_low_parts(dve, n0 + 1, x_hl, 1, LN_BANKS[1])
                    for c in range(NCH):
                        if c < NCH - 1:
                            hidden(c + 1)
                        output(c)

                @block.gpsimd
                def _(pool):
                    with pool.Fori(0, B) as b:
                        pool.wait_ge(xn_done, 1 + TB * (b + n0 + 1))
                        for t in range(TB):
                            nc.gpsimd.tensor_tensor(h[:, b * TB + t, :], h[:, b * TB + t, :], b2_sb[:],
                                                    ALU.add).then_inc(b2_done, 1)

                @block.scalar
                def _(act):
                    def hidden(c):
                        for f in range(HC):
                            w = c * HC + f
                            act.wait_ge(hid_ps, 1 + w + 1)
                            act.wait_ge(hid_lo, reach(w - 3))
                            nc.scalar.activation(hid[:, f % 4, :], ps[:, HB_[f % 4], :],
                                                 ACT.Gelu, bias=b1_sb[:, f:f + 1]).then_inc(hid_f, 1)
                            act.wait_ge(hid_f, 1 + w + 1)
                            act.wait_ge(mo_ps, reach(4 * (c - 1)))
                            nc.scalar.activation(hT[0][:, c % 2, f, :], hid[:, f % 4, :], ACT.Copy).then_inc(hid_hi, 1)

                    def transposed(b):
                        ln_scalar(act, n0 + b, lambda k, c: x_hl[0][:, k, b * T + c * 512:b * T + (c + 1) * 512],
                                  LN_BANKS[b])
                    ln_deviation(act, n0)
                    transposed(0)
                    ln_deviation(act, n0 + 1)
                    hidden(0)
                    transposed(1)
                    for c in range(1, NCH):
                        hidden(c)

                @block.tensor
                def _(pe):
                    def hidden(c):
                        for f in range(HC):
                            pe.wait_ge(hid_f, reach(c * HC + f - 3))
                            products(ps[:, HB_[f % 4], :], lambda x, k: w1T[x][:, k, f * P:(f + 1) * P],
                                     lambda x, k: x_hl[x][:, k, c * 512:(c + 1) * 512], KC).then_inc(hid_ps, 1)

                    def output(c):
                        pe.wait_ge(hid_lo, 1 + (c + 1) * HC)
                        for t in range(4):
                            pe.wait_ge(mo_done, reach(4 * c + t - 1))
                            products(ps[:, 6 + t % 2, 0:D], lambda x, f: hT[x][:, c % 2, f, t * P:(t + 1) * P],
                                     lambda x, f: w2T[x][:, f, :], HC).then_inc(mo_ps, 1)
                    ln_tensor(pe, n0, xn, LN_BANKS[0])
                    pe.wait_ge(xlo_done, 1 + 4 * (B + 1))
                    hidden(0)
                    ln_tensor(pe, n0 + 1, xn, LN_BANKS[1])
                    for c in range(NCH):
                        if c < NCH - 1:
                            if c == 0:
                                pe.wait_ge(xlo_done, 1 + 4 * (B + 2))
                            hidden(c + 1)
                        output(c)

                @block.sync
                def _(sp):
                    with sp.Fori(0, NT) as w:
                        sp.wait_ge(mo_done, 1 + w + 1)
                        sp.dma_start(out[bass.ds(w * P, P), :], h[:, w, :]).then_inc(stored, 16)
                    sp.wait_ge(stored, 1 + 16 * NT)

        with nc.Block() as block:
            @block.sync
            def _(sp):
                for s in semaphores[0::5]:
                    sp.sem_inc(s, 1)

            @block.vector
            def _(dve):
                for s in semaphores[1::5]:
                    dve.sem_inc(s, 1)

            @block.scalar
            def _(act):
                for s in semaphores[2::5]:
                    act.sem_inc(s, 1)

            @block.tensor
            def _(pe):
                for s in semaphores[3::5]:
                    pe.sem_inc(s, 1)

            @block.gpsimd
            def _(pool):
                for s in semaphores[4::5]:
                    pool.sem_inc(s, 1)

        embed_phase()
        for layer in range(2):
            with ExitStack() as scope:
                v_all = attn = sb(f"v_attn{layer}", [P, TB, B * D], scope=scope)
                stacks = sb(f"stacks{layer}", [P, 3, 2, 4, T], BF16, scope=scope)
                qkv_phase(layer, v_all, stacks)
                if layer == 0:
                    softplus_attention(v_all, stacks, attn)
                else:
                    softmax_attention(v_all, stacks, attn)
                proj_phase(layer, attn)
            if layer == 0:
                experts_phase()
            else:
                mlp_phase()


def kernel(**inputs):
    import numpy as np
    import concourse.bacc as bacc
    from concourse.bass_utils import run_bass_kernel_spmd

    a = {k: np.asarray(v) for k, v in inputs.items()}
    D = 256

    def chunks(w):
        return w.reshape(-1, P, w.shape[-1]).transpose(1, 0, 2)

    gu = a["L0_ffn_gate_up_w"]
    gub = a["L0_ffn_gate_up_b"]
    gu = np.concatenate([gu[:, 0::2], gu[:, 1::2]], 1)
    gub = np.concatenate([gub[:, 0::2], gub[:, 1::2]], 1)
    gu = gu.transpose(0, 2, 1).reshape(8, 2, P, 512).transpose(0, 2, 1, 3).reshape(8, P, 1024)
    dn = a["L0_ffn_down_w"].transpose(0, 2, 1).reshape(8, 2, P, D).transpose(0, 2, 1, 3).reshape(8, P, 512)
    expert_w = np.concatenate([gu, dn], 2)
    arrays = {
        "ids": a["x"].reshape(-1, P).T,
        "W0": a["L0_tok_W0"],
        "w1_tok": chunks(a["L0_tok_W1"]),
        "wqkv0": chunks(a["L0_attn_w_qkv"].T),
        "wproj0": chunks(a["L0_attn_w_proj"].T),
        "bproj0": a["L0_attn_b_proj"][None],
        "router_w": chunks(a["L0_ffn_router_w"].T),
        "router_b": a["L0_ffn_router_b"][None],
        "expert_w": expert_w,
        "gate_up_b": gub.reshape(8, 4, P).transpose(2, 0, 1),
        "down_b": a["L0_ffn_down_b"],
        "wqkv1": chunks(np.concatenate([a["L1_attn_Wq"], a["L1_attn_Wk"], a["L1_attn_Wv"]], 0).T),
        "wproj1": chunks(a["L1_attn_Wo"].T),
        "w1": chunks(a["L1_ffn_w1"]),
        "b1": a["L1_ffn_b1"].reshape(-1, P).T,
        "w2": chunks(a["L1_ffn_w2"]),
        "b2": a["L1_ffn_b2"][None],
    }
    arrays = {k: np.ascontiguousarray(v) for k, v in arrays.items()}
    nc = bacc.Bacc("TRN2", target_bir_lowering=False, num_devices=1)
    args = [nc.dram_tensor(f"in_{k}", v.shape, mybir.dt.from_np(v.dtype), kind="ExternalInput").ap()
            for k, v in arrays.items()]
    tokens = a["x"].size
    out = nc.dram_tensor("out", (tokens, D), F32, kind="ExternalOutput").ap()
    lm_tower(nc, *args, out)
    r = run_bass_kernel_spmd(nc, [{f"in_{k}": v for k, v in arrays.items()}], core_ids=[0])
    return r.results[0]["out"].reshape(*a["x"].shape, D)
```
